# Optimizing a Trainium2 kernel written in Bass

```python
import numpy as np
import jax
import jax.numpy as jnp

def _softmax(x, axis=-1):
    return jax.nn.softmax(x, axis=axis)

def _gelu(x):
    return jax.nn.gelu(x, approximate=True)

def _silu(x):
    return jax.nn.silu(x)

def _sigmoid(x):
    return jax.nn.sigmoid(x)

def _layernorm(x, axis=-1, eps=1e-05):
    m = jnp.mean(x, axis=axis, keepdims=True)
    v = jnp.var(x, axis=axis, keepdims=True)
    return (x - m) / jnp.sqrt(v + eps)

def _scatter_add(tgt, idx, src, axis=0):
    return tgt.at[idx].add(src)

def _segment_sum(src, seg, n):
    return jax.ops.segment_sum(src, seg, n)
kernel_name = 'mk_flamingo_gated_d2_seqx_r4_ec4d10'

def setup_inputs(seed: int=0):
    np.random.seed(seed)
    _w = jnp.asarray

    def _rec_inputs():
        import jax
        import jax.numpy as jnp
        _rk = jax.random.key(seed)
        x = 7.22e-05 + 1 * jax.random.normal(jax.random.fold_in(_rk, 1), (4, 1024, 256), jnp.float32)
        _lenS = 1024 - jax.random.randint(jax.random.fold_in(_rk, 7), (4,), 0, max(1, 1024 // 4) + 1, jnp.int32)
        _lenS2 = 77 - jax.random.randint(jax.random.fold_in(_rk, 8), (4,), 0, max(1, 77 // 4) + 1, jnp.int32)
        _ctx_1024P = jax.random.normal(jax.random.fold_in(_rk, 11), (4, 16, 256), jnp.float32)
        _ctx_1024c = jax.random.dirichlet(jax.random.fold_in(_rk, 511), 0.3 * jnp.ones((16,), jnp.float32), (4, 77))
        _ctx_1024t = jnp.einsum('bsk,bkd->bsd', _ctx_1024c, _ctx_1024P)
        _ctx_1024t = _ctx_1024t * jax.lax.rsqrt(jnp.mean(jnp.square(_ctx_1024t)) + 1e-12) * 0.953939
        ctx_1024 = 4.13588e-05 + 0.999923 * (_ctx_1024t + 0.3 * jax.random.normal(jax.random.fold_in(_rk, 611), (4, 77, 256), jnp.float32))
        _validS = jnp.arange(1024)[None, :] < _lenS[:, None]
        _validS2 = jnp.arange(77)[None, :] < _lenS2[:, None]
        _causal = jnp.tril(jnp.ones((1024, 1024), dtype=bool))
        mask_BxSxS2_bk0 = jnp.logical_not(jnp.broadcast_to(_validS2[:, None, :], (4, 1024, 77)))
        mask_1x1xSxS2_bk0 = jnp.logical_not(jnp.broadcast_to(_validS2[0:1, None, None, :], (1, 1, 1024, 77)))
        _g = jax.random.normal(jax.random.fold_in(_rk, 9001), (2, 2), jnp.float32)
        _g = jnp.sign(_g) * jnp.maximum(jnp.abs(_g), 1.0) + (_g == 0) * 1.0
        g_xattn = _g[0]
        g_ffn = _g[1]
        return (x, ctx_1024, mask_BxSxS2_bk0, mask_1x1xSxS2_bk0, g_xattn, g_ffn)
    x, ctx_1024, mask_BxSxS2_bk0, mask_1x1xSxS2_bk0, g_xattn, g_ffn = _rec_inputs()

    def _L0_xattn_setup():
        import jax, jax.numpy as jnp
        import numpy as np
        B, S, D_IN, D_H = (4, 512, 256, 256)
        key = jax.random.key(seed)
        k1, k2, k3, k4, k5, k6 = jax.random.split(key, 6)
        seq1 = jax.random.normal(k1, (B, S, D_IN), dtype=jnp.float32)
        seq2 = jax.random.normal(k2, (B, S, D_IN), dtype=jnp.float32)
        attn_mask = jax.random.randint(k3, (B, S, S), 0, 2).astype(jnp.bool_)
        scale = 1.0 / np.sqrt(D_IN)
        Wq = jax.random.uniform(k4, (D_H, D_IN), dtype=jnp.float32, minval=-scale, maxval=scale)
        Wk = jax.random.uniform(k5, (D_H, D_IN), dtype=jnp.float32, minval=-scale, maxval=scale)
        Wv = jax.random.uniform(k6, (D_H, D_IN), dtype=jnp.float32, minval=-scale, maxval=scale)
        return {'seq1': seq1, 'seq2': seq2, 'attn_mask': attn_mask, 'Wq': Wq, 'Wk': Wk, 'Wv': Wv}
    _L0_xattn_all = _L0_xattn_setup()
    _L0_xattn_in = {k: v for k, v in _L0_xattn_all.items() if k in ('Wq', 'Wk', 'Wv')}
    del _L0_xattn_all

    def _L0_ffn_setup():
        import jax, jax.numpy as jnp
        import numpy as np
        from jax import lax
        TOP_K = 1
        key = jax.random.key(seed)
        ks = jax.random.split(key, 9)
        B, N, C = (4, 512, 256)
        E, L, R = (6, 100, 16)
        return {'feats': jax.random.normal(ks[0], (B, N, C), jnp.float32), 'A': jax.random.normal(ks[1], (E, L, R), jnp.float32) * 0.05, 'B': jax.random.normal(ks[2], (E, R, C), jnp.float32) * 0.05, 'w_gate': jax.random.normal(ks[3], (C, E), jnp.float32) * 0.02, 'wt_w': jax.random.normal(ks[4], (C, C), jnp.float32) * (1.0 / np.sqrt(C)), 'wt_b': jax.random.normal(ks[5], (C,), jnp.float32) * 0.01, 'wd_w': jax.random.normal(ks[6], (C, C), jnp.float32) * (1.0 / np.sqrt(C)), 'wd_b': jax.random.normal(ks[7], (C,), jnp.float32) * 0.01, 'scale': jnp.full((1,), 0.001, jnp.float32)}
    _L0_ffn_all = _L0_ffn_setup()
    _L0_ffn_in = {k: v for k, v in _L0_ffn_all.items() if k in ('A', 'B', 'w_gate', 'wt_w', 'wt_b', 'wd_w', 'wd_b', 'scale')}
    del _L0_ffn_all

    def _L1_xattn_setup():
        import jax, jax.numpy as jnp
        import numpy as np
        B, S, EMBED, HEADS = (2, 512, 256, 16)
        HEAD = EMBED // HEADS
        key = jax.random.key(seed)
        ks = jax.random.split(key, 8)
        inp = {'values': jax.random.normal(ks[0], (B, S, EMBED), jnp.float32), 'keys': jax.random.normal(ks[1], (B, S, EMBED), jnp.float32), 'queries': jax.random.normal(ks[2], (B, S, EMBED), jnp.float32), 'mask': jnp.tril(jnp.ones((S, S), jnp.bool_))[None, None, :, :], 'Wv': jax.random.normal(ks[3], (HEAD, HEAD), jnp.float32) / np.sqrt(HEAD), 'Wk': jax.random.normal(ks[4], (HEAD, HEAD), jnp.float32) / np.sqrt(HEAD), 'Wq': jax.random.normal(ks[5], (HEAD, HEAD), jnp.float32) / np.sqrt(HEAD), 'Wo': jax.random.normal(ks[6], (EMBED, EMBED), jnp.float32) / np.sqrt(EMBED), 'bo': jax.random.normal(ks[7], (EMBED,), jnp.float32) * 0.01}
        return inp
    _L1_xattn_all = _L1_xattn_setup()
    _L1_xattn_in = {k: v for k, v in _L1_xattn_all.items() if k in ('Wv', 'Wk', 'Wq', 'Wo', 'bo')}
    del _L1_xattn_all

    def _L1_ffn_setup():
        import jax, jax.numpy as jnp
        import numpy as np
        B, N, C, H, REG = (1, 2309, 256, 16, 5)
        D = C // H
        key = jax.random.key(seed)
        k0, k1, k2, k3 = jax.random.split(key, 4)
        x = jax.random.normal(k0, (B, N, C), dtype=jnp.float32)
        g_info = jax.random.normal(k1, (12, 2, C), dtype=jnp.float32)
        W_qkv = jax.random.normal(k2, (C, 3 * C), dtype=jnp.float32) * 0.02
        W_proj = jax.random.normal(k3, (C, C), dtype=jnp.float32) * 0.02
        b_proj = jnp.zeros((C,), dtype=jnp.float32)
        return {'x': x, 'g_info': g_info, 'W_qkv': W_qkv, 'W_proj': W_proj, 'b_proj': b_proj}
    _L1_ffn_all = _L1_ffn_setup()
    _L1_ffn_in = {k: v for k, v in _L1_ffn_all.items() if k in ('g_info', 'W_qkv', 'W_proj', 'b_proj')}
    del _L1_ffn_all
    return {'x': x, 'ctx_1024': ctx_1024, 'mask_BxSxS2_bk0': mask_BxSxS2_bk0, 'mask_1x1xSxS2_bk0': mask_1x1xSxS2_bk0, 'g_xattn': g_xattn, 'g_ffn': g_ffn, 'L0_xattn_Wq': _L0_xattn_in['Wq'], 'L0_xattn_Wk': _L0_xattn_in['Wk'], 'L0_xattn_Wv': _L0_xattn_in['Wv'], 'L0_ffn_A': _L0_ffn_in['A'], 'L0_ffn_B': _L0_ffn_in['B'], 'L0_ffn_w_gate': _L0_ffn_in['w_gate'], 'L0_ffn_wt_w': _L0_ffn_in['wt_w'], 'L0_ffn_wt_b': _L0_ffn_in['wt_b'], 'L0_ffn_wd_w': _L0_ffn_in['wd_w'], 'L0_ffn_wd_b': _L0_ffn_in['wd_b'], 'L0_ffn_scale': _L0_ffn_in['scale'], 'L1_xattn_Wv': _L1_xattn_in['Wv'], 'L1_xattn_Wk': _L1_xattn_in['Wk'], 'L1_xattn_Wq': _L1_xattn_in['Wq'], 'L1_xattn_Wo': _L1_xattn_in['Wo'], 'L1_xattn_bo': _L1_xattn_in['bo'], 'L1_ffn_g_info': _L1_ffn_in['g_info'], 'L1_ffn_W_qkv': _L1_ffn_in['W_qkv'], 'L1_ffn_W_proj': _L1_ffn_in['W_proj'], 'L1_ffn_b_proj': _L1_ffn_in['b_proj']}

def reference(x, ctx_1024, mask_BxSxS2_bk0, mask_1x1xSxS2_bk0, g_xattn, g_ffn, L0_xattn_Wq, L0_xattn_Wk, L0_xattn_Wv, L0_ffn_A, L0_ffn_B, L0_ffn_w_gate, L0_ffn_wt_w, L0_ffn_wt_b, L0_ffn_wd_w, L0_ffn_wd_b, L0_ffn_scale, L1_xattn_Wv, L1_xattn_Wk, L1_xattn_Wq, L1_xattn_Wo, L1_xattn_bo, L1_ffn_g_info, L1_ffn_W_qkv, L1_ffn_W_proj, L1_ffn_b_proj):
    import jax
    import jax.numpy as jnp

    def _L0_xattn_ref(seq1, seq2, attn_mask, Wq, Wk, Wv):
        import jax, jax.numpy as jnp
        import numpy as np
        B, S, D_IN, D_H = (4, 512, 256, 256)
        q = jnp.einsum('bsd,hd->bsh', seq1, Wq)
        k = jnp.einsum('bsd,hd->bsh', seq2, Wk)
        v = jnp.einsum('bsd,hd->bsh', seq2, Wv)
        score = jnp.einsum('bqh,bkh->bqk', q, k) / jnp.sqrt(jnp.float32(q.shape[-1]))
        mask_score = jnp.where(attn_mask, jnp.float32(1e-09), score)
        score_matrix = jax.nn.softmax(mask_score, axis=1)
        out = jnp.einsum('bqk,bkh->bqh', score_matrix, v)
        return out

    def _L0_ffn_ref(feats, A, B, w_gate, wt_w, wt_b, wd_w, wd_b, scale):
        import jax, jax.numpy as jnp
        import numpy as np
        from jax import lax
        TOP_K = 1
        Bsz, N, C = feats.shape
        x = feats.reshape(-1, C)
        n = x.shape[0]
        logits = x @ w_gate
        top_vals, top_idx = lax.top_k(logits, TOP_K)
        top_g = jax.nn.softmax(top_vals, axis=-1)
        gates = jnp.zeros_like(logits).at[jnp.arange(n)[:, None], top_idx].set(top_g)
        tokens = jnp.einsum('elr,erc->elc', A, B)
        attn = jnp.einsum('nc,elc->nel', x, tokens) * C ** (-0.5)
        attn = jax.nn.softmax(attn, axis=-1)
        val = jnp.einsum('elc,dc->eld', tokens, wt_w) + wt_b
        delta_f = jnp.einsum('nel,eld->ned', attn[:, :, 1:], val[:, 1:, :])
        delta = (jnp.einsum('ned,cd->nec', delta_f + x[:, None, :], wd_w) + wd_b) * scale[0]
        combined = jnp.sum(jnp.exp(delta) * gates[:, :, None], axis=1)
        combined = jnp.where(combined == 0, jnp.finfo(jnp.float32).eps, combined)
        out = jnp.log(combined)
        return feats + out.reshape(Bsz, N, C)

    def _L1_xattn_ref(values, keys, queries, mask, Wv, Wk, Wq, Wo, bo):
        import jax, jax.numpy as jnp
        import numpy as np
        B, S, EMBED, HEADS = (2, 512, 256, 16)
        HEAD = EMBED // HEADS
        N, Lq = (queries.shape[0], queries.shape[1])
        Lk = keys.shape[1]
        v = values.reshape(N, -1, HEADS, HEAD) @ Wv.T
        k = keys.reshape(N, Lk, HEADS, HEAD) @ Wk.T
        q = queries.reshape(N, Lq, HEADS, HEAD) @ Wq.T
        energy = jnp.einsum('bqhd,bkhd->bhqk', q, k)
        energy = jnp.where(mask, energy, jnp.float32(-1e+20))
        attn = jax.nn.softmax(energy / np.sqrt(HEAD), axis=-1)
        out = jnp.einsum('bhqk,bkhd->bqhd', attn, v).reshape(N, Lq, EMBED)
        return out @ Wo.T + bo

    def _L1_ffn_ref(x, g_info, W_qkv, W_proj, b_proj):
        import jax, jax.numpy as jnp
        import numpy as np
        B, N, C, H, REG = (1, 2309, 256, 16, 5)
        D = C // H
        Bx, Nx, Cx = x.shape
        scale = D ** (-0.5)
        qkv = (x @ W_qkv).reshape(Bx, Nx, 3, H, D)
        q, k, v = (qkv[:, :, 0], qkv[:, :, 1], qkv[:, :, 2])
        g_layer = g_info[0].reshape(-1, H, D)
        q_g = g_layer[0]
        q_pure = q[:, REG:]
        q_n = q_pure / jnp.linalg.norm(q_pure, axis=-1, keepdims=True)
        qg_n = q_g / jnp.linalg.norm(q_g, axis=-1, keepdims=True)
        sim = (qg_n[None, None] * q_n).sum(-1).mean(-1)
        sim = (sim - sim.min()) / (sim.max() - sim.min())
        pos = sim > 0.9
        logits = jnp.einsum('bqhd,bkhd->bhqk', q * scale, k)

        def masked_attn(tok_mask):
            key_mask = jnp.concatenate([jnp.ones((Bx, REG), bool), tok_mask], axis=1)
            l = jnp.where(key_mask[:, None, None, :], logits, -jnp.inf)
            a = jax.nn.softmax(l, axis=-1)
            return jnp.einsum('bhqk,bkhd->bqhd', a, v)
        x_pos = masked_attn(pos)
        x_neg = masked_attn(~pos)
        reg_out = (x_pos[:, :REG] + x_neg[:, :REG]) * 0.5
        tok_out = jnp.where(pos[:, :, None, None], x_pos[:, REG:], x_neg[:, REG:])
        out = jnp.concatenate([reg_out, tok_out], axis=1).reshape(Bx, Nx, Cx)
        return out @ W_proj + b_proj
    x = x + jnp.tanh(g_xattn[0]) * _L0_xattn_ref(_layernorm(x, axis=-1), ctx_1024, mask_BxSxS2_bk0, L0_xattn_Wq, L0_xattn_Wk, L0_xattn_Wv)
    x = x + jnp.tanh(g_ffn[0]) * _L0_ffn_ref(_layernorm(x, axis=-1), L0_ffn_A, L0_ffn_B, L0_ffn_w_gate, L0_ffn_wt_w, L0_ffn_wt_b, L0_ffn_wd_w, L0_ffn_wd_b, L0_ffn_scale)
    x = x + jnp.tanh(g_xattn[1]) * _L1_xattn_ref(ctx_1024, ctx_1024, _layernorm(x, axis=-1), mask_1x1xSxS2_bk0, L1_xattn_Wv, L1_xattn_Wk, L1_xattn_Wq, L1_xattn_Wo, L1_xattn_bo)
    x = x + jnp.tanh(g_ffn[1]) * _L1_ffn_ref(_layernorm(x, axis=-1), L1_ffn_g_info, L1_ffn_W_qkv, L1_ffn_W_proj, L1_ffn_b_proj)
    return x

_drawn_inputs = setup_inputs


def setup_inputs(seed=0):
    import zlib

    import numpy as np

    out = dict(_drawn_inputs(seed))
    spreads = {'g_ffn': (-1.0, 0.6), 'L1_ffn_b_proj': (0.0, 0.1)}
    factors = {'L0_xattn_Wq': 8.0,
     'L0_xattn_Wk': 8.0,
     'L0_xattn_Wv': 6.636,
     'L0_ffn_A': 8.0,
     'L0_ffn_B': 8.0,
     'L0_ffn_w_gate': 8.0,
     'L0_ffn_wt_w': 8.0,
     'L0_ffn_wt_b': 8.0,
     'L0_ffn_wd_w': 8.0,
     'L0_ffn_wd_b': 8.0,
     'L1_xattn_bo': 4.401,
     'L1_ffn_g_info': 8.0}
    for name, (base, spread) in spreads.items():
        noise = np.random.default_rng([zlib.crc32(name.encode()), seed]).standard_normal(out[name].shape)
        drawn = base * np.exp(spread * noise) if base else spread * noise
        out[name] = jnp.asarray(drawn.astype(out[name].dtype))
    for name, factor in factors.items():
        out[name] = (out[name] * factor).astype(out[name].dtype)
    return out
```

```python
from contextlib import ExitStack

import numpy as np
import concourse.bass as bass
from concourse import mybir

F32 = mybir.dt.float32
BF16 = mybir.dt.bfloat16
U8 = mybir.dt.uint8
ALU = mybir.AluOpType
ACT = mybir.ActivationFunctionType
AX = mybir.AxisListType.X

B, S, C = 4, 1024, 256
KX = 77
H, D = 16, 16
E, L, R = 6, 100, 16
REG = 5
P = 128
T = B * S
NT = T // P
NC = T // 512
TB = S // P
UNITS = B * 4
BIG = 2.0 ** 66
LN_EPS = 1e-5
TINY = float(np.finfo(np.float32).eps)
Q_ORDER, K_ORDER = (0, 0, 0, 1, 1, 2), (0, 1, 2, 0, 1, 0)
SR = 96
NEG_ROW, POS_ROW, MAX_ROW = 96, 97, 98


def build_program(nc, ins, out):
    ctx = ExitStack()
    with ctx:
        def sb(name, shape, dt=F32):
            return ctx.enter_context(nc.sbuf_tensor(name, shape, dt))

        def sem(name):
            return ctx.enter_context(nc.semaphore(name))

        X = sb("X", [P, NT, C])
        R1 = sb("R1", [P, 8192])
        R2 = sb("R2", [P, 8192])
        R3 = sb("R3", [P, 8192])
        R4 = sb("R4", [P, 4096])
        XNT = R1[:, :].rearrange("p (j t) -> p j t", j=2)

        XN = sb("XN", [P, 2, 4, C])
        stats = sb("stats", [P, NT, 6])
        mv = sb("mv", [P, NT, 2])
        rstd = sb("rstd", [P, NT])
        mhalf = sb("mhalf", [P, NT])
        identF = sb("identF", [P, P])
        identB = sb("identB", [P, P], BF16)
        gates = sb("gates", [P, 4])
        small = sb("small", [P, 640])

        ps = ctx.enter_context(nc.psum_tensor("ps", [P, 4096], F32))

        def bank(i, n=1):
            return ps[:, 512 * i:512 * (i + n)]

        W = sb("W", [P, 4608])
        at = [0]

        def w(n):
            at[0] += n
            assert at[0] <= 4608
            return W[:, at[0] - n:at[0]]

        def w2(n):
            return w(2 * n).rearrange("p (j n) -> p j n", j=2)

        ctxT = w2(B * KX)
        wbig = w(1536)
        wk0 = wbig[:, 0:512].rearrange("p (j n) -> p j n", j=2)
        wq0 = wbig[:, 512:1024].rearrange("p (j n) -> p j n", j=2)
        wv0 = wbig[:, 1024:1536].rearrange("p (j n) -> p j n", j=2)
        wqkv = wbig.rearrange("p (j n) -> p j n", j=2)
        wA = w(1616)

        def wa(a, n, j=None):
            v = wA[:, a:a + n]
            return v if j is None else v.rearrange("p (j n) -> p j n", j=j)

        wg, ballT, wtT, wdT = wa(0, 12, 2), wa(12, 192, 2), wa(204, 512, 2), wa(716, 512, 2)
        AT, A1x = wa(1228, 100), wa(1328, 98)
        wtb = wa(1426, 2)
        BW = sb("BW", [P, C])
        BWt = sb("BWt", [P, 2, 97])
        wo1 = sb("wo1", [P, 2, C])
        wproj = sb("wproj", [P, 2, C])
        bo1 = sb("bo1", [P, C])
        bp2 = sb("bp2", [P, C])
        w16 = sb("w16", [P, 3, 16])
        bd = sb("bd", [P, 3, P])
        blk = sb("blk", [P, 8])

        R2f = R2[:, :]
        R3f = R3[:, :]

        s_x = [sem(f"x_loaded{b}") for b in range(B)]
        s_w0 = sem("xattn0_weights_loaded")
        s_m0 = sem("mask0_loaded")
        s_g = sem("gates_loaded")
        s_const = sem("constants_made")
        s_gt = sem("gates_tanh")
        s_ks = sem("setup_product")
        s_ksc = sem("setup_copied")
        s_st = sem("stats_done")
        s_ag = sem("aggregated")
        s_rs = sem("rstd_done")
        s_xn = sem("chunk_normalised")
        s_tr = sem("chunk_transposed")
        s_xt = sem("chunk_transpose_copied")

        R5 = sb("R5", [P, 4096])
        block = ctx.enter_context(nc.Block())
        kT0 = R2f[:, 0:616].rearrange("p (j n) -> p j n", j=2)
        KW0 = R2f[:, 616:1232].rearrange("p (j n) -> p j n", j=2)
        V0 = R2f[0:KX, 1232:2256].rearrange("p (b n) -> p b n", b=B)
        P0 = R2f[0:KX, 2256:6352].rearrange("p (b n) -> p b n", b=B)
        V0s = R2f[0:KX, 6352:7376].rearrange("p (b n) -> p b n", b=B)
        M0 = R3f[0:KX, 0:1024].bitcast(U8).rearrange("p (b n) -> p b n", b=B)
        masked = R3f[0:KX, 1024:1025]
        mx0 = small[0:KX, 0:4]
        nb0 = small[0:KX, 4:8]
        den0 = small[0:KX, 8:12]
        rd0 = small[0:KX, 12:16]
        graw = small[:, 16:20]
        s_s0 = sem("scores0")
        s_mk0 = sem("scores0_masked")
        s_mx0 = sem("scores0_max")
        s_nb0 = sem("scores0_negmax")
        s_e0 = sem("probs0")
        s_rd0 = sem("recip0")
        s_v0 = sem("values0_scaled")
        s_o0 = sem("out0")
        s_x1 = sem("x1_added")

        NB16 = E * R
        OH96 = R3f[:, 0:1568].bitcast(BF16).rearrange("p (i n) -> p i n", i=NT)
        attn = R3f[:, 1568:4768].rearrange("p (i l) -> p i l", i=NT)
        OHT = R4[0:98, 0:2048].bitcast(BF16)
        ysel = R2f[0:NB16, 0:4096]
        usel = R2f[0:98, 0:4096]
        aT = R2f[0:L, 4096:8192]
        comb = R3f.rearrange("p (i c) -> p i c", i=NT)
        zfix = R4[:, 2048:4096].rearrange("p (u n) -> p u n", u=2)
        gmx = small[:, 32:64]
        eq6 = small[:, 64:256].rearrange("p (i e) -> p i e", e=E)
        gm2 = small[:, 256:288]
        wtie = small[:, 288:294]
        amx = small[:, 296:328].rearrange("p (i o) -> p i o", o=1)
        asum = small[:, 328:360].rearrange("p (i o) -> p i o", o=1)
        arec = small[:, 360:392].rearrange("p (i o) -> p i o", o=1)
        fscale = small[:, 392:393]
        s_wf = sem("ffn0_weights_loaded")
        s_fc = sem("ffn0_constants")
        s_fs = sem("ffn0_setup_product")
        s_fsc = sem("ffn0_setup_copied")
        s_xg = sem("gated_ln_added")
        s_gl = sem("gate_logits")
        s_gc = sem("gate_chain")
        s_ot = sem("onehot_transposed")
        s_otc = sem("onehot_copied")
        s_y = sem("y_product")
        s_ys = sem("y_selected")
        s_lg = sem("landmark_logits")
        s_am = sem("landmark_max")
        s_ad = sem("landmark_minus_max")
        s_ae = sem("landmark_exp")
        s_as = sem("landmark_sum")
        s_ar = sem("landmark_recip")
        s_an = sem("landmark_attn")
        s_at = sem("attn_transposed")
        s_atc = sem("attn_copied")
        s_u = sem("u_product")
        s_us = sem("u_selected")
        s_dl = sem("delta_product")
        s_de = sem("delta_exp")
        s_z1 = sem("zero_found")
        s_z2 = sem("zero_replaced")
        s_ln = sem("combined_log")
        s_x2 = sem("x2_added")

        XP = nc.dram_tensor("x_parts", (3, C, T), BF16).ap()
        KXP = nc.dram_tensor("ctx_key_parts", (3, C, B * KX), BF16).ap()
        K1s = R2f[0:SR, 0:2464].bitcast(BF16).rearrange("p (h n) -> p h n", h=H)
        V1a = R2f[0:KX, 2464:4512].rearrange("p (b h d) -> p b h d", b=B, h=H)
        mb1 = R2f[0:KX, 4512:5024].bitcast(BF16)
        M1u = R2f[0:KX, 5024:5280].bitcast(U8)
        I4 = R2f[0:KX, 5280:5434].bitcast(BF16)
        HS = R2f[0:4, 5434:5588].bitcast(BF16).rearrange("p (j n) -> p j n", j=4)
        mrow = R2f[0:4, 5588:6100].bitcast(BF16)
        Oe = R2f[:, 6100:7124].rearrange("p (u n) -> p u n", u=2)
        k1T = R3f[:, 0:616].rearrange("p (j n) -> p j n", j=2)
        kr1 = R3f[:, 616:1232].rearrange("p (j n) -> p j n", j=2)
        kpart = R3f[:, 1232:2156].bitcast(BF16).rearrange("p (a j n) -> p a j n", a=3, j=2)
        P1 = R3f[0:KX, 0:4096].rearrange("p (u j n) -> p u j n", u=2, j=4)
        PB = R3f[:, 4096:7168].bitcast(BF16).rearrange("p (u a j n) -> p u a j n", u=2, a=3, j=2)
        xres = R4[:, 2048:4096].rearrange("p (u j n) -> p u j n", u=2, j=2)
        Xs = [v.bitcast(BF16).rearrange("p (j n) -> p j n", j=4)
              for v in (R4[0:SR, 0:2048], R5[0:SR, 0:2048], R5[0:SR, 2048:4096])]
        On = R1[:, :].rearrange("p (i c) -> p i c", i=NT)
        OnT = R3f[:, 0:2048].rearrange("p (u j n) -> p u j n", u=2, j=2)
        M1 = small[:, 400:464].rearrange("p (u q j) -> p u q j", u=2, q=8)
        Mn = small[:, 464:528].rearrange("p (u q j) -> p u q j", u=2, q=8)
        rc1 = small[:, 528:544].rearrange("p (q j) -> p q j", q=4)
        s_w1 = sem("layer1_weights_loaded")
        s_bd = sem("block_diagonals_made")
        s_k1 = sem("ctx_keys_product")
        s_k1c = sem("ctx_keys_copied")
        s_kr = sem("ctx_keys_residue")
        s_kw = sem("ctx_key_parts_written")
        s_k1s = sem("ctx_key_stack_loaded")
        s_v1 = sem("ctx_values_product")
        s_v1c = sem("ctx_values_copied")
        s_v1m = sem("ctx_values_preset")
        s_mk1 = sem("mask1_made")
        s_m1 = sem("mask1_loaded")
        s_ph = sem("part_h")
        s_pr = sem("part_residue")
        s_pm = sem("part_m")
        s_pl = sem("part_l")
        s_pw = [sem(f"parts_written{n}") for n in range(2)]
        s_xs = [sem(f"x_stack_loaded{n}") for n in range(3)]
        s_mp = sem("max1_product")
        s_mr = sem("max1_reduced")
        s_mn = sem("max1_negated")
        s_mt = sem("max1_transposed")
        s_mrc = sem("max1_rows")
        s_sc = sem("scores1")
        s_e1 = sem("probs1")
        s_pv = sem("values1_product")
        s_oc = sem("out1_copied")
        s_ot1 = sem("out1_transposed")
        s_rc = sem("out1_recip")
        s_on = sem("out1_normalised")
        s_gb = sem("gated_bias")
        s_xb = sem("bias_added")
        s_onT = sem("heads_transposed")
        s_onc = sem("heads_copied")
        s_wo = sem("projected")
        s_x3 = sem("x3_added")

        STACK_DMAS = 6

        QP = nc.dram_tensor("q_parts", (3, B * C, S), BF16).ap()
        KP = nc.dram_tensor("k_parts", (3, B * C, S), BF16).ap()
        MR = nc.dram_tensor("max_rows", (2, 16, P), BF16).ap()
        CR = nc.dram_tensor("class_rows", (4, B, 4, S), BF16).ap()
        KT = R2[:, :].rearrange("p (j t) -> p j t", j=2)
        V2 = R3[:, :].rearrange("p (u k n) -> p u k n", u=UNITS, k=TB)
        On2 = R1[:, :].rearrange("p (k u n) -> p k (u n)", u=UNITS, k=TB)
        PB2 = R5[:, 0:3072].bitcast(BF16).rearrange("p (u a j n) -> p u a j n", u=2, a=3, j=2)
        res2 = XN[:, :, :, :].rearrange("p u i c -> p u (i c)").rearrange("p u (j n) -> p u j n", j=2)
        Qf = R4[:, 0:2048].rearrange("p (u j n) -> p u j n", u=2, j=2)
        Qsq = R4[:, 2048:4096].rearrange("p (u j n) -> p u j n", u=2, j=2)
        QST = [v.bitcast(BF16).rearrange("p (j n) -> p j n", j=4)
               for v in (R4[:, 0:2048], R2[:, 0:2048], R2[:, 4096:6144])]
        KST = [v.bitcast(BF16).rearrange("p (j n) -> p j n", j=4)
               for v in (R4[:, 2048:4096], R2[:, 2048:4096], R2[:, 6144:8192])]
        VST = [R5[:, 1024 * n:1024 * n + 1024].rearrange("p (k j d) -> p k j d", k=TB, j=4) for n in range(3)]
        regn = R5[0:REG, 3072:4096].rearrange("p (b c) -> p b c", b=B)
        PR = W[:, 0:4096].rearrange("p (u j n) -> p u j n", u=2, j=4)
        XNf = XN[:, :, :, :].rearrange("p u i c -> p (u i c)")
        Oe2 = XNf[:, 0:1024].rearrange("p (u n) -> p u n", u=2)
        mro = XNf[0:16, 1024:1152].bitcast(BF16).rearrange("p (u n) -> p u n", u=2)
        crow = XNf[0:1, 0:2048].bitcast(BF16)
        Pn = W[:, 0:1024]
        PnT = W[:, 1024:2048].rearrange("p (k n) -> p k n", k=TB)
        Qbd = W[:, 2048:2560].rearrange("p (b j n) -> p b j n", b=B, j=2)
        omk = W[:, 2560:2816].rearrange("p (j n) -> p j n", j=2)
        rn2 = W[:, 2816:3328]
        dt2 = W[:, 3328:3840]
        sm2 = sb("sm2", [P, 1024])
        qgc = sm2[:, 0:2]
        qg2 = sm2[:, 2:4]
        qgn = sm2[:, 4:6]
        qgb = sm2[:, 8:24].rearrange("p (j g) -> p j g", j=2)
        BBm = sm2[:, 24:152]
        Rfull = sm2[:, 152:192].rearrange("p (g r) -> p g r", g=8)
        Rsel = sm2[:, 192:197]
        rmask = sm2[:, 200:208]
        regm = sm2[:, 208:240]
        QR = sm2[:, 240:280].rearrange("p (j b r) -> p j b r", j=2, b=B)
        simc = sm2[:, 280:312]
        cls = sm2[:, 312:440].rearrange("p (k i) -> p k i", k=4)
        tmp32 = sm2[:, 440:472]
        mm2 = sm2[:, 472:474]
        mmr = sm2[0:2, 474:475]
        mmd = sm2[0:2, 476:478]
        ones2 = sm2[0:2, 480:608]
        mmb = sm2[:, 608:610]
        rng = sm2[:, 610:611]
        rrg = sm2[:, 611:612]
        clsT = sm2[:, 612:676].bitcast(BF16)
        onesb = sm2[0:1, 676:708].bitcast(BF16)
        rmx = sm2[:, 708:712]
        rnm = sm2[:, 712:716]
        rden = sm2[:, 716:720]
        rrd = sm2[:, 720:724]
        MX = sm2[:, 728:760].rearrange("p (u q j) -> p u q j", u=2, q=4)
        MXn = sm2[:, 760:792].rearrange("p (u q j) -> p u q j", u=2, q=4)
        rc2 = sm2[:, 792:808].rearrange("p (q j) -> p q j", q=4)
        simr = sm2[:, 808:840]
        s_wq3 = sem("wqkv_loaded")
        s_qgl = sem("q_g_loaded")
        s_qc = sem("q_g_chain")
        s_qk = sem("q_g_product")
        s_c2 = sem("class_constants")
        s_gb2 = sem("gated_bias2")
        s_xb2 = sem("bias2_added")
        s_qp = sem("qkv_product")
        s_qh = sem("q_part_h")
        s_qf = sem("q_copied")
        s_qs = sem("q_squared")
        s_qm = sem("q_part_m")
        s_kh = sem("k_part_h")
        s_km = sem("k_part_m")
        s_qr = sem("q_residue")
        s_krs = sem("k_residue")
        s_kf = sem("k_copied")
        s_vf = sem("v_copied")
        s_ql = sem("q_part_l")
        s_kl = sem("k_part_l")
        s_qw = sem("q_parts_written")
        s_kw2 = sem("k_parts_written")
        s_qrr = sem("register_queries_kept")
        s_sim = sem("sim_products")
        s_sc2 = sem("sim_chain")
        s_rp = sem("norms_inverted")
        s_mmt = sem("extremes_transposed")
        s_mmb = sem("extremes_broadcast")
        s_clt = sem("classes_transposed")
        s_clw = sem("class_rows_written")
        s_crl = sem("register_key_row_loaded")
        s_rq = sem("register_scores")
        s_rm = sem("register_chain")
        s_rex = sem("register_probs")
        s_rpt = sem("register_probs_transposed")
        s_rpc = sem("register_probs_copied")
        s_rv = sem("register_values")
        s_rk = sem("register_masked")
        s_rsm = sem("register_summed")
        s_rgn = sem("register_kept")
        s_stk = [sem(f"stacks_loaded{n}") for n in range(3)]
        s_one = sem("max_row_factor_set")
        s_mrw = [sem(f"max_rows_in_dram{n}") for n in range(2)]
        s_row = [sem(f"max_rows_loaded{n}") for n in range(2)]
        s_turn = sem("turn_filled")
        s_tfree = sem("turn_free")
        s_neg = sem("maxima_negated")
        s_sco = sem("scores2")
        s_sfree = sem("score_bank_free")
        s_pv2 = sem("values2_product")
        s_oe2 = sem("out2_copied")
        s_vst = sem("values_staged")
        s_vpre = sem("value_stage_preset")
        s_rc2 = sem("out2_recip")
        s_avg = sem("registers_averaged")
        s_out = sem("output_written")

        OnT2 = W[:, 0:2048].rearrange("p (u j n) -> p u j n", u=2, j=2)
        SIM_READ, CLS_DONE = 2, 23
        STACK2_DMAS = 14
        PLAN = [[("tile", n)] for n in range(30)] + [[], []] + [[("tile", 30), ("tile", 31), ("out", 1)]]
        PLAN[2].append(("rows", 1))
        PLAN[19].append(("rows", 0))
        PLAN[22].append(("out", 0))
        PLAN_LAST = [[] for _ in range(32)] + [[("out", 1)]]
        PLAN_LAST[2].append(("rows", 1))
        PLAN_LAST[22].append(("out", 0))
        TURNS0 = 33
        TURNS = sum(len(x) for x in PLAN)
        flat, flat_last = sum(PLAN, []), sum(PLAN_LAST, [])
        ROWS1, ROWS0, ROWS1_LAST = flat.index(("rows", 1)), flat.index(("rows", 0)), flat_last.index(("rows", 1))

        def ln_chunk_buf(c):
            return XN[:, c % 2]

        @block.sync
        def _(sp):
            for b in range(B):
                sp.dma_start(X[:, TB * b:TB * b + TB, :],
                             ins["x"][b].rearrange("(i p) c -> p i c", p=P)).then_inc(s_x[b], 16)
            for dst, src in ((ctxT, ins["ctxT"]), (wk0, ins["wk0T"]), (wq0, ins["wq0"]), (wv0, ins["wv0T"])):
                sp.dma_start(dst, src.rearrange("(j p) n -> p j n", p=P)).then_inc(s_w0, 16)
            for b in range(B):
                sp.dma_start(M0[:, b, :], ins["mask0T"][b]).then_inc(s_m0, 16)
            for i, n in enumerate(("g_xattn", "g_ffn")):
                sp.dma_start(graw[:, 2 * i:2 * i + 2],
                             ins[n].rearrange("(a n) -> a n", a=1).to_broadcast([P, 2])).then_inc(s_g, 16)
            sp.dma_start(wg, ins["w_gate"].rearrange("(j p) n -> p j n", p=P)).then_inc(s_wf, 16)
            sp.dma_start(ballT, ins["ballT"].rearrange("(j p) n -> p j n", p=P)).then_inc(s_wf, 16)
            sp.dma_start(wtT, ins["wtT"].rearrange("(j p) n -> p j n", p=P)).then_inc(s_wf, 16)
            sp.dma_start(wdT, ins["wdT"].rearrange("(j p) n -> p j n", p=P)).then_inc(s_wf, 16)
            sp.dma_start(AT[0:NB16, :], ins["AT"]).then_inc(s_wf, 16)
            sp.wait_ge(s_fc, 2)
            sp.dma_start(A1x[1:L, 0:NB16], ins["A1"][1:L, :]).then_inc(s_wf, 16)
            sp.dma_start(BWt[:, :, 96], ins["wt_b"].rearrange("(j p) -> p j", p=P),
                         allow_slow_non_contiguous=True).then_inc(s_wf, 16)
            sp.dma_start(BW[97:98, :], ins["wd_b"].rearrange("(a n) -> a n", a=1)).then_inc(s_wf, 16)
            sp.dma_start(fscale, ins["scale"].rearrange("(a n) -> a n", a=1).to_broadcast([P, 1])).then_inc(s_wf, 16)
            sp.dma_start(wo1[:, :, :], ins["wo1T"].rearrange("(j p) n -> p j n", p=P)).then_inc(s_w1, 16)
            sp.dma_start(wproj[:, :, :], ins["wproj"].rearrange("(j p) n -> p j n", p=P)).then_inc(s_w1, 16)
            sp.dma_start(bo1[:, :], ins["bo1"].rearrange("(a n) -> a n", a=1).to_broadcast([P, C])).then_inc(s_w1, 16)
            sp.dma_start(bp2[:, :], ins["bproj"].rearrange("(a n) -> a n", a=1).to_broadcast([P, C])).then_inc(s_w1, 16)
            for i, n in enumerate(("wv1T", "wk1T", "wq1")):
                for g in range(8):
                    sp.dma_start(w16[16 * g:16 * g + 16, i, :], ins[n]).then_inc(s_w1, 16)
            sp.wait_ge(s_u, NC)
            sp.wait_ge(s_dl, NC)
            sp.dma_start(M1u, ins["mask1T"]).then_inc(s_m1, 16)
            sp.wait_ge(s_kr, 5)
            sp.dma_start(KXP.rearrange("a (j p) n -> p a j n", p=P), kpart).then_inc(s_kw, 16)
            sp.wait_ge(s_kw, 16)
            for n, p in enumerate(K_ORDER):
                sp.dma_start(K1s[16 * n:16 * n + 16],
                             KXP[p].rearrange("(h d) n -> d h n", d=D)).then_inc(s_k1s, 16)

            def write_parts(n, dst):
                sp.wait_ge(s_pl, n + 1)
                sp.dma_start(dst, PB[:, n % 2]).then_inc(s_pw[n % 2], 16)

            def load_x_stack(u):
                b, hg = u // 4, u % 4
                if u >= 3:
                    sp.wait_ge(s_sc, 8 * (u - 2))
                for n, p in enumerate(Q_ORDER):
                    sp.dma_start(Xs[u % 3][16 * n:16 * n + 16],
                                 XP[p, 64 * hg:64 * hg + 64, S * b:S * b + S]
                                 .rearrange("(j d) t -> d j t", d=D)).then_inc(s_xs[u % 3], 16)

            for c in range(NC):
                write_parts(c, XP[:, :, 512 * c:512 * c + 512].rearrange("a (j p) n -> p a j n", p=P))
            for u in range(UNITS):
                b = u // 4
                if u % 4 == 0:
                    sp.wait_ge(s_pw[0], 16 * (b + 1))
                    sp.wait_ge(s_pw[1], 16 * (b + 1))
                load_x_stack(u)
            sp.wait_ge(s_ksc, 6)
            sp.wait_ge(s_ks, 6)
            sp.dma_start(wqkv, ins["wqkv"].rearrange("(j p) n -> p j n", p=P)).then_inc(s_wq3, 16)
            sp.dma_start(qgc, ins["g_info"][0, 0].rearrange("(j p) -> p j", p=P),
                         allow_slow_non_contiguous=True).then_inc(s_qgl, 16)
            for c in range(NC):
                rows = slice(C * (c // 2), C * (c // 2) + C)
                t = slice(512 * (c % 2), 512 * (c % 2) + 512)
                sp.wait_ge(s_ql, c + 1)
                for a in range(3):
                    sp.dma_start(QP[a, rows, t].rearrange("(j p) n -> p j n", p=P), PB2[:, 0, a]).then_inc(s_qw, 16)
                sp.wait_ge(s_kl, c + 1)
                for a in range(3):
                    sp.dma_start(KP[a, rows, t].rearrange("(j p) n -> p j n", p=P), PB2[:, 1, a]).then_inc(s_kw2, 16)
            sp.wait_ge(s_sc2, CLS_DONE)
            for k in range(4):
                for b in range(B):
                    row = TB * (B * k + b)
                    sp.dma_start(CR[k, b].rearrange("g (i n) -> i g n", n=P),
                                 clsT[row:row + TB].unsqueeze(1).to_broadcast([TB, 4, P])).then_inc(s_clw, 16)
            sp.wait_ge(s_clw, 16 * 16)
            sp.dma_start(crow.rearrange("p (b t) -> p b t", b=B), CR[2, :, 0, :].unsqueeze(0)).then_inc(s_crl, 16)
            sp.wait_ge(s_qw, 48 * NC)
            sp.wait_ge(s_kw2, 48 * NC)
            CRu = CR.rearrange("k b g t -> k (b g) t")

            def load_stacks(u, j):
                for dst, parts, order in ((QST[j], QP, Q_ORDER), (KST[j], KP, K_ORDER)):
                    for n, a in enumerate(order):
                        src = parts[a].rearrange("(u j d) t -> u d j t", u=UNITS, d=D)
                        sp.dma_start(dst[16 * n:16 * n + 16], src[u]).then_inc(s_stk[j], 16)
                for dst, k in ((QST[j], 0), (KST[j], 2)):
                    sp.dma_start(dst[NEG_ROW:POS_ROW + 1],
                                 CRu[k:k + 2].rearrange("k u t -> u k t")[u].unsqueeze(1)
                                 .to_broadcast([2, 4, S])).then_inc(s_stk[j], 16)

            def store_row(j, half, filled, stored):
                sp.wait_ge(s_tfree, filled)
                sp.dma_start(MR[half], mro[:, half, :]).then_inc(s_mrw[half], 16)
                sp.wait_ge(s_mrw[half], 16 * stored + 16)
                sp.dma_start(QST[j][MAX_ROW:MAX_ROW + 1, :, 512 * half:512 * half + 512],
                             MR[half].rearrange("(h q) n -> h (q n)", h=4).unsqueeze(0)).then_inc(s_row[half], 16)

            sp.wait_ge(s_sim, NC)
            sp.wait_ge(s_one, 1)
            load_stacks(0, 0)
            sp.wait_ge(s_rq, B)
            sp.wait_ge(s_one, 3)
            load_stacks(1, 1)
            load_stacks(2, 2)
            store_row(0, 0, 2 + 17, 0)

            def body_sp(u, j, last=False, load=True):
                base = 2 + TURNS0 + TURNS * u + 1
                store_row(j, 1, base + (ROWS1_LAST if last else ROWS1), u)
                if not last:
                    store_row((j + 1) % 3, 0, base + ROWS0, u + 1)
                if load:
                    sp.wait_ge(s_pv2, 2 + 16 * (u + 1))
                    load_stacks(u + 3, j)

            with sp.Fori(0, 4) as i:
                for j in range(3):
                    body_sp(3 * i + j, j)
            body_sp(12, 0)
            body_sp(13, 1, load=False)
            body_sp(14, 2, load=False)
            body_sp(15, 0, last=True, load=False)
            for c in range(NC):
                sp.wait_ge(s_x3, NC + c + 1)
                sp.dma_start(out[c // 2].rearrange("(i p) c -> p i c", p=P)[:, 4 * (c % 2):4 * (c % 2) + 4, :],
                             X[:, 4 * c:4 * c + 4, :]).then_inc(s_out, 16)
            sp.wait_ge(s_out, 16 * NC)

        @block.gpsimd
        def _(pool):
            pool.memset(identF[:, :], 0.0).then_inc(s_const, 1)
            pool.memset(blk[:, :], 1.0).then_inc(s_const, 1)
            pool.memset(mhalf[:, :], -0.5).then_inc(s_const, 1)
            pool.memset(masked, 1e-9 * 16.0).then_inc(s_const, 1)
            pool.wait_ge(s_const, 4)
            pool.affine_select(out=identF[:, :], in_=identF[:, :], compare_op=ALU.not_equal, fill=1.0,
                               base=0, pattern=[[-1, P]], channel_multiplier=1).then_inc(s_const, 1)
            pool.wait_ge(s_const, 5)
            pool.tensor_copy(identB[:, :], identF[:, :]).then_inc(s_const, 1)
            pool.affine_select(out=blk[:, :], in_=blk[:, :], compare_op=ALU.is_ge, fill=0.0,
                               base=0, pattern=[[-16, 8]], channel_multiplier=1).then_inc(s_const, 1)
            pool.wait_ge(s_const, 7)
            pool.affine_select(out=blk[:, :], in_=blk[:, :], compare_op=ALU.is_ge, fill=0.0,
                               base=15, pattern=[[16, 8]], channel_multiplier=-1).then_inc(s_const, 1)

            def ln_rstd(k):
                for b in range(B):
                    v = slice(TB * b, TB * b + TB)
                    pool.wait_ge(s_ag, B * k + b + 1)
                    pool.tensor_scalar(rstd[:, v], mv[:, v, 1], LN_EPS, None, ALU.add).then_inc(s_rs, 1)
                    pool.wait_ge(s_rs, 2 * (B * k + b) + 1)
                    pool.tensor_tensor(rstd[:, v], rstd[:, v], mhalf[:, v], ALU.pow).then_inc(s_rs, 1)

            ln_rstd(0)
            pool.memset(A1x[0:L, :], 1.0).then_inc(s_fc, 1)
            pool.wait_ge(s_fc, 1)
            pool.memset(A1x[0:1, 0:97], 0.0).then_inc(s_fc, 1)
            for e in range(E):
                pool.memset(wtie[:, e:e + 1], float(E - e)).then_inc(s_fc, 1)

            ln_rstd(1)
            for c in range(NC):
                v = comb[:, 4 * c:4 * c + 4, :]
                pool.wait_ge(s_de, c + 1)
                if c >= 2:
                    pool.wait_ge(s_z2, c - 1)
                pool.tensor_scalar(zfix[:, c % 2].rearrange("p (i n) -> p i n", i=4), v, 0.0, TINY,
                                   ALU.is_equal, ALU.mult).then_inc(s_z1, 1)
                pool.wait_ge(s_z1, c + 1)
                pool.tensor_tensor(v, v, zfix[:, c % 2].rearrange("p (i n) -> p i n", i=4), ALU.add).then_inc(s_z2, 1)

            ln_rstd(2)
            pool.wait_ge(s_dl, NC)
            pool.memset(V1a, 0.0).then_inc(s_v1m, 1)
            pool.wait_ge(s_v1m, 1)
            pool.memset(V1a[:, :, :, D:D + 1], 1.0).then_inc(s_v1m, 1)
            pool.wait_ge(s_w1, 16 * 28)
            pool.wait_ge(s_gt, 1)
            pool.tensor_scalar(bo1[:, :], bo1[:, :], gates[:, 1:2], None, ALU.mult).then_inc(s_gb, 1)
            pool.wait_ge(s_gb, 1)

            def last_parts(k, n0):
                for c in range(NC):
                    n = n0 + c
                    pool.wait_ge(s_pm, n + 1)
                    pool.tensor_tensor(PB[:, n % 2, 2], xres[:, n % 2], PB[:, n % 2, 1],
                                       ALU.subtract).then_inc(s_pl, 1)
            last_parts(2, 0)
            for b in range(B):
                pool.wait_ge(s_xn, NC * 2 + 2 * b + 2)
                xs = X[:, TB * b:TB * b + TB, :]
                pool.tensor_tensor(xs, xs, bo1[:, :].unsqueeze(1).to_broadcast([P, TB, C]), ALU.add).then_inc(s_xb, 1)

            pool.memset(Rfull, 0.0).then_inc(s_c2, 1)
            pool.memset(regm, 0.0).then_inc(s_c2, 1)
            pool.memset(ones2, 1.0).then_inc(s_c2, 1)
            pool.memset(onesb, 1.0).then_inc(s_c2, 1)
            pool.wait_ge(s_c2, 4)
            for q in range(2):
                v = Rfull[64 * q:64 * q + 64]
                pool.affine_select(out=v, in_=v, compare_op=ALU.not_equal, fill=1.0, base=0,
                                   pattern=[[-REG, 8], [-1, REG]], channel_multiplier=1).then_inc(s_c2, 1)
                pool.wait_ge(s_c2, 5 + q)
            for b in range(B):
                pool.memset(regm[0:REG, TB * b:TB * b + 1], 1.0).then_inc(s_c2, 1)
            pool.wait_ge(s_c2, 6 + B)
            pool.wait_ge(s_qk, 1)
            pool.wait_ge(s_qc, 3)
            pool.tensor_tensor(qgn, qgn, mhalf[:, 0:2], ALU.pow).then_inc(s_qc, 1)
            pool.tensor_scalar(bp2[:, :], bp2[:, :], gates[:, 3:4], None, ALU.mult).then_inc(s_gb2, 1)
            ln_rstd(3)
            for c in range(NC):
                pool.wait_ge(s_qm, c + 1)
                pool.tensor_tensor(PB2[:, 0, 2], res2[:, 0], PB2[:, 0, 1], ALU.subtract).then_inc(s_ql, 1)
                pool.wait_ge(s_km, c + 1)
                pool.tensor_tensor(PB2[:, 1, 2], res2[:, 1], PB2[:, 1, 1], ALU.subtract).then_inc(s_kl, 1)
            pool.wait_ge(s_sc2, 1)
            pool.tensor_tensor(rn2, rn2, mhalf[:, 0:1].to_broadcast([P, 512]), ALU.pow).then_inc(s_rp, 1)
            pool.wait_ge(s_sim, NC)
            pool.wait_ge(s_rp, 1)
            pool.memset(KST[0][NEG_ROW:MAX_ROW + 1], 1.0).then_inc(s_one, 1)
            pool.wait_ge(s_rq, B)
            for j in (1, 2):
                pool.wait_ge(s_one, j)
                pool.memset(KST[j][NEG_ROW:MAX_ROW + 1], 1.0).then_inc(s_one, 1)
            pool.wait_ge(s_one, 3)
            pool.wait_ge(s_kw2, 48 * NC)
            pool.wait_ge(s_qw, 48 * NC)
            for j in range(3):
                pool.memset(VST[j], 0.0).then_inc(s_vpre, 1)
            pool.wait_ge(s_vpre, 3)
            for j in range(3):
                pool.memset(VST[j][:, :, :, D:D + 1], 1.0).then_inc(s_vpre, 1)
            pool.wait_ge(s_vf, NC)

            def stage_values(u, j):
                pool.tensor_copy(VST[j][:, :, :, 0:D].unsqueeze(1),
                                 V2[:, bass.ds(u, 1)].rearrange("p u k (j d) -> p u k j d", j=4)).then_inc(s_vst, 1)

            for j in range(3):
                stage_values(j, j)
            pool.wait_ge(s_gb2, 1)
            pool.wait_ge(s_xn, 4 * NC)
            for b in range(B):
                xs = X[:, TB * b:TB * b + TB, :]
                pool.tensor_tensor(xs, xs, bp2[:, :].unsqueeze(1).to_broadcast([P, TB, C]), ALU.add).then_inc(s_xb2, 1)
            with pool.Fori(0, 4) as i:
                for j in range(3):
                    pool.wait_ge(s_pv2, 2 + 16 * (3 * i + j + 1))
                    stage_values(3 * i + j + 3, j)
            pool.wait_ge(s_pv2, 2 + 16 * 13)
            stage_values(15, 0)

        @block.scalar
        def _(act):
            act.wait_ge(s_g, 32)
            act.activation(gates[:, :], graw, ACT.Tanh).then_inc(s_gt, 1)
            for n, (dst, i, rows, cols) in enumerate(
                    [(kT0[:, j, :], 4 + j, P, 308) for j in range(2)]
                    + [(KW0[:, j, :], 6 + j, P, 308) for j in range(2)]):
                act.wait_ge(s_ks, n + 1)
                act.copy(dst, bank(i)[0:rows, 0:cols]).then_inc(s_ksc, 1)
            for n in range(2):
                act.wait_ge(s_ks, 5 + n)
                act.copy(V0[:, 2 * n:2 * n + 2, :], bank(4 + n)[0:KX, :].rearrange("p (b n) -> p b n", b=2)).then_inc(s_ksc, 1)

            def ln_copy(k):
                for c in range(NC):
                    act.wait_ge(s_tr, NC * k + c + 1)
                    act.copy(XNT[:, :, 512 * c:512 * c + 512],
                             bank(2 * (c % 2), 2).rearrange("p (j t) -> p j t", j=2)).then_inc(s_xt, 1)

            ln_copy(0)
            for b in range(B):
                act.wait_ge(s_nb0, b + 1)
                act.activation(P0[:, b, :], bank(4 + 2 * (b % 2), 2)[0:KX, :], ACT.Exp, bias=nb0[:, b:b + 1],
                               scale=1.0 / 16, accum_out=den0[:, b:b + 1]).then_inc(s_e0, 1)

            for j in range(2):
                act.wait_ge(s_fs, j + 1)
                act.copy(BWt[:, j, 0:NB16], bank(4 + j)[:, 0:NB16]).then_inc(s_fsc, 1)
            act.wait_ge(s_fs, 3)
            act.copy(BW[0:97, :], bank(6)[0:97, 0:C]).then_inc(s_fsc, 1)
            ln_copy(1)
            for c in range(NC):
                act.wait_ge(s_ot, c + 1)
                act.copy(OHT[:, 512 * c:512 * c + 512], bank(4 + c % 2)[0:98, :]).then_inc(s_otc, 1)
            for c in range(NC):
                v = attn[:, 4 * c:4 * c + 4, :]
                act.wait_ge(s_ad, c + 1)
                act.activation(v, v, ACT.Exp, scale=C ** -0.5).then_inc(s_ae, 1)
            for c in range(NC):
                act.wait_ge(s_at, c + 1)
                act.copy(aT[:, 512 * c:512 * c + 512], bank(6 + c % 2)[0:L, :]).then_inc(s_atc, 1)
            act.wait_ge(s_atc, NC)
            for c in range(NC):
                act.wait_ge(s_dl, c + 1)
                act.activation(comb[:, 4 * c:4 * c + 4, :],
                               bank(2 * (c % 2), 2).rearrange("p (i n) -> p i n", i=4), ACT.Exp,
                               scale=fscale).then_inc(s_de, 1)
            for c in range(NC):
                v = comb[:, 4 * c:4 * c + 4, :]
                act.wait_ge(s_z2, c + 1)
                act.activation(v, v, ACT.Ln).then_inc(s_ln, 1)

            act.wait_ge(s_k1, 1)
            act.copy(k1T, bank(4, 2).rearrange("p (j n) -> p j n", j=2)[:, :, 0:308]).then_inc(s_k1c, 1)
            act.wait_ge(s_k1, 2)
            act.copy(kpart[:, 0], bank(6, 2).rearrange("p (j n) -> p j n", j=2)[:, :, 0:308]).then_inc(s_k1c, 1)
            act.wait_ge(s_kr, 1)
            act.wait_ge(s_v1, 1)
            act.wait_ge(s_v1m, 2)
            for j in range(2):
                act.copy(V1a[:, :, 8 * j:8 * j + 8, 0:D],
                         bank(4 + j)[0:KX, :].rearrange("p (b h d) -> p b h d", b=B, h=8)).then_inc(s_v1c, 1)

            for n in range(NC):
                act.wait_ge(s_tr, NC * 2 + n + 1)
                if n >= 2:
                    act.wait_ge(s_pw[n % 2], 16 * (n // 2))
                act.copy(PB[:, n % 2, 0], bank(2 * (n % 2), 2).rearrange("p (j t) -> p j t", j=2)).then_inc(s_ph, 1)
                act.wait_ge(s_pr, n + 1)
                act.copy(PB[:, n % 2, 1], xres[:, n % 2]).then_inc(s_pm, 1)

            def max_rows1(u):
                for q in range(2):
                    act.wait_ge(s_mt, 2 * u + q + 1)
                    if u >= 1:
                        act.wait_ge(s_sc, 8 * u - 4 + 4 * q)
                    act.copy(mrow[:, 512 * q:512 * q + 512], bank(2)[0:4, :]).then_inc(s_mrc, 1)

            def copy_out1(m):
                act.wait_ge(s_pv, m + 1)
                if m >= 2:
                    act.wait_ge(s_ot1, m - 1)
                act.copy(Oe[:, m % 2], bank(7)).then_inc(s_oc, 1)

            max_rows1(0)
            for m in range(2 * UNITS):
                if m >= 2:
                    act.wait_ge(s_pv, m - 1)
                for j in range(4):
                    n = 4 * m + j
                    act.wait_ge(s_sc, n + 1)
                    act.activation(P1[:, m % 2, j, :], bank(4 + n % 3)[0:KX, :], ACT.Exp,
                                   scale=0.25).then_inc(s_e1, 1)
                if m >= 1:
                    copy_out1(m - 1)
                if m % 2 == 1 and m + 1 < 2 * UNITS:
                    max_rows1(m // 2 + 1)
            copy_out1(2 * UNITS - 1)

            def heads_copy(k):
                for c in range(NC):
                    n = NC * k + c
                    act.wait_ge(s_onT, n + 1)
                    if n >= 2:
                        act.wait_ge(s_wo, n - 1)
                    act.copy(OnT[:, c % 2], bank(2 * (c % 2), 2).rearrange("p (j t) -> p j t", j=2)).then_inc(s_onc, 1)

            heads_copy(0)

            act.wait_ge(s_onT, NC)
            for c in range(NC):
                act.wait_ge(s_tr, NC * 3 + c + 1)
                act.copy(XNT[:, :, 512 * c:512 * c + 512],
                         bank(2 * (c % 2), 2).rearrange("p (j t) -> p j t", j=2)).then_inc(s_xt, 1)
            for c in range(NC):
                q = bank(2, 2).rearrange("p (j t) -> p j t", j=2)
                act.wait_ge(s_qp, 3 * c + 1)
                if c >= 2:
                    act.wait_ge(s_sim, c - 1)
                    act.wait_ge(s_qrr, c // 2)
                act.copy(Qf[:, c % 2], q).then_inc(s_qf, 1)
                act.wait_ge(s_qf, c + 1)
                if c >= 1:
                    act.wait_ge(s_qw, 48 * c)
                act.copy(PB2[:, 0, 0], Qf[:, c % 2]).then_inc(s_qh, 1)
                act.activation(Qsq[:, c % 2], Qf[:, c % 2], ACT.Square).then_inc(s_qs, 1)
                act.wait_ge(s_qr, c + 1)
                act.copy(PB2[:, 0, 1], res2[:, 0]).then_inc(s_qm, 1)
                act.wait_ge(s_kf, c + 1)
                if c >= 1:
                    act.wait_ge(s_kw2, 48 * c)
                act.copy(PB2[:, 1, 0], KT[:, :, 512 * c:512 * c + 512]).then_inc(s_kh, 1)
                act.wait_ge(s_krs, c + 1)
                act.copy(PB2[:, 1, 1], res2[:, 1]).then_inc(s_km, 1)
            for b in range(B):
                act.wait_ge(s_rm, 2 * b + 2)
                if b >= 1:
                    act.wait_ge(s_rpt, b)
                act.activation(Pn, bank(2 + 2 * (b % 2), 2), ACT.Exp, bias=rnm[:, b:b + 1], scale=0.25,
                               accum_out=rden[:, b:b + 1]).then_inc(s_rex, 1)
                act.wait_ge(s_rpt, b + 1)
                if b >= 1:
                    act.wait_ge(s_rv, b)
                act.copy(PnT, bank(6, 2).rearrange("p (k n) -> p k n", k=TB)).then_inc(s_rpc, 1)
            act.wait_ge(s_rv, B)

            def body_act(u, j):
                for s in range(16):
                    act.wait_ge(s_pv2, 16 * u + s + 1)
                    for h in range(4):
                        n = 4 * s + h
                        act.wait_ge(s_sco, 64 * u + n + 1)
                        act.activation(PR[:, s % 2, h, :], bank(4 + (64 * j + n) % 3), ACT.Exp,
                                       scale=0.25).then_inc(s_sfree, 1)
                    if s in (8, 15):
                        act.wait_ge(s_pv2, 16 * u + s // 8 * 8 + 8 + 2 if s == 15 else 16 * u + 10)
                        act.copy(Oe2[:, s // 15, :], bank(7)).then_inc(s_oe2, 1)

            act.sem_inc(s_sfree, 3)
            act.sem_inc(s_oe2, 1)
            with act.Fori(0, 5) as i:
                for j in range(3):
                    body_act(3 * i + j, j)
            body_act(15, 0)
            for c in range(NC):
                n = NC + c
                act.wait_ge(s_onT, n + 1)
                if c >= 2:
                    act.wait_ge(s_wo, n - 1)
                act.copy(OnT2[:, c % 2], bank(2 * (c % 2), 2).rearrange("p (j t) -> p j t", j=2)).then_inc(s_onc, 1)

        @block.tensor
        def _(pe):
            pe.wait_ge(s_w0, 64)
            for j in range(2):
                for i in range(2):
                    mm = pe.matmul(bank(4 + j)[:, 0:308], wk0[:, i, P * j:P * j + P], ctxT[:, i, :],
                                   start=(i == 0), stop=(i == 1))
                mm.then_inc(s_ks, 1)
            pe.wait_ge(s_ksc, 2)
            for j in range(2):
                for i in range(2):
                    mm = pe.matmul(bank(6 + j)[:, 0:308], wq0[:, i, P * j:P * j + P], kT0[:, i, :],
                                   start=(i == 0), stop=(i == 1))
                mm.then_inc(s_ks, 1)
            for n in range(2):
                for b in (2 * n, 2 * n + 1):
                    for i in range(2):
                        mm = pe.matmul(bank(4 + n)[0:KX, C * (b % 2):C * (b % 2) + C],
                                       ctxT[:, i, KX * b:KX * b + KX], wv0[:, i, :],
                                       start=(i == 0 and b % 2 == 0), stop=(i == 1), skip_group_check=True)
                mm.then_inc(s_ks, 1)

            def ln_transposes(k):
                pe.wait_ge(s_const, 8)
                for c in range(NC):
                    pe.wait_ge(s_xn, NC * k + c + 1)
                    if NC * k + c >= 2:
                        pe.wait_ge(s_xt, NC * k + c - 1)
                    for j in range(2):
                        for i in range(4):
                            mm = pe.transpose(bank(2 * (c % 2) + j)[:, P * i:P * i + P],
                                              ln_chunk_buf(c)[:, i, P * j:P * j + P], identF[:, :])
                    mm.then_inc(s_tr, 1)

            ln_transposes(0)

            def scores0(b):
                if b < 2:
                    pe.wait_ge(s_ksc, 6)
                else:
                    pe.wait_ge(s_e0, b - 1)
                for q in range(2):
                    for i in range(2):
                        mm = pe.matmul(bank(4 + 2 * (b % 2) + q)[0:KX, :], KW0[:, i, KX * b:KX * b + KX],
                                       XNT[:, i, S * b + 512 * q:S * b + 512 * q + 512],
                                       start=(i == 0), stop=(i == 1))
                mm.then_inc(s_s0, 1)

            pe.wait_ge(s_xt, NC)
            scores0(0)
            for b in range(B):
                if b + 1 < B:
                    scores0(b + 1)
                pe.wait_ge(s_v0, b + 1)
                for g in range(4):
                    n = 4 * b + g
                    if n >= 4:
                        pe.wait_ge(s_x1, n - 3)
                    for i in range(2):
                        q = P * (2 * g + i)
                        mm = pe.matmul(bank(g)[:, C * i:C * i + C], P0[:, b, q:q + P], V0s[:, b, :],
                                       start=(i == 0), stop=True, skip_group_check=True)
                    mm.then_inc(s_o0, 1)

            pe.wait_ge(s_wf, 16 * 9)
            pe.wait_ge(s_e0, B)
            for j in range(2):
                for i in range(2):
                    mm = pe.matmul(bank(4 + j)[:, 0:NB16], wtT[:, i, P * j:P * j + P], ballT[:, i, :],
                                   start=(i == 0), stop=(i == 1))
                mm.then_inc(s_fs, 1)
            pe.wait_ge(s_fsc, 2)
            for j in range(2):
                mm = pe.matmul(bank(6)[0:97, 0:C], BWt[:, j, :], wdT[:, j, :], start=(j == 0), stop=(j == 1))
            mm.then_inc(s_fs, 1)
            pe.wait_ge(s_x1, 4 * B)
            ln_transposes(1)
            for i in range(NT):
                pe.wait_ge(s_xt, NC + i // 4 + 1)
                for j in range(2):
                    mm = pe.matmul(bank(7)[:, E * i:E * i + E], XNT[:, j, P * i:P * i + P], wg[:, j, :],
                                   start=(i == 0 and j == 0), stop=(j == 1), skip_group_check=True)
            mm.then_inc(s_gl, 1)
            pe.wait_ge(s_gc, 7)
            pe.wait_ge(s_fsc, 3)
            for c in range(NC):
                if c >= 2:
                    pe.wait_ge(s_otc, c - 1)
                for i in range(4):
                    mm = pe.matmul(bank(4 + c % 2)[0:98, P * i:P * i + P], OH96[:, 4 * c + i, :], identB[:, :],
                                   start=True, stop=True)
                mm.then_inc(s_ot, 1)
            for c in range(NC):
                if c >= 2:
                    pe.wait_ge(s_ys, c - 1)
                for j in range(2):
                    mm = pe.matmul(bank(6 + c % 2)[0:NB16, :], ballT[:, j, :], XNT[:, j, 512 * c:512 * c + 512],
                                   start=(j == 0), stop=(j == 1))
                mm.then_inc(s_y, 1)
            pe.wait_ge(s_otc, NC)
            for c in range(NC):
                pe.wait_ge(s_ys, c + 1)
                if c >= 2:
                    pe.wait_ge(s_ad, c - 1)
                for i in range(4):
                    t = 512 * c + P * i
                    mm = pe.matmul(bank(4 + c % 2)[:, L * i:L * i + L], ysel[:, t:t + P], AT[0:NB16, :],
                                   start=(i == 0), stop=True, skip_group_check=True)
                mm.then_inc(s_lg, 1)
            for c in range(NC):
                pe.wait_ge(s_an, c + 1)
                if c >= 2:
                    pe.wait_ge(s_atc, c - 1)
                for i in range(4):
                    mm = pe.transpose(bank(6 + c % 2)[0:L, P * i:P * i + P], attn[:, 4 * c + i, :], identF[:, :])
                mm.then_inc(s_at, 1)
            for c in range(NC):
                pe.wait_ge(s_atc, c + 1)
                if c >= 2:
                    pe.wait_ge(s_us, c - 1)
                else:
                    pe.wait_ge(s_ad, NC)
                pe.matmul(bank(4 + c % 2)[0:98, :], A1x[0:L, :], aT[:, 512 * c:512 * c + 512],
                          start=True, stop=True).then_inc(s_u, 1)
            for c in range(NC):
                pe.wait_ge(s_us, c + 1)
                if c >= 2:
                    pe.wait_ge(s_de, c - 1)
                for i in range(4):
                    t = 512 * c + P * i
                    o = bank(2 * (c % 2) + i // 2)[:, C * (i % 2):C * (i % 2) + C]
                    pe.matmul(o, usel[:, t:t + P], BW[0:98, :], start=(i % 2 == 0), stop=False,
                              skip_group_check=True)
                    for j in range(2):
                        mm = pe.matmul(o, XNT[:, j, t:t + P], wdT[:, j, :], start=False, stop=(j == 1),
                                       skip_group_check=True)
                mm.then_inc(s_dl, 1)

            pe.wait_ge(s_bd, 3)
            pe.wait_ge(s_us, NC)
            for j in range(2):
                mm = pe.matmul(bank(4 + j)[:, 0:308], bd[:, 1, :], ctxT[:, j, :], start=True, stop=True)
            mm.then_inc(s_k1, 1)
            pe.wait_ge(s_k1c, 1)
            for j in range(2):
                mm = pe.matmul(bank(6 + j)[:, 0:308], bd[:, 2, :], k1T[:, j, :], start=True, stop=True)
            mm.then_inc(s_k1, 1)
            for j in range(2):
                for b in range(B):
                    mm = pe.matmul(bank(4 + j)[0:KX, P * b:P * b + P], ctxT[:, j, KX * b:KX * b + KX], bd[:, 0, :],
                                   start=(b == 0), stop=True, skip_group_check=True)
            mm.then_inc(s_v1, 1)
            pe.wait_ge(s_de, NC)
            for c in range(NC):
                pe.wait_ge(s_xn, NC * 2 + c + 1)
                if c >= 2:
                    pe.wait_ge(s_pr, c - 1)
                for j in range(2):
                    for i in range(4):
                        mm = pe.transpose(bank(2 * (c % 2) + j)[:, P * i:P * i + P],
                                          ln_chunk_buf(c)[:, i, P * j:P * j + P], identF[:, :])
                mm.then_inc(s_tr, 1)
            pe.wait_ge(s_pr, NC)
            pe.wait_ge(s_k1s, 16 * STACK_DMAS)
            pe.wait_ge(s_mk1, 3)
            pe.wait_ge(s_v1c, 2)

            def max_product1(u, qs):
                b, hg = u // 4, u % 4
                pe.wait_ge(s_xs[u % 3], 16 * STACK_DMAS * (u // 3 + 1))
                for q in qs:
                    n = 8 * u + q
                    if n >= 2:
                        pe.wait_ge(s_mr, n - 1)
                    o = bank(n % 2)[:, 0:4 * KX]
                    pe.matmul(o, mb1[:, P * q:P * q + P], I4, start=True, stop=False, skip_group_check=True)
                    for j in range(4):
                        mm = pe.matmul(o[:, KX * j:KX * j + KX], Xs[u % 3][:, j, P * q:P * q + P],
                                       K1s[:, 4 * hg + j, KX * b:KX * b + KX], start=False, stop=True,
                                       skip_group_check=True)
                    mm.then_inc(s_mp, 1)

            def max_transposes1(u):
                pe.wait_ge(s_mn, u + 1)
                for q in range(2):
                    if 2 * u + q >= 1:
                        pe.wait_ge(s_mrc, 2 * u + q)
                    for i in range(4):
                        mm = pe.transpose(bank(2)[0:4, P * i:P * i + P], Mn[:, u % 2, 4 * q + i, :], identF[:, :])
                    mm.then_inc(s_mt, 1)

            def scores1(m):
                u, q = m // 2, m % 2
                b, hg = u // 4, u % 4
                pe.wait_ge(s_mrc, m + 1)
                for j in range(4):
                    n = 4 * m + j
                    if n >= 3:
                        pe.wait_ge(s_e1, n - 2)
                    o = bank(4 + n % 3)[0:KX, :]
                    t = slice(512 * q, 512 * q + 512)
                    pe.matmul(o, K1s[:, 4 * hg + j, KX * b:KX * b + KX], Xs[u % 3][:, j, t], start=True, stop=False)
                    pe.matmul(o, I4[:, 0:KX], mb1[:, t], start=False, stop=False)
                    pe.matmul(o, HS[:, j, :], mrow[:, t], start=False, stop=True).then_inc(s_sc, 1)

            def values1(m):
                u = m // 2
                pe.wait_ge(s_e1, 4 * m + 4)
                if m >= 1:
                    pe.wait_ge(s_oc, m)
                for j in range(4):
                    mm = pe.matmul(bank(7)[32 * j:32 * j + 32, :], V1a[:, u // 4, 4 * (u % 4) + j, :],
                                   P1[:, m % 2, j, :], start=True, stop=True)
                mm.then_inc(s_pv, 1)

            def out_transposes1(m):
                pe.wait_ge(s_oc, m + 1)
                if m >= 1:
                    pe.wait_ge(s_on, m)
                for i in range(4):
                    mm = pe.transpose(bank(3)[:, P * i:P * i + P], Oe[:, m % 2, P * i:P * i + P], identF[:, :])
                mm.then_inc(s_ot1, 1)

            max_product1(0, range(8))
            max_transposes1(0)
            for m in range(2 * UNITS):
                if m // 2 + 1 < UNITS:
                    max_product1(m // 2 + 1, range(4 * (m % 2), 4 * (m % 2) + 4))
                scores1(m)
                if m >= 1:
                    values1(m - 1)
                if m >= 2:
                    out_transposes1(m - 2)
                if m % 2 == 1 and m // 2 + 1 < UNITS:
                    max_transposes1(m // 2 + 1)
            values1(2 * UNITS - 1)
            out_transposes1(2 * UNITS - 2)
            out_transposes1(2 * UNITS - 1)

            def project(k, weights, ready):
                def transposes(c):
                    n = NC * k + c
                    ready(c)
                    if n >= 2:
                        pe.wait_ge(s_onc, n - 1)
                    for j in range(2):
                        for i in range(4):
                            mm = pe.transpose(bank(2 * (c % 2) + j)[:, P * i:P * i + P],
                                              On[:, 4 * c + i, P * j:P * j + P], identF[:, :])
                    mm.then_inc(s_onT, 1)

                transposes(0)
                for c in range(NC):
                    n = NC * k + c
                    if c + 1 < NC:
                        transposes(c + 1)
                    pe.wait_ge(s_onc, n + 1)
                    if n >= 2:
                        pe.wait_ge(s_x3, n - 1)
                    for i in range(4):
                        o = bank(4 + 2 * (c % 2) + i // 2)[:, C * (i % 2):C * (i % 2) + C]
                        for j in range(2):
                            mm = pe.matmul(o, OnT[:, c % 2, j, P * i:P * i + P], weights[:, j, :],
                                           start=(i % 2 == 0 and j == 0), stop=(j == 1), skip_group_check=True)
                    mm.then_inc(s_wo, 1)

            pe.wait_ge(s_on, 2 * UNITS)
            project(0, wo1, lambda c: None)

            pe.wait_ge(s_qc, 2)
            pe.wait_ge(s_x3, NC)
            pe.matmul(bank(6)[:, 0:2], BBm, qg2, start=True, stop=True).then_inc(s_qk, 1)
            pe.wait_ge(s_onc, NC)
            for c in range(NC):
                pe.wait_ge(s_xn, NC * 3 + c + 1)
                if c >= 2:
                    pe.wait_ge(s_xt, NC * 2 + c - 1)
                for j in range(2):
                    for i in range(4):
                        mm = pe.transpose(bank(2 * (c % 2) + j)[:, P * i:P * i + P],
                                          ln_chunk_buf(c)[:, i, P * j:P * j + P], identF[:, :])
                mm.then_inc(s_tr, 1)
            pe.wait_ge(s_xt, 3 * NC)
            pe.wait_ge(s_wq3, 16)
            pe.wait_ge(s_qc, 7)

            def sim_products(c):
                pe.wait_ge(s_qs, c + 1)
                for i in range(4):
                    for j in range(2):
                        o = 16 * (4 * c + i) + 8 * j
                        first = c == 0 and i == 0 and j == 0
                        pe.matmul(bank(0)[:, o:o + 8], Qsq[:, c % 2, j, P * i:P * i + P], blk[:, :],
                                  start=first, stop=True, skip_group_check=True)
                        mm = pe.matmul(bank(1)[:, o:o + 8], Qf[:, c % 2, j, P * i:P * i + P], qgb[:, j, :],
                                       start=first, stop=True, skip_group_check=True)
                mm.then_inc(s_sim, 1)

            for c in range(NC):
                t = slice(512 * c, 512 * c + 512)
                for kind in range(2):
                    if c >= 1:
                        if kind == 0:
                            pe.wait_ge(s_qf, c)
                        else:
                            pe.wait_ge(s_kf, c)
                    for j in range(2):
                        for i in range(2):
                            mm = pe.matmul(bank(2 + 2 * kind + j), wqkv[:, i, C * kind + P * j:C * kind + P * j + P],
                                           XNT[:, i, t], start=(i == 0), stop=(i == 1))
                    mm.then_inc(s_qp, 1)
                if c >= 1:
                    pe.wait_ge(s_vf, c)
                for i in range(4):
                    for j in range(2):
                        mm = pe.matmul(bank(6 + i // 2)[:, C * (i % 2):C * (i % 2) + C],
                                       XNT[:, j, 512 * c + P * i:512 * c + P * i + P], wqkv[:, j, 2 * C:3 * C],
                                       start=(i % 2 == 0 and j == 0), stop=(j == 1), skip_group_check=True)
                mm.then_inc(s_qp, 1)
                if c >= 1:
                    sim_products(c - 1)
            sim_products(NC - 1)
            pe.wait_ge(s_sc2, 9)
            pe.transpose(bank(2)[0:2, 0:P], mm2, identF[:, :]).then_inc(s_mmt, 1)
            pe.wait_ge(s_sc2, 11)
            pe.matmul(bank(3)[:, 0:2], ones2, mmd, start=True, stop=True).then_inc(s_mmb, 1)
            pe.wait_ge(s_sc2, CLS_DONE - 1)
            pe.transpose(bank(2)[:, 0:P], cls.rearrange("p k i -> p (k i)"), identF[:, :]).then_inc(s_clt, 1)
            pe.wait_ge(s_sc2, CLS_DONE)
            pe.wait_ge(s_crl, 16)

            def register_scores(b):
                if b >= 2:
                    pe.wait_ge(s_rex, b - 1)
                for q in range(2):
                    t = slice(S * b + 512 * q, S * b + 512 * q + 512)
                    for j in range(2):
                        o = bank(2 + 2 * (b % 2) + q)[64 * j:64 * j + 64, :]
                        pe.matmul(o, Qbd[:, b, j, :], KT[:, j, t], start=True, stop=False)
                        mm = pe.matmul(o, onesb, crow[:, t], start=False, stop=True)
                mm.then_inc(s_rq, 1)

            pe.wait_ge(s_qrr, B + 3)
            register_scores(0)
            for b in range(B):
                if b + 1 < B:
                    register_scores(b + 1)
                pe.wait_ge(s_rex, b + 1)
                if b >= 1:
                    pe.wait_ge(s_rpc, b)
                for k in range(TB):
                    mm = pe.transpose(bank(6 + k // 4)[:, P * (k % 4):P * (k % 4) + P], Pn[:, P * k:P * k + P],
                                      identF[:, :])
                mm.then_inc(s_rpt, 1)
                pe.wait_ge(s_rpc, b + 1)
                if b >= 1:
                    pe.wait_ge(s_rk, 2 * b)
                for j in range(2):
                    for k in range(TB):
                        mm = pe.matmul(bank(0)[64 * j:64 * j + 64, 0:P], PnT[:, k, 64 * j:64 * j + 64],
                                       V2[:, 4 * b + 2 * j:4 * b + 2 * j + 2, k, :],
                                       start=(k == 0), stop=(k == TB - 1))
                mm.then_inc(s_rv, 1)
                pe.wait_ge(s_rk, 2 * b + 2)
                if b >= 1:
                    pe.wait_ge(s_rgn, b)
                pe.matmul(bank(1)[0:REG, 0:C], Rsel, omk.rearrange("p j n -> p (j n)"),
                          start=True, stop=True).then_inc(s_rsm, 1)
            pe.wait_ge(s_rgn, B)
            pe.wait_ge(s_vpre, 6)

            def take_turn(n, k):
                pe.wait_ge(s_tfree, n + 1)
                return bank(2 * (k % 2), 2)

            def max_tile(n, k, a, j):
                pl = take_turn(n, k)
                q, h = a // 4, a % 4
                for i in range(2):
                    mm = pe.matmul(pl[:, 512 * i:512 * i + 512], QST[j][0:MAX_ROW, h, P * q:P * q + P],
                                   KST[j][0:MAX_ROW, h, 512 * i:512 * i + 512], start=True, stop=True)
                mm.then_inc(s_turn, 1)

            def max_rows(n, k, half, seen):
                pl = take_turn(n, k)
                pe.wait_ge(s_neg, seen)
                pe.transpose(pl[0:16, 0:P], MXn[:, half].rearrange("p j q -> p (j q)"), identF[:, :]).then_inc(s_turn, 1)

            def out_turn(n, k, half, seen):
                pl = take_turn(n, k)
                pe.wait_ge(s_oe2, seen)
                for i in range(4):
                    mm = pe.transpose(pl[:, P * i:P * i + P], Oe2[:, half, P * i:P * i + P], identF[:, :])
                mm.then_inc(s_turn, 1)

            def values2(u, s, j):
                half, k = s // 8, s % 8
                pe.wait_ge(s_sfree, 3 + 64 * u + 4 * s + 4)
                if k == 0:
                    pe.wait_ge(s_oe2, 2 * u + half + 1)
                for h in range(4):
                    mm = pe.matmul(bank(7)[32 * h:32 * h + 32, :], VST[j][:, k, h, :], PR[:, s % 2, h, :],
                                   start=(k == 0), stop=(k == TB - 1))
                mm.then_inc(s_pv2, 1)

            def body_pe(u, j, loads, last=False):
                base = TURNS0 + TURNS * u
                jn = (j + 1) % 3
                k = 0
                pe.wait_ge(s_vst, u + 1)
                if not last:
                    pe.wait_ge(s_stk[jn], 16 * STACK2_DMAS * loads)
                for s in range(16):
                    half = s // 8
                    if s % 8 == 0:
                        pe.wait_ge(s_row[half], 16 * (u + 1))
                    for h in range(4):
                        n = 4 * s + h
                        pe.wait_ge(s_sfree, 64 * u + n + 1)
                        pe.matmul(bank(4 + (64 * j + n) % 3), KST[j][0:MAX_ROW + 1, h, P * (s % 8):P * (s % 8) + P],
                                  QST[j][0:MAX_ROW + 1, h, 512 * half:512 * half + 512],
                                  start=True, stop=True).then_inc(s_sco, 1)
                        if h % 2 == 1:
                            for what, arg in PLAN_LAST[2 * s + h // 2] if last else PLAN[2 * s + h // 2]:
                                if what == "tile":
                                    max_tile(base + k, k, arg, jn)
                                elif what == "rows":
                                    max_rows(base + k, k, arg, 2 * u + 2 if arg else 2 * u + 3)
                                else:
                                    out_turn(base + k, k, arg, 2 * u + 2 + arg)
                                k += 1
                    if s >= 1:
                        values2(u, s - 1, j)
                values2(u, 15, j)
                for what, arg in PLAN_LAST[32] if last else PLAN[32]:
                    if what == "tile":
                        max_tile(base + k, k, arg, jn)
                    else:
                        out_turn(base + k, k, arg, 2 * u + 2 + arg)
                    k += 1

            pe.sem_inc(s_pv2, 2)
            pe.wait_ge(s_stk[0], 16 * STACK2_DMAS)
            for a in range(16):
                max_tile(a, a + 1, a, 0)
            max_rows(16, 17, 0, 1)
            for a in range(16, 32):
                max_tile(a + 1, a + 2, a, 0)
            pe.wait_ge(s_one, 3)
            with pe.Fori(0, 5) as i:
                for j in range(3):
                    body_pe(3 * i + j, j, i + 1 if j < 2 else i + 2)
            body_pe(15, 0, 0, last=True)

            pe.wait_ge(s_avg, 1)

            def transposes2(c):
                n = NC + c
                if c >= 2:
                    pe.wait_ge(s_onc, n - 1)
                for j in range(2):
                    for i in range(4):
                        b, t = c // 2, 4 * (c % 2) + i
                        mm = pe.transpose(bank(2 * (c % 2) + j)[:, P * i:P * i + P],
                                          On2[:, t, C * b + P * j:C * b + P * j + P], identF[:, :])
                mm.then_inc(s_onT, 1)

            transposes2(0)
            for c in range(NC):
                n = NC + c
                if c + 1 < NC:
                    transposes2(c + 1)
                pe.wait_ge(s_onc, n + 1)
                if c >= 2:
                    pe.wait_ge(s_x3, n - 1)
                for i in range(4):
                    o = bank(4 + 2 * (c % 2) + i // 2)[:, C * (i % 2):C * (i % 2) + C]
                    for j in range(2):
                        mm = pe.matmul(o, OnT2[:, c % 2, j, P * i:P * i + P], wproj[:, j, :],
                                       start=(i % 2 == 0 and j == 0), stop=(j == 1), skip_group_check=True)
                mm.then_inc(s_wo, 1)

        @block.vector
        def _(dve):
            def ln(k, ready, then):
                for b in range(B):
                    ready(b)
                    for i in range(TB * b, TB * b + TB):
                        dve.bn_stats(stats[:, i, :], X[:, i, :]).then_inc(s_st, 1)
                    for i in range(TB * b, TB * b + TB):
                        dve.wait_ge(s_st, NT * k + i + 1)
                        ins_ = dve.bn_aggr(mv[:, i, :], stats[:, i, :])
                    ins_.then_inc(s_ag, 1)
                for c in range(NC):
                    dve.wait_ge(s_rs, 2 * (B * k + c // 2) + 2)
                    if NC * k + c >= 2:
                        dve.wait_ge(s_tr, NC * k + c - 1)
                    for i in range(4):
                        ins_ = dve.tensor_scalar(ln_chunk_buf(c)[:, i, :], X[:, 4 * c + i, :],
                                                 mv[:, 4 * c + i, 0:1], rstd[:, 4 * c + i:4 * c + i + 1],
                                                 ALU.subtract, ALU.mult)
                    ins_.then_inc(s_xn, 1)
                    then(c)

            ln(0, lambda b: dve.wait_ge(s_x[b], 16), lambda c: None)
            dve.wait_ge(s_const, 8)
            dve.wait_ge(s_m0, 64)
            dve.wait_ge(s_gt, 1)
            for b in range(B):
                sc = bank(4 + 2 * (b % 2), 2)[0:KX, :]
                dve.wait_ge(s_s0, b + 1)
                dve.copy_predicated(sc, M0[:, b, :], masked.to_broadcast([KX, S])).then_inc(s_mk0, 1)
                dve.wait_ge(s_mk0, b + 1)
                dve.tensor_reduce(mx0[:, b:b + 1], sc, AX, ALU.max).then_inc(s_mx0, 1)
                dve.wait_ge(s_mx0, b + 1)
                dve.tensor_scalar(nb0[:, b:b + 1], mx0[:, b:b + 1], -1.0 / 16, None, ALU.mult).then_inc(s_nb0, 1)
                dve.wait_ge(s_e0, b + 1)
                dve.reciprocal(rd0[:, b:b + 1], den0[:, b:b + 1]).then_inc(s_rd0, 1)
                dve.wait_ge(s_rd0, b + 1)
                dve.tensor_scalar(V0s[:, b, :], V0[:, b, :], rd0[:, b:b + 1], gates[0:KX, 0:1],
                                  ALU.mult, ALU.mult).then_inc(s_v0, 1)
                for g in range(4):
                    dve.wait_ge(s_o0, 4 * b + g + 1)
                    xs = X[:, TB * b + 2 * g:TB * b + 2 * g + 2, :]
                    dve.tensor_tensor(xs, bank(g).rearrange("p (i c) -> p i c", i=2), xs, ALU.add).then_inc(s_x1, 1)

            def gated_ln(c):
                if c >= 2:
                    dve.wait_ge(s_xg, c - 1)
                dve.wait_ge(s_xn, NC + c + 1)
                xs = X[:, 4 * c:4 * c + 4, :]
                dve.scalar_tensor_tensor(xs, ln_chunk_buf(c), gates[:, 2:3], xs, ALU.mult, ALU.add).then_inc(s_xg, 1)

            ln(1, lambda b: dve.wait_ge(s_x1, 4 * b + 4), gated_ln)
            G = bank(7)[:, 0:E * NT].rearrange("p (i e) -> p i e", e=E)
            dve.wait_ge(s_fc, 2 + E)
            dve.wait_ge(s_gl, 1)
            dve.tensor_reduce(gmx, G, AX, ALU.max).then_inc(s_gc, 1)
            dve.wait_ge(s_gc, 1)
            dve.tensor_tensor(eq6, G, gmx.unsqueeze(2).to_broadcast([P, NT, E]), ALU.is_equal).then_inc(s_gc, 1)
            dve.wait_ge(s_gc, 2)
            dve.tensor_tensor(eq6, eq6, wtie.unsqueeze(1).to_broadcast([P, NT, E]), ALU.mult).then_inc(s_gc, 1)
            dve.wait_ge(s_gc, 3)
            dve.tensor_reduce(gm2, eq6, AX, ALU.max).then_inc(s_gc, 1)
            dve.wait_ge(s_gc, 4)
            dve.tensor_tensor(eq6, eq6, gm2.unsqueeze(2).to_broadcast([P, NT, E]), ALU.is_equal).then_inc(s_gc, 1)
            dve.wait_ge(s_gc, 5)
            dve.tensor_copy(OH96[:, :, 0:NB16].rearrange("p i (e r) -> p i e r", e=E),
                            eq6.unsqueeze(3).to_broadcast([P, NT, E, R])).then_inc(s_gc, 1)
            dve.memset(OH96[:, :, NB16:98], 1.0).then_inc(s_gc, 1)
            for c in range(NC):
                dve.wait_ge(s_otc, c + 1)
                dve.wait_ge(s_y, c + 1)
                v = slice(512 * c, 512 * c + 512)
                dve.tensor_tensor(ysel[:, v], bank(6 + c % 2)[0:NB16, :], OHT[0:NB16, v], ALU.mult).then_inc(s_ys, 1)

            def attn_norm(c):
                v = slice(4 * c, 4 * c + 4)
                dve.wait_ge(s_ae, c + 1)
                dve.tensor_reduce(asum[:, v, :], attn[:, v, :], AX, ALU.add).then_inc(s_as, 1)
                dve.wait_ge(s_as, c + 1)
                dve.reciprocal(arec[:, v, :], asum[:, v, :]).then_inc(s_ar, 1)
                dve.wait_ge(s_ar, c + 1)
                dve.tensor_tensor(attn[:, v, :], attn[:, v, :], arec[:, v, :].to_broadcast([P, 4, L]),
                                  ALU.mult).then_inc(s_an, 1)

            for c in range(NC):
                v = slice(4 * c, 4 * c + 4)
                lg = bank(4 + c % 2)[:, 0:4 * L].rearrange("p (i l) -> p i l", i=4)
                dve.wait_ge(s_lg, c + 1)
                dve.tensor_reduce(amx[:, v, :], lg, AX, ALU.max).then_inc(s_am, 1)
                dve.wait_ge(s_am, c + 1)
                dve.tensor_tensor(attn[:, v, :], lg, amx[:, v, :].to_broadcast([P, 4, L]),
                                  ALU.subtract).then_inc(s_ad, 1)
                if c >= 1:
                    attn_norm(c - 1)
            attn_norm(NC - 1)
            for c in range(NC):
                v = slice(512 * c, 512 * c + 512)
                dve.wait_ge(s_u, c + 1)
                dve.tensor_tensor(usel[:, v], bank(4 + c % 2)[0:98, :], OHT[:, v], ALU.mult).then_inc(s_us, 1)
            for c in range(NC):
                xs = X[:, 4 * c:4 * c + 4, :]
                dve.wait_ge(s_ln, c + 1)
                dve.scalar_tensor_tensor(xs, comb[:, 4 * c:4 * c + 4, :], gates[:, 2:3], xs,
                                         ALU.mult, ALU.add).then_inc(s_x2, 1)

            dve.wait_ge(s_w1, 16 * 28)
            for i in range(3):
                dve.tensor_tensor(bd[:, i, :].rearrange("p (g d) -> p g d", g=8),
                                  w16[:, i, :].unsqueeze(1).to_broadcast([P, 8, 16]),
                                  blk[:, :].unsqueeze(2).to_broadcast([P, 8, 16]), ALU.mult).then_inc(s_bd, 1)
            dve.wait_ge(s_m1, 16)
            dve.tensor_scalar(mb1, M1u, -1.0, BIG, ALU.add, ALU.mult).then_inc(s_mk1, 1)
            dve.tensor_copy(I4.rearrange("p (j n) -> p j n", j=4),
                            identB[0:KX, 0:KX].unsqueeze(1).to_broadcast([KX, 4, KX])).then_inc(s_mk1, 1)
            dve.tensor_copy(HS, identB[0:4, 0:4].unsqueeze(2).to_broadcast([4, 4, KX])).then_inc(s_mk1, 1)
            dve.wait_ge(s_k1c, 2)
            dve.tensor_tensor(kr1, bank(6, 2).rearrange("p (j n) -> p j n", j=2)[:, :, 0:308], kpart[:, 0],
                              ALU.subtract).then_inc(s_kr, 1)
            dve.wait_ge(s_kr, 1)
            dve.tensor_copy(kpart[:, 1], kr1).then_inc(s_kr, 1)
            dve.wait_ge(s_kr, 2)
            dve.tensor_tensor(kr1, kr1, kpart[:, 1], ALU.subtract).then_inc(s_kr, 1)
            dve.wait_ge(s_kr, 3)
            dve.tensor_copy(kpart[:, 2], kr1).then_inc(s_kr, 2)

            def residue(c):
                dve.wait_ge(s_ph, c + 1)
                if c >= 2:
                    dve.wait_ge(s_pl, c - 1)
                dve.tensor_tensor(xres[:, c % 2], bank(2 * (c % 2), 2).rearrange("p (j t) -> p j t", j=2),
                                  PB[:, c % 2, 0], ALU.subtract).then_inc(s_pr, 1)

            ln(2, lambda b: dve.wait_ge(s_x2, 2 * b + 2), lambda c: residue(c - 1) if c >= 1 else None)
            residue(NC - 1)

            def reduce1(u, qs):
                for q in qs:
                    n = 8 * u + q
                    dve.wait_ge(s_mp, n + 1)
                    dve.tensor_reduce(M1[:, u % 2, q, :],
                                      bank(n % 2)[:, 0:4 * KX].rearrange("p (j n) -> p j n", j=4), AX,
                                      ALU.max).then_inc(s_mr, 1)

            def negate1(u):
                if u >= 2:
                    dve.wait_ge(s_mt, 2 * u - 2)
                dve.wait_ge(s_mr, 8 * u + 8)
                dve.tensor_scalar(Mn[:, u % 2], M1[:, u % 2], -1.0, None, ALU.mult).then_inc(s_mn, 1)

            def normalise1(m):
                u, q = m // 2, m % 2
                b, hg = u // 4, u % 4
                O = bank(3).rearrange("p (q j d) -> p q j d", q=4, j=4)
                dve.wait_ge(s_ot1, m + 1)
                if m >= 1:
                    dve.wait_ge(s_on, m)
                dve.reciprocal(rc1, O[:, :, :, D]).then_inc(s_rc, 1)
                dve.wait_ge(s_rc, m + 1)
                dst = On[:, TB * b + 4 * q:TB * b + 4 * q + 4, 64 * hg:64 * hg + 64]
                dve.tensor_tensor(dst.rearrange("p q (j d) -> p q j d", j=4), O[:, :, :, 0:D],
                                  rc1.unsqueeze(3).to_broadcast([P, 4, 4, D]), ALU.mult).then_inc(s_on, 1)

            reduce1(0, range(8))
            negate1(0)
            for u in range(UNITS):
                if u + 1 < UNITS:
                    reduce1(u + 1, range(4))
                if u >= 1:
                    normalise1(2 * u - 2)
                if u + 1 < UNITS:
                    reduce1(u + 1, range(4, 8))
                    negate1(u + 1)
                if u >= 1:
                    normalise1(2 * u - 1)
            normalise1(2 * UNITS - 2)
            normalise1(2 * UNITS - 1)

            def add_projected(k, gate, ready):
                for c in range(NC):
                    dve.wait_ge(s_wo, NC * k + c + 1)
                    ready(c)
                    xs = X[:, 4 * c:4 * c + 4, :]
                    dve.scalar_tensor_tensor(xs, bank(4 + 2 * (c % 2), 2).rearrange("p (i n) -> p i n", i=4),
                                             gate, xs, ALU.mult, ALU.add).then_inc(s_x3, 1)

            add_projected(0, gates[:, 1:2], lambda c: dve.wait_ge(s_xb, c // 2 + 1))

            dve.wait_ge(s_qgl, 16)
            dve.tensor_tensor(qg2, qgc, qgc, ALU.mult).then_inc(s_qc, 1)
            dve.tensor_copy(BBm.rearrange("p (g d) -> p g d", g=8),
                            blk[:, :].unsqueeze(2).to_broadcast([P, 8, 16])).then_inc(s_qc, 1)
            dve.wait_ge(s_qk, 1)
            dve.tensor_copy(qgn, bank(6)[:, 0:2]).then_inc(s_qc, 1)
            dve.wait_ge(s_qc, 4)
            dve.tensor_tensor(qgn, qgn, qgc, ALU.mult).then_inc(s_qc, 1)
            dve.wait_ge(s_qc, 5)
            for j in range(2):
                dve.tensor_scalar(qgb[:, j, :], blk[:, :], qgn[:, j:j + 1], None, ALU.mult).then_inc(s_qc, 1)
            ln(3, lambda b: dve.wait_ge(s_x3, 2 * b + 2), lambda c: None)
            for c in range(NC):
                if c == 0:
                    dve.wait_ge(s_tr, 4 * NC)
                dve.wait_ge(s_qh, c + 1)
                if c >= 1:
                    dve.wait_ge(s_ql, c)
                dve.tensor_tensor(res2[:, 0], Qf[:, c % 2], PB2[:, 0, 0], ALU.subtract).then_inc(s_qr, 1)
                dve.wait_ge(s_qp, 3 * c + 2)
                kt = KT[:, :, 512 * c:512 * c + 512]
                dve.tensor_copy(kt, bank(4, 2).rearrange("p (j t) -> p j t", j=2)).then_inc(s_kf, 1)
                dve.wait_ge(s_kh, c + 1)
                if c >= 1:
                    dve.wait_ge(s_kl, c)
                dve.tensor_tensor(res2[:, 1], kt, PB2[:, 1, 0], ALU.subtract).then_inc(s_krs, 1)
                dve.wait_ge(s_qp, 3 * c + 3)
                b, t = c // 2, 4 * (c % 2)
                for g in range(4):
                    vv = dve.tensor_copy(V2[:, 4 * b + g, t:t + 4, :],
                                         bank(6, 2).rearrange("p (i n) -> p i n", i=4)[:, :, 64 * g:64 * g + 64])
                vv.then_inc(s_vf, 1)
                if c % 2 == 0:
                    dve.wait_ge(s_qf, c + 1)
                    dve.tensor_copy(QR[:, :, b, :], Qf[:, c % 2, :, 0:REG]).then_inc(s_qrr, 1)
            ch = [0]

            def link(ins_, wait=True):
                ch[0] += 1
                ins_.then_inc(s_sc2, 1)
                if wait:
                    dve.wait_ge(s_sc2, ch[0])

            dve.wait_ge(s_sim, NC)
            dve.wait_ge(s_c2, 6 + B)
            link(dve.tensor_copy(rn2, bank(0)))
            dve.wait_ge(s_rp, 1)
            link(dve.tensor_tensor(dt2, bank(1), rn2, ALU.mult))
            assert ch[0] == SIM_READ
            link(dve.tensor_reduce(simr, dt2.rearrange("p (i h) -> p i h", h=H), AX, ALU.add))
            link(dve.tensor_scalar(simc, simr, 1.0 / H, None, ALU.mult))
            link(dve.scalar_tensor_tensor(tmp32, regm, -BIG, simc, ALU.mult, ALU.add))
            link(dve.tensor_reduce(mm2[:, 0:1], tmp32, AX, ALU.max))
            link(dve.scalar_tensor_tensor(tmp32, regm, BIG, simc, ALU.mult, ALU.add))
            link(dve.tensor_reduce(mm2[:, 1:2], tmp32, AX, ALU.min))
            link(dve.tensor_scalar(mm2[:, 1:2], mm2[:, 1:2], -1.0, None, ALU.mult))
            dve.wait_ge(s_mmt, 1)
            link(dve.tensor_reduce(mmr, bank(2)[0:2, 0:P], AX, ALU.max))
            link(dve.tensor_scalar(mmd, identF[0:2, 0:2], mmr, None, ALU.mult))
            dve.wait_ge(s_mmb, 1)
            link(dve.tensor_copy(mmb, bank(3)[:, 0:2]))
            link(dve.tensor_tensor(rng, mmb[:, 0:1], mmb[:, 1:2], ALU.add))
            link(dve.reciprocal(rrg, rng))
            link(dve.tensor_scalar(simc, simc, mmb[:, 1:2], rrg, ALU.add, ALU.mult))
            link(dve.tensor_scalar(tmp32, simc, 0.9, None, ALU.is_gt))
            link(dve.tensor_scalar(simr, regm, -1.0, 1.0, ALU.mult, ALU.add))
            link(dve.tensor_tensor(tmp32, tmp32, simr, ALU.mult))
            link(dve.tensor_tensor(cls[:, 1, :], tmp32, regm, ALU.add))
            link(dve.tensor_scalar(cls[:, 0, :], cls[:, 1, :], -1.0, 1.0, ALU.mult, ALU.add))
            link(dve.tensor_scalar(cls[:, 2, :], tmp32, -BIG, None, ALU.mult))
            link(dve.tensor_scalar(cls[:, 3, :], cls[:, 0, :], -BIG, None, ALU.mult))
            dve.wait_ge(s_clt, 1)
            link(dve.tensor_copy(clsT, bank(2)[:, 0:P]))
            assert ch[0] == CLS_DONE
            dve.memset(W[:, 2048:2816], 0.0).then_inc(s_qrr, 1)
            dve.wait_ge(s_qrr, B + 1)
            for j in range(2):
                dve.tensor_tensor(Qbd[:, :, j, 0:8 * REG].rearrange("p b (g r) -> p b g r", g=8),
                                  QR[:, j].unsqueeze(2).to_broadcast([P, B, 8, REG]),
                                  blk[:, :].unsqueeze(1).unsqueeze(3).to_broadcast([P, B, 8, REG]),
                                  ALU.mult).then_inc(s_qrr, 1)
            dve.tensor_reduce(rmask, Rfull, AX, ALU.add).then_inc(s_c2, 1)
            dve.tensor_reduce(Rsel, Rfull.rearrange("p g r -> p r g"), AX, ALU.add).then_inc(s_c2, 1)
            dve.wait_ge(s_c2, 8 + B)

            def register_values(b):
                dve.wait_ge(s_rex, b + 1)
                dve.reciprocal(rrd[:, b:b + 1], rden[:, b:b + 1]).then_inc(s_rc2, 1)
                dve.wait_ge(s_rc2, b + 1)
                dve.wait_ge(s_rv, b + 1)
                if b >= 1:
                    dve.wait_ge(s_rsm, b)
                for j in range(2):
                    v = slice(64 * j, 64 * j + 64)
                    dve.scalar_tensor_tensor(omk[v, j].rearrange("p (g d) -> p g d", g=8),
                                             bank(0)[v, 0:P].rearrange("p (g d) -> p g d", g=8), rrd[v, b:b + 1],
                                             rmask[v].unsqueeze(2).to_broadcast([64, 8, D]), ALU.mult,
                                             ALU.mult).then_inc(s_rk, 1)
                dve.wait_ge(s_rsm, b + 1)
                dve.tensor_scalar(regn[:, b, :], bank(1)[0:REG, 0:C], 0.5, None, ALU.mult).then_inc(s_rgn, 1)

            for b in range(B):
                dve.wait_ge(s_rq, b + 1)
                dve.tensor_reduce(rmx[:, b:b + 1], bank(2 + 2 * (b % 2), 2), AX, ALU.max).then_inc(s_rm, 1)
                dve.wait_ge(s_rm, 2 * b + 1)
                dve.tensor_scalar(rnm[:, b:b + 1], rmx[:, b:b + 1], -0.25, None, ALU.mult).then_inc(s_rm, 1)
                if b >= 1:
                    register_values(b - 1)
            register_values(B - 1)

            def turn_wait(n):
                dve.wait_ge(s_turn, n + 1)

            def reduce_tile(n, k, a):
                half, q, h = a // 16, a // 4 % 4, a % 4
                turn_wait(n)
                dve.tensor_reduce(MX[:, half, h, q:q + 1], bank(2 * (k % 2), 2), AX, ALU.max).then_inc(s_tfree, 1)

            def negate(n, half):
                dve.wait_ge(s_tfree, 2 + n)
                dve.tensor_scalar(MXn[:, half], MX[:, half], -1.0, None, ALU.mult).then_inc(s_neg, 1)

            def rows_turn(n, k, half):
                turn_wait(n)
                dve.tensor_copy(mro[:, half, :], bank(2 * (k % 2))[0:16, 0:P]).then_inc(s_tfree, 1)

            def normalise2(n, k, u, half):
                O = bank(2 * (k % 2)).rearrange("p (q j d) -> p q j d", q=4, j=4)
                dve.wait_ge(s_tfree, 2 + n)
                turn_wait(n)
                dve.reciprocal(rc2, O[:, :, :, D]).then_inc(s_rc2, 1)
                dve.wait_ge(s_rc2, 2 * u + half + 1 + B)
                dst = On2[:, 4 * half:4 * half + 4, bass.ds(64 * u, 64)].rearrange("p q (j d) -> p q j d", j=4)
                dve.tensor_tensor(dst, O[:, :, :, 0:D], rc2.unsqueeze(3).to_broadcast([P, 4, 4, D]),
                                  ALU.mult).then_inc(s_tfree, 1)

            dve.sem_inc(s_tfree, 2)
            for a in range(16):
                reduce_tile(a, a + 1, a)
            negate(16, 0)
            rows_turn(16, 17, 0)
            for a in range(16, 32):
                reduce_tile(a + 1, a + 2, a)
            negate(33, 1)

            def body_dve(u, j, last=False):
                base = TURNS0 + TURNS * u
                k = 0
                for step in (PLAN_LAST if last else PLAN):
                    for what, arg in step:
                        if what == "tile":
                            reduce_tile(base + k, k, arg)
                        elif what == "rows":
                            rows_turn(base + k, k, arg)
                        else:
                            normalise2(base + k, k, u, arg)
                        k += 1
                        if (what, arg) == ("tile", 15):
                            negate(base + k, 0)
                        if (what, arg) == ("tile", 31):
                            negate(base + k, 1)

            with dve.Fori(0, 5) as i:
                for j in range(3):
                    body_dve(3 * i + j, j)
            body_dve(15, 0, last=True)
            dve.wait_ge(s_tfree, 2 + TURNS0 + TURNS * 15 + 3)
            dve.scalar_tensor_tensor(On2[0:REG, 0, :], On2[0:REG, 0, :], 0.5,
                                     regn.rearrange("p b c -> p (b c)"), ALU.mult,
                                     ALU.add).then_inc(s_avg, 1)
            for c in range(NC):
                dve.wait_ge(s_wo, NC + c + 1)
                dve.wait_ge(s_xb2, c // 2 + 1)
                xs = X[:, 4 * c:4 * c + 4, :]
                dve.scalar_tensor_tensor(xs, bank(4 + 2 * (c % 2), 2).rearrange("p (i n) -> p i n", i=4),
                                         gates[:, 3:4], xs, ALU.mult, ALU.add).then_inc(s_x3, 1)


def kernel(**inputs):
    import numpy as _np
    import concourse.bacc as _bacc
    from concourse import mybir as _mybir
    from concourse.bass_utils import run_bass_kernel_spmd as _run

    i = {k: _np.asarray(v) for k, v in inputs.items()}
    lay = {
        "x": i["x"],
        "ctxT": i["ctx_1024"].transpose(2, 0, 1).reshape(C, B * KX),
        "wk0T": i["L0_xattn_Wk"].T,
        "wq0": i["L0_xattn_Wq"],
        "wv0T": i["L0_xattn_Wv"].T,
        "mask0T": i["mask_BxSxS2_bk0"].transpose(0, 2, 1),
        "mask1T": i["mask_1x1xSxS2_bk0"][0, 0].T,
        "g_xattn": i["g_xattn"],
        "g_ffn": i["g_ffn"],
        "w_gate": i["L0_ffn_w_gate"],
        "ballT": i["L0_ffn_B"].transpose(2, 0, 1).reshape(C, E * R),
        "AT": i["L0_ffn_A"].transpose(0, 2, 1).reshape(E * R, L),
        "A1": i["L0_ffn_A"].transpose(1, 0, 2).reshape(L, E * R),
        "wtT": i["L0_ffn_wt_w"].T,
        "wt_b": i["L0_ffn_wt_b"],
        "wdT": i["L0_ffn_wd_w"].T,
        "wd_b": i["L0_ffn_wd_b"],
        "scale": i["L0_ffn_scale"],
        "wv1T": i["L1_xattn_Wv"].T,
        "wk1T": i["L1_xattn_Wk"].T,
        "wq1": i["L1_xattn_Wq"],
        "wo1T": i["L1_xattn_Wo"].T,
        "bo1": i["L1_xattn_bo"],
        "g_info": i["L1_ffn_g_info"],
        "wqkv": i["L1_ffn_W_qkv"],
        "wproj": i["L1_ffn_W_proj"],
        "bproj": i["L1_ffn_b_proj"],
    }
    nc = _bacc.Bacc("TRN2", target_bir_lowering=False, num_devices=1)
    arrays, args = {}, {}
    for name, a in lay.items():
        a = _np.ascontiguousarray(a)
        arrays[f"in_{name}"] = a
        args[name] = nc.dram_tensor(f"in_{name}", a.shape, _mybir.dt.from_np(a.dtype), kind="ExternalInput").ap()
    out = nc.dram_tensor("out_0", (B, S, C), F32, kind="ExternalOutput").ap()
    build_program(nc, args, out)
    r = _run(nc, [arrays], core_ids=[0])
    return r.results[0]["out_0"]
```

```python
from contextlib import ExitStack

import numpy as np
import concourse.bass as bass
from concourse import mybir

F32 = mybir.dt.float32
BF16 = mybir.dt.bfloat16
U8 = mybir.dt.uint8
ALU = mybir.AluOpType
ACT = mybir.ActivationFunctionType
AX = mybir.AxisListType.X

B, S, C = 4, 1024, 256
KX = 77
H, D = 16, 16
E, L, R = 6, 100, 16
REG = 5
P = 128
T = B * S
NT = T // P
NC = T // 512
TB = S // P
UNITS = B * 4
BIG = 2.0 ** 66
LN_EPS = 1e-5
TINY = float(np.finfo(np.float32).eps)
Q_ORDER, K_ORDER = (0, 0, 0, 1, 1, 2), (0, 1, 2, 0, 1, 0)
SR = 96
NEG_ROW, POS_ROW, MAX_ROW = 96, 97, 98


def build_program(nc, ins, out):
    ctx = ExitStack()
    with ctx:
        def sb(name, shape, dt=F32):
            return ctx.enter_context(nc.sbuf_tensor(name, shape, dt))

        def sem(name):
            return ctx.enter_context(nc.semaphore(name))

        X = sb("X", [P, NT, C])
        R1 = sb("R1", [P, 8192])
        R2 = sb("R2", [P, 8192])
        R3 = sb("R3", [P, 8192])
        R4 = sb("R4", [P, 4096])
        XNT = R1[:, :].rearrange("p (j t) -> p j t", j=2)

        XN = sb("XN", [P, 2, 4, C])
        stats = sb("stats", [P, NT, 6])
        mv = sb("mv", [P, NT, 2])
        rstd = sb("rstd", [P, NT])
        mhalf = sb("mhalf", [P, NT])
        identF = sb("identF", [P, P])
        identB = sb("identB", [P, P], BF16)
        gates = sb("gates", [P, 4])
        small = sb("small", [P, 640])

        ps = ctx.enter_context(nc.psum_tensor("ps", [P, 4096], F32))

        def bank(i, n=1):
            return ps[:, 512 * i:512 * (i + n)]

        W = sb("W", [P, 4608])
        at = [0]

        def w(n):
            at[0] += n
            assert at[0] <= 4608
            return W[:, at[0] - n:at[0]]

        def w2(n):
            return w(2 * n).rearrange("p (j n) -> p j n", j=2)

        ctxT = w2(B * KX)
        wbig = w(1536)
        wk0 = wbig[:, 0:512].rearrange("p (j n) -> p j n", j=2)
        wq0 = wbig[:, 512:1024].rearrange("p (j n) -> p j n", j=2)
        wv0 = wbig[:, 1024:1536].rearrange("p (j n) -> p j n", j=2)
        wqkv = wbig.rearrange("p (j n) -> p j n", j=2)
        wA = w(1616)

        def wa(a, n, j=None):
            v = wA[:, a:a + n]
            return v if j is None else v.rearrange("p (j n) -> p j n", j=j)

        ballg, wtT, wdT = wa(0, 204, 2), wa(204, 512, 2), wa(716, 512, 2)
        ballT, wg = ballg[:, :, 0:96], ballg[:, :, 96:102]
        AT, A1x = wa(1228, 100), wa(1328, 98)
        wtb = wa(1426, 2)
        BW = sb("BW", [P, C])
        BWt = sb("BWt", [P, 2, 97])
        wo1 = sb("wo1", [P, 2, C])
        wproj = sb("wproj", [P, 2, C])
        bo1 = sb("bo1", [P, C])
        bp2 = sb("bp2", [P, C])
        w16 = sb("w16", [P, 3, 16])
        bd = sb("bd", [P, 3, P])
        blk = sb("blk", [P, 8])

        R2f = R2[:, :]
        R3f = R3[:, :]

        s_x = [sem(f"x_loaded{b}") for b in range(B)]
        s_w0 = sem("xattn0_weights_loaded")
        s_m0 = sem("mask0_loaded")
        s_g = sem("gates_loaded")
        s_const = sem("constants_made")
        s_gt = sem("gates_tanh")
        s_ks = sem("setup_product")
        s_ksc = sem("setup_copied")
        s_st = sem("stats_done")
        s_ag = sem("aggregated")
        s_rs = sem("rstd_done")
        s_xn = sem("chunk_normalised")
        s_tr = sem("chunk_transposed")
        s_xt = sem("chunk_transpose_copied")

        R5 = sb("R5", [P, 4096])
        block = ctx.enter_context(nc.Block())
        kT0 = R2f[:, 0:616].rearrange("p (j n) -> p j n", j=2)
        KW0 = R2f[:, 616:1232].rearrange("p (j n) -> p j n", j=2)
        V0 = R2f[0:KX, 1232:2256].rearrange("p (b n) -> p b n", b=B)
        P0 = R2f[0:KX, 2256:6352].rearrange("p (b n) -> p b n", b=B)
        V0s = R2f[0:KX, 6352:7376].rearrange("p (b n) -> p b n", b=B)
        M0 = R3f[0:KX, 0:1024].bitcast(U8).rearrange("p (b n) -> p b n", b=B)
        masked = R3f[0:KX, 1024:1025]
        mx0 = small[0:KX, 0:4]
        nb0 = small[0:KX, 4:8]
        den0 = small[0:KX, 8:12]
        rd0 = small[0:KX, 12:16]
        graw = small[:, 16:20]
        s_s0 = sem("scores0")
        s_mk0 = sem("scores0_masked")
        s_mx0 = sem("scores0_max")
        s_nb0 = sem("scores0_negmax")
        s_e0 = sem("probs0")
        s_rd0 = sem("recip0")
        s_v0 = sem("values0_scaled")
        s_o0 = sem("out0")
        s_x1 = sem("x1_added")

        NB16 = E * R
        OH96 = R3f[:, 0:1568].bitcast(BF16).rearrange("p (i n) -> p i n", i=NT)
        attn = R3f[:, 1568:4768].rearrange("p (i l) -> p i l", i=NT)
        OHT = R4[0:98, 0:2048].bitcast(BF16)
        ysel = R2f[0:NB16, 0:4096]
        yg = R2f[0:NB16 + E, 0:4096]
        usel = R2f[0:98, 0:4096]
        aT = R2f[0:L, 4096:8192]
        comb = R3f.rearrange("p (i c) -> p i c", i=NT)
        zfix = R4[:, 2048:4096].rearrange("p (u n) -> p u n", u=2)
        gmx = small[:, 32:64]
        eq6 = small[:, 64:256].rearrange("p (i e) -> p i e", e=E)
        gm2 = small[:, 256:288]
        wtie = small[:, 288:294]
        amx = small[:, 296:328].rearrange("p (i o) -> p i o", o=1)
        asum = small[:, 328:360].rearrange("p (i o) -> p i o", o=1)
        arec = small[:, 360:392].rearrange("p (i o) -> p i o", o=1)
        fscale = small[:, 392:393]
        s_wf = sem("ffn0_weights_loaded")
        s_fc = sem("ffn0_constants")
        s_fs = sem("ffn0_setup_product")
        s_fsc = sem("ffn0_setup_copied")
        s_xg = sem("gated_ln_added")
        s_gl = sem("gate_logits")
        s_gc = sem("gate_chain")
        s_ot = sem("onehot_transposed")
        s_otc = sem("onehot_copied")
        s_y = sem("y_product")
        s_yc = sem("y_copied")
        s_ys = sem("y_selected")
        s_lg = sem("landmark_logits")
        s_am = sem("landmark_max")
        s_ad = sem("landmark_minus_max")
        s_ae = sem("landmark_exp")
        s_as = sem("landmark_sum")
        s_ar = sem("landmark_recip")
        s_an = sem("landmark_attn")
        s_at = sem("attn_transposed")
        s_atc = sem("attn_copied")
        s_u = sem("u_product")
        s_us = sem("u_selected")
        s_dl = sem("delta_product")
        s_de = sem("delta_exp")
        s_z1 = sem("zero_found")
        s_z2 = sem("zero_replaced")
        s_ln = sem("combined_log")
        s_x2 = sem("x2_added")

        XP = nc.dram_tensor("x_parts", (3, C, T), BF16).ap()
        KXP = nc.dram_tensor("ctx_key_parts", (3, C, B * KX), BF16).ap()
        K1s = R2f[0:SR, 0:2464].bitcast(BF16).rearrange("p (h n) -> p h n", h=H)
        V1a = R2f[0:KX, 2464:4512].rearrange("p (b h d) -> p b h d", b=B, h=H)
        mb1 = R2f[0:KX, 4512:5024].bitcast(BF16)
        M1u = R2f[0:KX, 5024:5280].bitcast(U8)
        I4 = R2f[0:KX, 5280:5434].bitcast(BF16)
        HS = R2f[0:4, 5434:5588].bitcast(BF16).rearrange("p (j n) -> p j n", j=4)
        mrow = R2f[0:4, 5588:6100].bitcast(BF16)
        Oe = R2f[:, 6100:7124].rearrange("p (u n) -> p u n", u=2)
        k1T = R3f[:, 0:616].rearrange("p (j n) -> p j n", j=2)
        kr1 = R3f[:, 616:1232].rearrange("p (j n) -> p j n", j=2)
        kpart = R3f[:, 1232:2156].bitcast(BF16).rearrange("p (a j n) -> p a j n", a=3, j=2)
        P1 = R3f[0:KX, 0:4096].rearrange("p (u j n) -> p u j n", u=2, j=4)
        PB = R3f[:, 4096:7168].bitcast(BF16).rearrange("p (u a j n) -> p u a j n", u=2, a=3, j=2)
        xres = R4[:, 2048:4096].rearrange("p (u j n) -> p u j n", u=2, j=2)
        Xs = [v.bitcast(BF16).rearrange("p (j n) -> p j n", j=4)
              for v in (R4[0:SR, 0:2048], R5[0:SR, 0:2048], R5[0:SR, 2048:4096])]
        On = R1[:, :].rearrange("p (i c) -> p i c", i=NT)
        OnT = R3f[:, 0:2048].rearrange("p (u j n) -> p u j n", u=2, j=2)
        M1 = small[:, 400:464].rearrange("p (u q j) -> p u q j", u=2, q=8)
        Mn = small[:, 464:528].rearrange("p (u q j) -> p u q j", u=2, q=8)
        rc1 = small[:, 528:544].rearrange("p (q j) -> p q j", q=4)
        s_w1 = sem("layer1_weights_loaded")
        s_bd = sem("block_diagonals_made")
        s_k1 = sem("ctx_keys_product")
        s_k1c = sem("ctx_keys_copied")
        s_kr = sem("ctx_keys_residue")
        s_kw = sem("ctx_key_parts_written")
        s_k1s = sem("ctx_key_stack_loaded")
        s_v1 = sem("ctx_values_product")
        s_v1c = sem("ctx_values_copied")
        s_v1m = sem("ctx_values_preset")
        s_mk1 = sem("mask1_made")
        s_m1 = sem("mask1_loaded")
        s_ph = sem("part_h")
        s_pr = sem("part_residue")
        s_pm = sem("part_m")
        s_pl = sem("part_l")
        s_pw = [sem(f"parts_written{n}") for n in range(2)]
        s_xs = [sem(f"x_stack_loaded{n}") for n in range(3)]
        s_mp = sem("max1_product")
        s_mr = sem("max1_reduced")
        s_mn = sem("max1_negated")
        s_mt = sem("max1_transposed")
        s_mrc = sem("max1_rows")
        s_sc = sem("scores1")
        s_e1 = sem("probs1")
        s_pv = sem("values1_product")
        s_oc = sem("out1_copied")
        s_ot1 = sem("out1_transposed")
        s_rc = sem("out1_recip")
        s_on = sem("out1_normalised")
        s_gb = sem("gated_bias")
        s_xb = sem("bias_added")
        s_onT = sem("heads_transposed")
        s_onc = sem("heads_copied")
        s_wo = sem("projected")
        s_x3 = sem("x3_added")

        STACK_DMAS = 6

        QP = nc.dram_tensor("q_parts", (3, B * C, S), BF16).ap()
        KP = nc.dram_tensor("k_parts", (3, B * C, S), BF16).ap()
        MR = nc.dram_tensor("max_rows", (2, 16, P), BF16).ap()
        CR = nc.dram_tensor("class_rows", (4, B, 4, S), BF16).ap()
        KT = R2[:, :].rearrange("p (j t) -> p j t", j=2)
        V2 = R3[:, :].rearrange("p (u k n) -> p u k n", u=UNITS, k=TB)
        On2 = R1[:, :].rearrange("p (k u n) -> p k (u n)", u=UNITS, k=TB)
        PB2 = R5[:, 0:3072].bitcast(BF16).rearrange("p (u a j n) -> p u a j n", u=2, a=3, j=2)
        res2 = XN[:, :, :, :].rearrange("p u i c -> p u (i c)").rearrange("p u (j n) -> p u j n", j=2)
        Qf = R4[:, 0:2048].rearrange("p (u j n) -> p u j n", u=2, j=2)
        Qsq = R4[:, 2048:4096].rearrange("p (u j n) -> p u j n", u=2, j=2)
        QST = [v.bitcast(BF16).rearrange("p (j n) -> p j n", j=4)
               for v in (R4[:, 0:2048], R2[:, 0:2048], R2[:, 4096:6144])]
        KST = [v.bitcast(BF16).rearrange("p (j n) -> p j n", j=4)
               for v in (R4[:, 2048:4096], R2[:, 2048:4096], R2[:, 6144:8192])]
        VST = [R5[:, 1024 * n:1024 * n + 1024].rearrange("p (k j d) -> p k j d", k=TB, j=4) for n in range(3)]
        regn = R5[0:REG, 3072:4096].rearrange("p (b c) -> p b c", b=B)
        PR = W[:, 0:4096].rearrange("p (u j n) -> p u j n", u=2, j=4)
        XNf = XN[:, :, :, :].rearrange("p u i c -> p (u i c)")
        Oe2 = XNf[:, 0:1024].rearrange("p (u n) -> p u n", u=2)
        mro = XNf[0:16, 1024:1152].bitcast(BF16).rearrange("p (u n) -> p u n", u=2)
        crow = XNf[0:1, 0:2048].bitcast(BF16)
        Pn = W[:, 0:1024]
        PnT = W[:, 1024:2048].rearrange("p (k n) -> p k n", k=TB)
        Qbd = W[:, 2048:2560].rearrange("p (b j n) -> p b j n", b=B, j=2)
        omk = W[:, 2560:2816].rearrange("p (j n) -> p j n", j=2)
        rn2 = W[:, 2816:3328]
        dt2 = W[:, 3328:3840]
        sm2 = sb("sm2", [P, 1024])
        qgc = sm2[:, 0:2]
        qg2 = sm2[:, 2:4]
        qgn = sm2[:, 4:6]
        qgb = sm2[:, 8:24].rearrange("p (j g) -> p j g", j=2)
        BBm = sm2[:, 24:152]
        Rfull = sm2[:, 152:192].rearrange("p (g r) -> p g r", g=8)
        Rsel = sm2[:, 192:197]
        rmask = sm2[:, 200:208]
        regm = sm2[:, 208:240]
        QR = sm2[:, 240:280].rearrange("p (j b r) -> p j b r", j=2, b=B)
        simc = sm2[:, 280:312]
        cls = sm2[:, 312:440].rearrange("p (k i) -> p k i", k=4)
        tmp32 = sm2[:, 440:472]
        mm2 = sm2[:, 472:474]
        mmr = sm2[0:2, 474:475]
        mmd = sm2[0:2, 476:478]
        ones2 = sm2[0:2, 480:608]
        mmb = sm2[:, 608:610]
        rng = sm2[:, 610:611]
        rrg = sm2[:, 611:612]
        clsT = sm2[:, 612:676].bitcast(BF16)
        onesb = sm2[0:1, 676:708].bitcast(BF16)
        rmx = sm2[:, 708:712]
        rnm = sm2[:, 712:716]
        rden = sm2[:, 716:720]
        rrd = sm2[:, 720:724]
        MX = sm2[:, 728:760].rearrange("p (u q j) -> p u q j", u=2, q=4)
        MXn = sm2[:, 760:792].rearrange("p (u q j) -> p u q j", u=2, q=4)
        rc2 = sm2[:, 792:808].rearrange("p (q j) -> p q j", q=4)
        simr = sm2[:, 808:840]
        s_wq3 = sem("wqkv_loaded")
        s_qgl = sem("q_g_loaded")
        s_qc = sem("q_g_chain")
        s_qk = sem("q_g_product")
        s_c2 = sem("class_constants")
        s_gb2 = sem("gated_bias2")
        s_xb2 = sem("bias2_added")
        s_qp = sem("qkv_product")
        s_qh = sem("q_part_h")
        s_qf = sem("q_copied")
        s_qs = sem("q_squared")
        s_qm = sem("q_part_m")
        s_kh = sem("k_part_h")
        s_km = sem("k_part_m")
        s_qr = sem("q_residue")
        s_krs = sem("k_residue")
        s_kf = sem("k_copied")
        s_vf = sem("v_copied")
        s_ql = sem("q_part_l")
        s_kl = sem("k_part_l")
        s_qw = sem("q_parts_written")
        s_kw2 = sem("k_parts_written")
        s_qrr = sem("register_queries_kept")
        s_sim = sem("sim_products")
        s_sc2 = sem("sim_chain")
        s_rp = sem("norms_made")
        s_mmt = sem("extremes_transposed")
        s_mmb = sem("extremes_broadcast")
        s_clt = sem("classes_transposed")
        s_clw = sem("class_rows_written")
        s_clw2 = sem("register_key_row_written")
        s_crl = sem("register_key_row_loaded")
        s_rq = sem("register_scores")
        s_rm = sem("register_chain")
        s_rex = sem("register_probs")
        s_rpt = sem("register_probs_transposed")
        s_rpc = sem("register_probs_copied")
        s_rv = sem("register_values")
        s_rk = sem("register_masked")
        s_rsm = sem("register_summed")
        s_rgn = sem("register_kept")
        s_stk = [sem(f"stacks_loaded{n}") for n in range(3)]
        s_one = sem("max_row_factor_set")
        s_mrw = [sem(f"max_rows_in_dram{n}") for n in range(2)]
        s_row = [sem(f"max_rows_loaded{n}") for n in range(2)]
        s_turn = sem("turn_filled")
        s_tfree = sem("turn_free")
        s_neg = sem("maxima_negated")
        s_sco = sem("scores2")
        s_sfree = sem("score_bank_free")
        s_pv2 = sem("values2_product")
        s_oe2 = sem("out2_copied")
        s_vst = sem("values_staged")
        s_vpre = sem("value_stage_preset")
        s_rc2 = sem("out2_recip")
        s_avg = sem("registers_averaged")
        s_out = sem("output_written")

        OnT2 = W[:, 0:2048].rearrange("p (u j n) -> p u j n", u=2, j=2)
        SIM_READ, CLS_DONE = 2, 23
        STACK2_DMAS = 14
        SHIFT = 2
        ORDER = [(n + SHIFT) % 16 for n in range(16)]
        PLAN = [[("tile", n)] for n in range(32)] + [[("out", 1)]]
        PLAN[1].append(("rows", 1))
        PLAN[19].append(("rows", 0))
        PLAN[18].append(("out", 0))
        PLAN_LAST = [[] for _ in range(32)] + [[("out", 1)]]
        PLAN_LAST[1].append(("rows", 1))
        PLAN_LAST[18].append(("out", 0))
        TURNS0 = 33
        TURNS = sum(len(x) for x in PLAN)
        flat, flat_last = sum(PLAN, []), sum(PLAN_LAST, [])
        ROWS1, ROWS0, ROWS1_LAST = flat.index(("rows", 1)), flat.index(("rows", 0)), flat_last.index(("rows", 1))

        def ln_chunk_buf(c):
            return XN[:, c % 2]

        @block.sync
        def _(sp):
            for b in range(B):
                sp.dma_start(X[:, TB * b:TB * b + TB, :],
                             ins["x"][b].rearrange("(i p) c -> p i c", p=P)).then_inc(s_x[b], 16)
            for dst, src in ((ctxT, ins["ctxT"]), (wk0, ins["wk0T"]), (wq0, ins["wq0"]), (wv0, ins["wv0T"])):
                sp.dma_start(dst, src.rearrange("(j p) n -> p j n", p=P)).then_inc(s_w0, 16)
            for b in range(B):
                sp.dma_start(M0[:, b, :], ins["mask0T"][b]).then_inc(s_m0, 16)
            for i, n in enumerate(("g_xattn", "g_ffn")):
                sp.dma_start(graw[:, 2 * i:2 * i + 2],
                             ins[n].rearrange("(a n) -> a n", a=1).to_broadcast([P, 2])).then_inc(s_g, 16)
            sp.dma_start(wg, ins["w_gate"].rearrange("(j p) n -> p j n", p=P)).then_inc(s_wf, 16)
            sp.dma_start(ballT, ins["ballT"].rearrange("(j p) n -> p j n", p=P)).then_inc(s_wf, 16)
            sp.dma_start(wtT, ins["wtT"].rearrange("(j p) n -> p j n", p=P)).then_inc(s_wf, 16)
            sp.dma_start(wdT, ins["wdT"].rearrange("(j p) n -> p j n", p=P)).then_inc(s_wf, 16)
            sp.dma_start(AT[0:NB16, :], ins["AT"]).then_inc(s_wf, 16)
            sp.wait_ge(s_fc, 2)
            sp.dma_start(A1x[1:L, 0:NB16], ins["A1"][1:L, :]).then_inc(s_wf, 16)
            sp.dma_start(BWt[:, :, 96], ins["wt_b"].rearrange("(j p) -> p j", p=P),
                         allow_slow_non_contiguous=True).then_inc(s_wf, 16)
            sp.dma_start(BW[97:98, :], ins["wd_b"].rearrange("(a n) -> a n", a=1)).then_inc(s_wf, 16)
            sp.dma_start(fscale, ins["scale"].rearrange("(a n) -> a n", a=1).to_broadcast([P, 1])).then_inc(s_wf, 16)
            sp.dma_start(wo1[:, :, :], ins["wo1T"].rearrange("(j p) n -> p j n", p=P)).then_inc(s_w1, 16)
            sp.dma_start(wproj[:, :, :], ins["wproj"].rearrange("(j p) n -> p j n", p=P)).then_inc(s_w1, 16)
            sp.dma_start(bo1[:, :], ins["bo1"].rearrange("(a n) -> a n", a=1).to_broadcast([P, C])).then_inc(s_w1, 16)
            sp.dma_start(bp2[:, :], ins["bproj"].rearrange("(a n) -> a n", a=1).to_broadcast([P, C])).then_inc(s_w1, 16)
            for i, n in enumerate(("wv1T", "wk1T", "wq1")):
                for g in range(8):
                    sp.dma_start(w16[16 * g:16 * g + 16, i, :], ins[n]).then_inc(s_w1, 16)
            sp.wait_ge(s_u, NC)
            sp.wait_ge(s_dl, NC)
            sp.dma_start(M1u, ins["mask1T"]).then_inc(s_m1, 16)
            sp.wait_ge(s_kr, 5)
            sp.dma_start(KXP.rearrange("a (j p) n -> p a j n", p=P), kpart).then_inc(s_kw, 16)
            sp.wait_ge(s_kw, 16)
            for n, p in enumerate(K_ORDER):
                sp.dma_start(K1s[16 * n:16 * n + 16],
                             KXP[p].rearrange("(h d) n -> d h n", d=D)).then_inc(s_k1s, 16)

            def write_parts(n, dst):
                sp.wait_ge(s_pl, n + 1)
                sp.dma_start(dst, PB[:, n % 2]).then_inc(s_pw[n % 2], 16)

            def load_x_stack(u):
                b, hg = u // 4, u % 4
                if u >= 3:
                    sp.wait_ge(s_sc, 8 * (u - 2))
                for n, p in enumerate(Q_ORDER):
                    sp.dma_start(Xs[u % 3][16 * n:16 * n + 16],
                                 XP[p, 64 * hg:64 * hg + 64, S * b:S * b + S]
                                 .rearrange("(j d) t -> d j t", d=D)).then_inc(s_xs[u % 3], 16)

            for c in range(NC):
                write_parts(c, XP[:, :, 512 * c:512 * c + 512].rearrange("a (j p) n -> p a j n", p=P))
                if c == 3:
                    sp.wait_ge(s_pw[0], 16)
                    sp.wait_ge(s_pw[1], 16)
                    load_x_stack(0)
            for u in range(1, UNITS):
                b = u // 4
                if u % 4 == 0:
                    sp.wait_ge(s_pw[0], 16 * (b + 1))
                    sp.wait_ge(s_pw[1], 16 * (b + 1))
                load_x_stack(u)
            sp.wait_ge(s_ksc, 6)
            sp.wait_ge(s_ks, 6)
            sp.dma_start(wqkv, ins["wqkv"].rearrange("(j p) n -> p j n", p=P)).then_inc(s_wq3, 16)
            sp.dma_start(qgc, ins["g_info"][0, 0].rearrange("(j p) -> p j", p=P),
                         allow_slow_non_contiguous=True).then_inc(s_qgl, 16)
            for c in range(NC):
                rows = slice(C * (c // 2), C * (c // 2) + C)
                t = slice(512 * (c % 2), 512 * (c % 2) + 512)
                sp.wait_ge(s_ql, c + 1)
                for a in range(3):
                    sp.dma_start(QP[a, rows, t].rearrange("(j p) n -> p j n", p=P), PB2[:, 0, a]).then_inc(s_qw, 16)
                sp.wait_ge(s_kl, c + 1)
                for a in range(3):
                    sp.dma_start(KP[a, rows, t].rearrange("(j p) n -> p j n", p=P), PB2[:, 1, a]).then_inc(s_kw2, 16)
            sp.wait_ge(s_sc2, CLS_DONE)
            for k in (2, 0, 1, 3):
                for b in range(B):
                    row = TB * (B * k + b)
                    sp.dma_start(CR[k, b].rearrange("g (i n) -> i g n", n=P),
                                 clsT[row:row + TB].unsqueeze(1).to_broadcast([TB, 4, P])
                                 ).then_inc(s_clw if k != 2 else s_clw2, 16)
                if k == 2:
                    sp.wait_ge(s_clw2, 16 * B)
                    sp.dma_start(crow.rearrange("p (b t) -> p b t", b=B),
                                 CR[2, :, 0, :].unsqueeze(0)).then_inc(s_crl, 16)
            sp.wait_ge(s_clw, 16 * 3 * B)
            sp.wait_ge(s_qw, 48 * NC)
            sp.wait_ge(s_kw2, 48 * NC)
            CRu = CR.rearrange("k b g t -> k (b g) t")

            def load_stacks(u, j):
                for dst, parts, order in ((QST[j], QP, Q_ORDER), (KST[j], KP, K_ORDER)):
                    for n, a in enumerate(order):
                        src = parts[a].rearrange("(u j d) t -> u d j t", u=UNITS, d=D)
                        sp.dma_start(dst[16 * n:16 * n + 16], src[u]).then_inc(s_stk[j], 16)
                for dst, k in ((QST[j], 0), (KST[j], 2)):
                    sp.dma_start(dst[NEG_ROW:POS_ROW + 1],
                                 CRu[k:k + 2].rearrange("k u t -> u k t")[u].unsqueeze(1)
                                 .to_broadcast([2, 4, S])).then_inc(s_stk[j], 16)

            def store_row(j, half, filled, stored):
                sp.wait_ge(s_tfree, filled)
                sp.dma_start(MR[half], mro[:, half, :]).then_inc(s_mrw[half], 16)
                sp.wait_ge(s_mrw[half], 16 * stored + 16)
                sp.dma_start(QST[j][MAX_ROW:MAX_ROW + 1, :, 512 * half:512 * half + 512],
                             MR[half].rearrange("(h q) n -> h (q n)", h=4).unsqueeze(0)).then_inc(s_row[half], 16)

            sp.wait_ge(s_sim, NC)
            sp.wait_ge(s_one, 1)
            load_stacks(0, 0)
            sp.wait_ge(s_rq, B)
            sp.wait_ge(s_one, 3)
            load_stacks(1, 1)
            load_stacks(2, 2)
            store_row(0, 0, 2 + 17, 0)

            def body_sp(u, j, last=False, load=True):
                base = 2 + TURNS0 + TURNS * u + 1
                store_row(j, 1, base + (ROWS1_LAST if last else ROWS1), u)
                if not last:
                    store_row((j + 1) % 3, 0, base + ROWS0, u + 1)
                if load:
                    sp.wait_ge(s_pv2, 2 + 16 * (u + 1))
                    load_stacks(u + 3, j)

            with sp.Fori(0, 4) as i:
                for j in range(3):
                    body_sp(3 * i + j, j)
            body_sp(12, 0)
            body_sp(13, 1, load=False)
            body_sp(14, 2, load=False)
            body_sp(15, 0, last=True, load=False)
            for c in range(NC):
                sp.wait_ge(s_x3, NC + c + 1)
                sp.dma_start(out[c // 2].rearrange("(i p) c -> p i c", p=P)[:, 4 * (c % 2):4 * (c % 2) + 4, :],
                             X[:, 4 * c:4 * c + 4, :]).then_inc(s_out, 16)
            sp.wait_ge(s_out, 16 * NC)

        @block.gpsimd
        def _(pool):
            pool.memset(identF[:, :], 0.0).then_inc(s_const, 1)
            pool.memset(blk[:, :], 1.0).then_inc(s_const, 1)
            pool.memset(mhalf[:, :], -0.5).then_inc(s_const, 1)
            pool.memset(masked, 1e-9 * 16.0).then_inc(s_const, 1)
            pool.wait_ge(s_const, 4)
            pool.affine_select(out=identF[:, :], in_=identF[:, :], compare_op=ALU.not_equal, fill=1.0,
                               base=0, pattern=[[-1, P]], channel_multiplier=1).then_inc(s_const, 1)
            pool.wait_ge(s_const, 5)
            pool.tensor_copy(identB[:, :], identF[:, :]).then_inc(s_const, 1)
            pool.affine_select(out=blk[:, :], in_=blk[:, :], compare_op=ALU.is_ge, fill=0.0,
                               base=0, pattern=[[-16, 8]], channel_multiplier=1).then_inc(s_const, 1)
            pool.wait_ge(s_const, 7)
            pool.affine_select(out=blk[:, :], in_=blk[:, :], compare_op=ALU.is_ge, fill=0.0,
                               base=15, pattern=[[16, 8]], channel_multiplier=-1).then_inc(s_const, 1)

            def ln_rstd(k):
                for b in range(B):
                    v = slice(TB * b, TB * b + TB)
                    pool.wait_ge(s_ag, B * k + b + 1)
                    pool.tensor_scalar(rstd[:, v], mv[:, v, 1], LN_EPS, None, ALU.add).then_inc(s_rs, 1)
                    pool.wait_ge(s_rs, 2 * (B * k + b) + 1)
                    pool.tensor_tensor(rstd[:, v], rstd[:, v], mhalf[:, v], ALU.pow).then_inc(s_rs, 1)

            ln_rstd(0)
            pool.memset(A1x[0:L, :], 1.0).then_inc(s_fc, 1)
            pool.wait_ge(s_fc, 1)
            pool.memset(A1x[0:1, 0:97], 0.0).then_inc(s_fc, 1)
            for e in range(E):
                pool.memset(wtie[:, e:e + 1], float(E - e)).then_inc(s_fc, 1)

            ln_rstd(1)
            ln_rstd(2)
            pool.wait_ge(s_w1, 16 * 28)
            pool.wait_ge(s_gt, 1)
            pool.tensor_scalar(bo1[:, :], bo1[:, :], gates[:, 1:2], None, ALU.mult).then_inc(s_gb, 1)
            pool.wait_ge(s_gb, 1)

            def last_parts(k, n0):
                for c in range(NC):
                    n = n0 + c
                    pool.wait_ge(s_pm, n + 1)
                    pool.tensor_tensor(PB[:, n % 2, 2], xres[:, n % 2], PB[:, n % 2, 1],
                                       ALU.subtract).then_inc(s_pl, 1)
            last_parts(2, 0)
            for b in range(B):
                pool.wait_ge(s_xn, NC * 2 + 2 * b + 2)
                xs = X[:, TB * b:TB * b + TB, :]
                pool.tensor_tensor(xs, xs, bo1[:, :].unsqueeze(1).to_broadcast([P, TB, C]), ALU.add).then_inc(s_xb, 1)

            pool.memset(Rfull, 0.0).then_inc(s_c2, 1)
            pool.memset(regm, 0.0).then_inc(s_c2, 1)
            pool.memset(ones2, 1.0).then_inc(s_c2, 1)
            pool.memset(onesb, 1.0).then_inc(s_c2, 1)
            pool.wait_ge(s_c2, 4)
            for q in range(2):
                v = Rfull[64 * q:64 * q + 64]
                pool.affine_select(out=v, in_=v, compare_op=ALU.not_equal, fill=1.0, base=0,
                                   pattern=[[-REG, 8], [-1, REG]], channel_multiplier=1).then_inc(s_c2, 1)
                pool.wait_ge(s_c2, 5 + q)
            for b in range(B):
                pool.memset(regm[0:REG, TB * b:TB * b + 1], 1.0).then_inc(s_c2, 1)
            ln_rstd(3)
            pool.wait_ge(s_qk, 1)
            pool.wait_ge(s_qc, 3)
            pool.tensor_tensor(qgn, qgn, mhalf[:, 0:2], ALU.pow).then_inc(s_qc, 1)
            pool.tensor_scalar(bp2[:, :], bp2[:, :], gates[:, 3:4], None, ALU.mult).then_inc(s_gb2, 1)
            for c in range(NC):
                pool.wait_ge(s_qm, c + 1)
                pool.tensor_tensor(PB2[:, 0, 2], res2[:, 0], PB2[:, 0, 1], ALU.subtract).then_inc(s_ql, 1)
                pool.wait_ge(s_km, c + 1)
                pool.tensor_tensor(PB2[:, 1, 2], res2[:, 1], PB2[:, 1, 1], ALU.subtract).then_inc(s_kl, 1)
            pool.wait_ge(s_kl, NC)
            pool.wait_ge(s_sim, NC)
            pool.memset(KST[0][NEG_ROW:MAX_ROW + 1], 1.0).then_inc(s_one, 1)
            pool.wait_ge(s_rq, B)
            for j in (1, 2):
                pool.wait_ge(s_one, j)
                pool.memset(KST[j][NEG_ROW:MAX_ROW + 1], 1.0).then_inc(s_one, 1)
            pool.wait_ge(s_one, 3)
            pool.wait_ge(s_kw2, 48 * NC)
            pool.wait_ge(s_qw, 48 * NC)
            for j in range(3):
                pool.memset(VST[j], 0.0).then_inc(s_vpre, 1)
            pool.wait_ge(s_vpre, 3)
            for j in range(3):
                pool.memset(VST[j][:, :, :, D:D + 1], 1.0).then_inc(s_vpre, 1)
            pool.wait_ge(s_vf, NC)

            def stage_values(u, j):
                pool.tensor_copy(VST[j][:, :, :, 0:D].unsqueeze(1),
                                 V2[:, bass.ds(u, 1)].rearrange("p u k (j d) -> p u k j d", j=4)).then_inc(s_vst, 1)

            for j in range(3):
                stage_values(j, j)
            pool.wait_ge(s_gb2, 1)
            pool.wait_ge(s_xn, 4 * NC)
            for b in range(B):
                xs = X[:, TB * b:TB * b + TB, :]
                pool.tensor_tensor(xs, xs, bp2[:, :].unsqueeze(1).to_broadcast([P, TB, C]), ALU.add).then_inc(s_xb2, 1)
            with pool.Fori(0, 4) as i:
                for j in range(3):
                    pool.wait_ge(s_pv2, 2 + 16 * (3 * i + j + 1))
                    stage_values(3 * i + j + 3, j)
            pool.wait_ge(s_pv2, 2 + 16 * 13)
            stage_values(15, 0)

        @block.scalar
        def _(act):
            act.wait_ge(s_g, 32)
            act.activation(gates[:, :], graw, ACT.Tanh).then_inc(s_gt, 1)
            for n, (dst, i, rows, cols) in enumerate(
                    [(kT0[:, j, :], 4 + j, P, 308) for j in range(2)]
                    + [(KW0[:, j, :], 6 + j, P, 308) for j in range(2)]):
                act.wait_ge(s_ks, n + 1)
                act.copy(dst, bank(i)[0:rows, 0:cols]).then_inc(s_ksc, 1)
            for n in range(2):
                act.wait_ge(s_ks, 5 + n)
                act.copy(V0[:, 2 * n:2 * n + 2, :], bank(4 + n)[0:KX, :].rearrange("p (b n) -> p b n", b=2)).then_inc(s_ksc, 1)

            def ln_copy(k, then=lambda c: None):
                for c in range(NC):
                    act.wait_ge(s_tr, NC * k + c + 1)
                    act.copy(XNT[:, :, 512 * c:512 * c + 512],
                             bank(2 * (c % 2), 2).rearrange("p (j t) -> p j t", j=2)).then_inc(s_xt, 1)
                    then(c)

            ln_copy(0)
            for b in range(B):
                act.wait_ge(s_nb0, b + 1)
                act.activation(P0[:, b, :], bank(4 + 2 * (b % 2), 2)[0:KX, :], ACT.Exp, bias=nb0[:, b:b + 1],
                               scale=1.0 / 16, accum_out=den0[:, b:b + 1]).then_inc(s_e0, 1)

            for j in range(2):
                act.wait_ge(s_fs, j + 1)
                act.copy(BWt[:, j, 0:NB16], bank(4 + j)[:, 0:NB16]).then_inc(s_fsc, 1)
            act.wait_ge(s_fs, 3)
            act.copy(BW[0:97, :], bank(6)[0:97, 0:C]).then_inc(s_fsc, 1)
            def y_copy(c):
                act.wait_ge(s_y, c + 1)
                act.copy(yg[:, 512 * c:512 * c + 512], bank(5 + c % 2)[0:NB16 + E, :]).then_inc(s_yc, 1)

            ln_copy(1, lambda c: y_copy(c - 1) if c >= 1 else None)
            y_copy(NC - 1)
            for c in range(NC):
                act.wait_ge(s_ot, c + 1)
                act.copy(OHT[:, 512 * c:512 * c + 512], bank(4 + c % 2)[0:98, :]).then_inc(s_otc, 1)
            for c in range(NC):
                v = attn[:, 4 * c:4 * c + 4, :]
                act.wait_ge(s_ad, c + 1)
                act.activation(v, v, ACT.Exp, scale=C ** -0.5).then_inc(s_ae, 1)
            for c in range(NC):
                act.wait_ge(s_at, c + 1)
                act.copy(aT[:, 512 * c:512 * c + 512], bank(6 + c % 2)[0:L, :]).then_inc(s_atc, 1)
            act.wait_ge(s_atc, NC)

            def log(c):
                v = comb[:, 4 * c:4 * c + 4, :]
                act.wait_ge(s_z2, c + 1)
                act.activation(v, v, ACT.Ln).then_inc(s_ln, 1)

            for c in range(NC):
                act.wait_ge(s_dl, c + 1)
                act.activation(comb[:, 4 * c:4 * c + 4, :],
                               bank(2 * (c % 2), 2).rearrange("p (i n) -> p i n", i=4), ACT.Exp,
                               scale=fscale).then_inc(s_de, 1)
                if c >= 1:
                    log(c - 1)
            log(NC - 1)

            act.wait_ge(s_k1, 1)
            act.copy(k1T, bank(4, 2).rearrange("p (j n) -> p j n", j=2)[:, :, 0:308]).then_inc(s_k1c, 1)
            act.wait_ge(s_k1, 2)
            act.copy(kpart[:, 0], bank(6, 2).rearrange("p (j n) -> p j n", j=2)[:, :, 0:308]).then_inc(s_k1c, 1)
            act.wait_ge(s_kr, 1)
            act.wait_ge(s_v1, 1)
            act.wait_ge(s_v1m, 2)
            for j in range(2):
                act.copy(V1a[:, :, 8 * j:8 * j + 8, 0:D],
                         bank(4 + j)[0:KX, :].rearrange("p (b h d) -> p b h d", b=B, h=8)).then_inc(s_v1c, 1)

            for n in range(NC + 1):
                if n < NC:
                    act.wait_ge(s_tr, NC * 2 + n + 1)
                    if n >= 2:
                        act.wait_ge(s_pw[n % 2], 16 * (n // 2))
                    act.copy(PB[:, n % 2, 0],
                             bank(2 * (n % 2), 2).rearrange("p (j t) -> p j t", j=2)).then_inc(s_ph, 1)
                if n >= 1:
                    act.wait_ge(s_pr, n)
                    act.copy(PB[:, (n - 1) % 2, 1], xres[:, (n - 1) % 2]).then_inc(s_pm, 1)

            def max_rows1(m):
                act.wait_ge(s_mt, m + 1)
                if m >= 2:
                    act.wait_ge(s_sc, 4 * m - 4)
                act.copy(mrow[:, 512 * (m % 2):512 * (m % 2) + 512], bank(2)[0:4, :]).then_inc(s_mrc, 1)

            def copy_out1(m):
                act.wait_ge(s_pv, m + 1)
                if m >= 2:
                    act.wait_ge(s_ot1, m - 1)
                act.copy(Oe[:, m % 2], bank(7)).then_inc(s_oc, 1)

            max_rows1(0)
            max_rows1(1)
            for m in range(2 * UNITS):
                if m >= 2:
                    act.wait_ge(s_pv, m - 1)
                for j in range(4):
                    n = 4 * m + j
                    act.wait_ge(s_sc, n + 1)
                    act.activation(P1[:, m % 2, j, :], bank(4 + n % 3)[0:KX, :], ACT.Exp,
                                   scale=0.25).then_inc(s_e1, 1)
                if m >= 1:
                    copy_out1(m - 1)
                if m + 2 < 2 * UNITS:
                    max_rows1(m + 2)
            copy_out1(2 * UNITS - 1)

            def heads_copy(k):
                for c in range(NC):
                    n = NC * k + c
                    act.wait_ge(s_onT, n + 1)
                    if n >= 2:
                        act.wait_ge(s_wo, n - 1)
                    act.copy(OnT[:, c % 2], bank(2 * (c % 2), 2).rearrange("p (j t) -> p j t", j=2)).then_inc(s_onc, 1)

            heads_copy(0)

            act.wait_ge(s_onT, NC)
            for c in range(NC):
                act.wait_ge(s_tr, NC * 3 + c + 1)
                act.copy(XNT[:, :, 512 * c:512 * c + 512],
                         bank(2 * (c % 2), 2).rearrange("p (j t) -> p j t", j=2)).then_inc(s_xt, 1)
            for c in range(NC):
                q = bank(2, 2).rearrange("p (j t) -> p j t", j=2)
                act.wait_ge(s_qp, 3 * c + 1)
                if c >= 2:
                    act.wait_ge(s_sim, c - 1)
                    act.wait_ge(s_qrr, c // 2)
                act.copy(Qf[:, c % 2], q).then_inc(s_qf, 1)
                act.wait_ge(s_qf, c + 1)
                if c >= 1:
                    act.wait_ge(s_qw, 48 * c)
                act.copy(PB2[:, 0, 0], Qf[:, c % 2]).then_inc(s_qh, 1)
                act.activation(Qsq[:, c % 2], Qf[:, c % 2], ACT.Square).then_inc(s_qs, 1)
                act.wait_ge(s_qr, c + 1)
                act.copy(PB2[:, 0, 1], res2[:, 0]).then_inc(s_qm, 1)
                act.wait_ge(s_kf, c + 1)
                if c >= 1:
                    act.wait_ge(s_kw2, 48 * c)
                act.copy(PB2[:, 1, 0], KT[:, :, 512 * c:512 * c + 512]).then_inc(s_kh, 1)
                act.wait_ge(s_krs, c + 1)
                act.copy(PB2[:, 1, 1], res2[:, 1]).then_inc(s_km, 1)
            act.wait_ge(s_sim, NC)
            act.activation(rn2, bank(0), ACT.Sqrt).then_inc(s_rp, 1)
            for b in range(B):
                act.wait_ge(s_rm, 2 * b + 2)
                if b >= 1:
                    act.wait_ge(s_rpt, b)
                act.activation(Pn, bank(2 + 2 * (b % 2), 2), ACT.Exp, bias=rnm[:, b:b + 1], scale=0.25,
                               accum_out=rden[:, b:b + 1]).then_inc(s_rex, 1)
                act.wait_ge(s_rpt, b + 1)
                if b >= 1:
                    act.wait_ge(s_rv, b)
                act.copy(PnT, bank(6, 2).rearrange("p (k n) -> p k n", k=TB)).then_inc(s_rpc, 1)
            act.wait_ge(s_rv, B)

            def exps(u, s, j):
                act.wait_ge(s_pv2, 16 * u + s + 1)
                for h in range(4):
                    n = 4 * s + h
                    act.wait_ge(s_sco, 64 * u + n + 1)
                    act.activation(PR[:, s % 2, h, :], bank(4 + (64 * j + n) % 3), ACT.Exp,
                                   scale=0.25).then_inc(s_sfree, 1)

            def copy_out2(u, half):
                act.wait_ge(s_pv2, 16 * u + 8 * half + 10)
                act.copy(Oe2[:, half, :], bank(7)).then_inc(s_oe2, 1)

            def body_act(u, j, last=False):
                for s in ORDER:
                    if s >= SHIFT:
                        exps(u, s, j)
                    elif not last:
                        exps(u + 1, s, (j + 1) % 3)
                    if s == 8:
                        copy_out2(u, 0)
                    if s == 0:
                        copy_out2(u, 1)

            act.sem_inc(s_sfree, 3)
            act.sem_inc(s_oe2, 1)
            for s in range(SHIFT):
                exps(0, s, 0)
            with act.Fori(0, 5) as i:
                for j in range(3):
                    body_act(3 * i + j, j)
            body_act(15, 0, last=True)
            for c in range(NC):
                n = NC + c
                act.wait_ge(s_onT, n + 1)
                if c >= 2:
                    act.wait_ge(s_wo, n - 1)
                act.copy(OnT2[:, c % 2], bank(2 * (c % 2), 2).rearrange("p (j t) -> p j t", j=2)).then_inc(s_onc, 1)

        @block.tensor
        def _(pe):
            def keep_warm(i, n):
                for _ in range(n):
                    pe.matmul(bank(i), identB[:, :], identB[:, :].unsqueeze(1).to_broadcast([P, 4, P]),
                              start=True, stop=True)

            pe.wait_ge(s_w0, 64)
            for j in range(2):
                for i in range(2):
                    mm = pe.matmul(bank(4 + j)[:, 0:308], wk0[:, i, P * j:P * j + P], ctxT[:, i, :],
                                   start=(i == 0), stop=(i == 1))
                mm.then_inc(s_ks, 1)
            pe.wait_ge(s_ksc, 2)
            for j in range(2):
                for i in range(2):
                    mm = pe.matmul(bank(6 + j)[:, 0:308], wq0[:, i, P * j:P * j + P], kT0[:, i, :],
                                   start=(i == 0), stop=(i == 1))
                mm.then_inc(s_ks, 1)
            for n in range(2):
                for b in (2 * n, 2 * n + 1):
                    for i in range(2):
                        mm = pe.matmul(bank(4 + n)[0:KX, C * (b % 2):C * (b % 2) + C],
                                       ctxT[:, i, KX * b:KX * b + KX], wv0[:, i, :],
                                       start=(i == 0 and b % 2 == 0), stop=(i == 1), skip_group_check=True)
                mm.then_inc(s_ks, 1)

            def ln_transposes(k, then=lambda c: None):
                pe.wait_ge(s_const, 8)
                for c in range(NC):
                    pe.wait_ge(s_xn, NC * k + c + 1)
                    if NC * k + c >= 2:
                        pe.wait_ge(s_xt, NC * k + c - 1)
                    for j in range(2):
                        for i in range(4):
                            mm = pe.transpose(bank(2 * (c % 2) + j)[:, P * i:P * i + P],
                                              ln_chunk_buf(c)[:, i, P * j:P * j + P], identF[:, :])
                    mm.then_inc(s_tr, 1)
                    then(c)

            ln_transposes(0)

            def scores0(b):
                if b < 2:
                    pe.wait_ge(s_ksc, 6)
                else:
                    pe.wait_ge(s_e0, b - 1)
                for q in range(2):
                    for i in range(2):
                        mm = pe.matmul(bank(4 + 2 * (b % 2) + q)[0:KX, :], KW0[:, i, KX * b:KX * b + KX],
                                       XNT[:, i, S * b + 512 * q:S * b + 512 * q + 512],
                                       start=(i == 0), stop=(i == 1))
                mm.then_inc(s_s0, 1)

            pe.wait_ge(s_xt, NC)
            scores0(0)
            for b in range(B):
                if b + 1 < B:
                    scores0(b + 1)
                pe.wait_ge(s_v0, b + 1)
                for g in range(4):
                    n = 4 * b + g
                    if n >= 4:
                        pe.wait_ge(s_x1, n - 3)
                    for i in range(2):
                        q = P * (2 * g + i)
                        mm = pe.matmul(bank(g)[:, C * i:C * i + C], P0[:, b, q:q + P], V0s[:, b, :],
                                       start=(i == 0), stop=True, skip_group_check=True)
                    mm.then_inc(s_o0, 1)

            pe.wait_ge(s_wf, 16 * 9)
            pe.wait_ge(s_e0, B)
            for j in range(2):
                for i in range(2):
                    mm = pe.matmul(bank(4 + j)[:, 0:NB16], wtT[:, i, P * j:P * j + P], ballT[:, i, :],
                                   start=(i == 0), stop=(i == 1))
                mm.then_inc(s_fs, 1)
            pe.wait_ge(s_fsc, 2)
            for j in range(2):
                mm = pe.matmul(bank(6)[0:97, 0:C], BWt[:, j, :], wdT[:, j, :], start=(j == 0), stop=(j == 1))
            mm.then_inc(s_fs, 1)
            pe.wait_ge(s_x1, 4 * B)
            pe.wait_ge(s_fsc, 3)

            def y_and_gates(c):
                pe.wait_ge(s_xt, NC + c + 1)
                if c >= 2:
                    pe.wait_ge(s_yc, c - 1)
                for j in range(2):
                    mm = pe.matmul(bank(5 + c % 2)[0:NB16 + E, :], ballg[:, j, :], XNT[:, j, 512 * c:512 * c + 512],
                                   start=(j == 0), stop=(j == 1))
                mm.then_inc(s_y, 1)

            def gates_back(c):
                pe.wait_ge(s_yc, c + 1)
                for i in range(4 * c, 4 * c + 4):
                    mm = pe.matmul(bank(7)[:, E * i:E * i + E], yg[:, P * i:P * i + P],
                                   identF[0:NB16 + E, NB16:NB16 + E], start=(i == 0), stop=True,
                                   skip_group_check=True)
                mm.then_inc(s_gl, 1)

            def with_y(c):
                if c >= 1:
                    y_and_gates(c - 1)
                if c >= 2:
                    gates_back(c - 2)

            ln_transposes(1, with_y)
            y_and_gates(NC - 1)
            gates_back(NC - 2)
            gates_back(NC - 1)
            pe.wait_ge(s_gc, 7)
            for c in range(NC):
                if c >= 2:
                    pe.wait_ge(s_otc, c - 1)
                for i in range(4):
                    mm = pe.matmul(bank(4 + c % 2)[0:98, P * i:P * i + P], OH96[:, 4 * c + i, :], identB[:, :],
                                   start=True, stop=True)
                mm.then_inc(s_ot, 1)
            pe.wait_ge(s_otc, NC)
            for c in range(NC):
                pe.wait_ge(s_ys, c + 1)
                if c >= 2:
                    pe.wait_ge(s_ad, c - 1)
                for i in range(4):
                    t = 512 * c + P * i
                    mm = pe.matmul(bank(4 + c % 2)[:, L * i:L * i + L], ysel[:, t:t + P], AT[0:NB16, :],
                                   start=(i == 0), stop=True, skip_group_check=True)
                mm.then_inc(s_lg, 1)
            for c in range(NC):
                pe.wait_ge(s_an, c + 1)
                if c >= 2:
                    pe.wait_ge(s_atc, c - 1)
                for i in range(4):
                    mm = pe.transpose(bank(6 + c % 2)[0:L, P * i:P * i + P], attn[:, 4 * c + i, :], identF[:, :])
                mm.then_inc(s_at, 1)
            for c in range(NC):
                pe.wait_ge(s_atc, c + 1)
                if c >= 2:
                    pe.wait_ge(s_us, c - 1)
                else:
                    pe.wait_ge(s_ad, NC)
                pe.matmul(bank(4 + c % 2)[0:98, :], A1x[0:L, :], aT[:, 512 * c:512 * c + 512],
                          start=True, stop=True).then_inc(s_u, 1)
            for c in range(NC):
                pe.wait_ge(s_us, c + 1)
                if c >= 2:
                    pe.wait_ge(s_de, c - 1)
                for i in range(4):
                    t = 512 * c + P * i
                    o = bank(2 * (c % 2) + i // 2)[:, C * (i % 2):C * (i % 2) + C]
                    pe.matmul(o, usel[:, t:t + P], BW[0:98, :], start=(i % 2 == 0), stop=False,
                              skip_group_check=True)
                    for j in range(2):
                        mm = pe.matmul(o, XNT[:, j, t:t + P], wdT[:, j, :], start=False, stop=(j == 1),
                                       skip_group_check=True)
                mm.then_inc(s_dl, 1)

            pe.wait_ge(s_bd, 3)
            pe.wait_ge(s_us, NC)
            for j in range(2):
                mm = pe.matmul(bank(4 + j)[:, 0:308], bd[:, 1, :], ctxT[:, j, :], start=True, stop=True)
            mm.then_inc(s_k1, 1)
            pe.wait_ge(s_k1c, 1)
            for j in range(2):
                mm = pe.matmul(bank(6 + j)[:, 0:308], bd[:, 2, :], k1T[:, j, :], start=True, stop=True)
            mm.then_inc(s_k1, 1)
            for j in range(2):
                for b in range(B):
                    mm = pe.matmul(bank(4 + j)[0:KX, P * b:P * b + P], ctxT[:, j, KX * b:KX * b + KX], bd[:, 0, :],
                                   start=(b == 0), stop=True, skip_group_check=True)
            mm.then_inc(s_v1, 1)
            pe.wait_ge(s_de, NC)
            for c in range(NC):
                pe.wait_ge(s_xn, NC * 2 + c + 1)
                if c >= 2:
                    pe.wait_ge(s_pr, c - 1)
                for j in range(2):
                    for i in range(4):
                        mm = pe.transpose(bank(2 * (c % 2) + j)[:, P * i:P * i + P],
                                          ln_chunk_buf(c)[:, i, P * j:P * j + P], identF[:, :])
                mm.then_inc(s_tr, 1)
            pe.wait_ge(s_pr, NC)
            pe.wait_ge(s_k1s, 16 * STACK_DMAS)
            pe.wait_ge(s_mk1, 3)
            pe.wait_ge(s_v1c, 2)

            def max_product1(u, qs):
                b, hg = u // 4, u % 4
                pe.wait_ge(s_xs[u % 3], 16 * STACK_DMAS * (u // 3 + 1))
                for q in qs:
                    n = 8 * u + q
                    if n >= 2:
                        pe.wait_ge(s_mr, n - 1)
                    o = bank(n % 2)[:, 0:4 * KX]
                    pe.matmul(o, mb1[:, P * q:P * q + P], I4, start=True, stop=False, skip_group_check=True)
                    for j in range(4):
                        mm = pe.matmul(o[:, KX * j:KX * j + KX], Xs[u % 3][:, j, P * q:P * q + P],
                                       K1s[:, 4 * hg + j, KX * b:KX * b + KX], start=False, stop=True,
                                       skip_group_check=True)
                    mm.then_inc(s_mp, 1)

            def max_transposes1(m):
                pe.wait_ge(s_mn, m + 1)
                if m >= 1:
                    pe.wait_ge(s_mrc, m)
                for i in range(4):
                    mm = pe.transpose(bank(2)[0:4, P * i:P * i + P], Mn[:, m // 2 % 2, 4 * (m % 2) + i, :], identF[:, :])
                mm.then_inc(s_mt, 1)

            def scores1(m):
                u, q = m // 2, m % 2
                b, hg = u // 4, u % 4
                pe.wait_ge(s_mrc, m + 1)
                for j in range(4):
                    n = 4 * m + j
                    if u + 1 < UNITS:
                        max_product1(u + 1, (4 * q + j,))
                    if n >= 3:
                        pe.wait_ge(s_e1, n - 2)
                    o = bank(4 + n % 3)[0:KX, :]
                    t = slice(512 * q, 512 * q + 512)
                    pe.matmul(o, K1s[:, 4 * hg + j, KX * b:KX * b + KX], Xs[u % 3][:, j, t], start=True, stop=False)
                    pe.matmul(o, I4[:, 0:KX], mb1[:, t], start=False, stop=False)
                    pe.matmul(o, HS[:, j, :], mrow[:, t], start=False, stop=True).then_inc(s_sc, 1)

            def values1(m):
                u = m // 2
                pe.wait_ge(s_e1, 4 * m + 4)
                if m >= 1:
                    pe.wait_ge(s_oc, m)
                for j in range(4):
                    mm = pe.matmul(bank(7)[32 * j:32 * j + 32, :], V1a[:, u // 4, 4 * (u % 4) + j, :],
                                   P1[:, m % 2, j, :], start=True, stop=True)
                mm.then_inc(s_pv, 1)

            def out_transposes1(m):
                pe.wait_ge(s_oc, m + 1)
                if m >= 1:
                    pe.wait_ge(s_on, m)
                for i in range(4):
                    mm = pe.transpose(bank(3)[:, P * i:P * i + P], Oe[:, m % 2, P * i:P * i + P], identF[:, :])
                mm.then_inc(s_ot1, 1)

            pe.wait_ge(s_xs[0], 16 * STACK_DMAS)
            keep_warm(4, 16)
            for q in range(2):
                max_product1(0, range(4 * q, 4 * q + 4))
                max_transposes1(q)
            for m in range(2 * UNITS):
                scores1(m)
                if m >= 1:
                    values1(m - 1)
                if m >= 2:
                    out_transposes1(m - 2)
                if m + 2 < 2 * UNITS:
                    max_transposes1(m + 2)
            values1(2 * UNITS - 1)
            out_transposes1(2 * UNITS - 2)
            out_transposes1(2 * UNITS - 1)

            def project(k, weights, ready):
                def transposes(c):
                    n = NC * k + c
                    ready(c)
                    if n >= 2:
                        pe.wait_ge(s_onc, n - 1)
                    for j in range(2):
                        for i in range(4):
                            mm = pe.transpose(bank(2 * (c % 2) + j)[:, P * i:P * i + P],
                                              On[:, 4 * c + i, P * j:P * j + P], identF[:, :])
                    mm.then_inc(s_onT, 1)

                transposes(0)
                for c in range(NC):
                    n = NC * k + c
                    if c + 1 < NC:
                        transposes(c + 1)
                    pe.wait_ge(s_onc, n + 1)
                    if n >= 2:
                        pe.wait_ge(s_x3, n - 1)
                    for i in range(4):
                        o = bank(4 + 2 * (c % 2) + i // 2)[:, C * (i % 2):C * (i % 2) + C]
                        for j in range(2):
                            mm = pe.matmul(o, OnT[:, c % 2, j, P * i:P * i + P], weights[:, j, :],
                                           start=(i % 2 == 0 and j == 0), stop=(j == 1), skip_group_check=True)
                    mm.then_inc(s_wo, 1)

            pe.wait_ge(s_on, 2 * UNITS)
            project(0, wo1, lambda c: None)

            pe.wait_ge(s_qc, 2)
            pe.wait_ge(s_x3, NC)
            pe.matmul(bank(6)[:, 0:2], BBm, qg2, start=True, stop=True).then_inc(s_qk, 1)
            pe.wait_ge(s_onc, NC)
            for c in range(NC):
                pe.wait_ge(s_xn, NC * 3 + c + 1)
                if c >= 2:
                    pe.wait_ge(s_xt, NC * 2 + c - 1)
                for j in range(2):
                    for i in range(4):
                        mm = pe.transpose(bank(2 * (c % 2) + j)[:, P * i:P * i + P],
                                          ln_chunk_buf(c)[:, i, P * j:P * j + P], identF[:, :])
                mm.then_inc(s_tr, 1)
            pe.wait_ge(s_xt, 3 * NC)
            pe.wait_ge(s_wq3, 16)
            pe.wait_ge(s_qc, 7)

            def sim_products(c):
                pe.wait_ge(s_qs, c + 1)
                for i in range(4):
                    for j in range(2):
                        o = 16 * (4 * c + i) + 8 * j
                        first = c == 0 and i == 0 and j == 0
                        pe.matmul(bank(0)[:, o:o + 8], Qsq[:, c % 2, j, P * i:P * i + P], blk[:, :],
                                  start=first, stop=True, skip_group_check=True)
                        mm = pe.matmul(bank(1)[:, o:o + 8], Qf[:, c % 2, j, P * i:P * i + P], qgb[:, j, :],
                                       start=first, stop=True, skip_group_check=True)
                mm.then_inc(s_sim, 1)

            for c in range(NC):
                t = slice(512 * c, 512 * c + 512)
                for kind in range(2):
                    if c >= 1:
                        if kind == 0:
                            pe.wait_ge(s_qf, c)
                        else:
                            pe.wait_ge(s_kf, c)
                    for j in range(2):
                        for i in range(2):
                            mm = pe.matmul(bank(2 + 2 * kind + j), wqkv[:, i, C * kind + P * j:C * kind + P * j + P],
                                           XNT[:, i, t], start=(i == 0), stop=(i == 1))
                    mm.then_inc(s_qp, 1)
                if c >= 1:
                    pe.wait_ge(s_vf, c)
                for i in range(4):
                    for j in range(2):
                        mm = pe.matmul(bank(6 + i // 2)[:, C * (i % 2):C * (i % 2) + C],
                                       XNT[:, j, 512 * c + P * i:512 * c + P * i + P], wqkv[:, j, 2 * C:3 * C],
                                       start=(i % 2 == 0 and j == 0), stop=(j == 1), skip_group_check=True)
                mm.then_inc(s_qp, 1)
                if c >= 1:
                    sim_products(c - 1)
            sim_products(NC - 1)
            pe.wait_ge(s_sc2, 9)
            pe.transpose(bank(2)[0:2, 0:P], mm2, identF[:, :]).then_inc(s_mmt, 1)
            pe.wait_ge(s_sc2, 11)
            pe.matmul(bank(3)[:, 0:2], ones2, mmd, start=True, stop=True).then_inc(s_mmb, 1)
            pe.wait_ge(s_sc2, CLS_DONE - 1)
            pe.transpose(bank(2)[:, 0:P], cls.rearrange("p k i -> p (k i)"), identF[:, :]).then_inc(s_clt, 1)
            pe.wait_ge(s_sc2, CLS_DONE)
            pe.wait_ge(s_crl, 16)

            def register_scores(b):
                if b >= 2:
                    pe.wait_ge(s_rex, b - 1)
                for q in range(2):
                    t = slice(S * b + 512 * q, S * b + 512 * q + 512)
                    for j in range(2):
                        o = bank(2 + 2 * (b % 2) + q)[64 * j:64 * j + 64, :]
                        pe.matmul(o, Qbd[:, b, j, :], KT[:, j, t], start=True, stop=False)
                        mm = pe.matmul(o, onesb, crow[:, t], start=False, stop=True)
                mm.then_inc(s_rq, 1)

            pe.wait_ge(s_qrr, B + 3)
            register_scores(0)
            for b in range(B):
                if b + 1 < B:
                    register_scores(b + 1)
                pe.wait_ge(s_rex, b + 1)
                if b >= 1:
                    pe.wait_ge(s_rpc, b)
                for k in range(TB):
                    mm = pe.transpose(bank(6 + k // 4)[:, P * (k % 4):P * (k % 4) + P], Pn[:, P * k:P * k + P],
                                      identF[:, :])
                mm.then_inc(s_rpt, 1)
                pe.wait_ge(s_rpc, b + 1)
                if b >= 1:
                    pe.wait_ge(s_rk, 2 * b)
                for j in range(2):
                    for k in range(TB):
                        mm = pe.matmul(bank(0)[64 * j:64 * j + 64, 0:P], PnT[:, k, 64 * j:64 * j + 64],
                                       V2[:, 4 * b + 2 * j:4 * b + 2 * j + 2, k, :],
                                       start=(k == 0), stop=(k == TB - 1))
                mm.then_inc(s_rv, 1)
                pe.wait_ge(s_rk, 2 * b + 2)
                if b >= 1:
                    pe.wait_ge(s_rgn, b)
                pe.matmul(bank(1)[0:REG, 0:C], Rsel, omk.rearrange("p j n -> p (j n)"),
                          start=True, stop=True).then_inc(s_rsm, 1)
            pe.wait_ge(s_rgn, B)
            pe.wait_ge(s_vpre, 6)

            def take_turn(n, k):
                pe.wait_ge(s_tfree, n + 1)
                return bank(2 * (k % 2), 2)

            def max_tile(n, k, a, j):
                pl = take_turn(n, k)
                q, h = a // 4, a % 4
                for i in range(2):
                    mm = pe.matmul(pl[:, 512 * i:512 * i + 512], QST[j][0:MAX_ROW, h, P * q:P * q + P],
                                   KST[j][0:MAX_ROW, h, 512 * i:512 * i + 512], start=True, stop=True)
                mm.then_inc(s_turn, 1)

            def max_rows(n, k, half, seen):
                pl = take_turn(n, k)
                pe.wait_ge(s_neg, seen)
                pe.transpose(pl[0:16, 0:P], MXn[:, half].rearrange("p j q -> p (j q)"), identF[:, :]).then_inc(s_turn, 1)

            def out_turn(n, k, half, seen):
                pl = take_turn(n, k)
                pe.wait_ge(s_oe2, seen)
                for i in range(4):
                    mm = pe.transpose(pl[:, P * i:P * i + P], Oe2[:, half, P * i:P * i + P], identF[:, :])
                mm.then_inc(s_turn, 1)

            def values2(u, s, j):
                half, k = s // 8, s % 8
                pe.wait_ge(s_sfree, 3 + 64 * u + 4 * s + 4)
                if k == 0:
                    pe.wait_ge(s_oe2, 2 * u + half + 1)
                for h in range(4):
                    mm = pe.matmul(bank(7)[32 * h:32 * h + 32, :], VST[j][:, k, h, :], PR[:, s % 2, h, :],
                                   start=(k == 0), stop=(k == TB - 1))
                mm.then_inc(s_pv2, 1)

            def scores2(u, s, h, j):
                n = 4 * s + h
                pe.wait_ge(s_sfree, 64 * u + n + 1)
                pe.matmul(bank(4 + (64 * j + n) % 3), KST[j][0:MAX_ROW + 1, h, P * (s % 8):P * (s % 8) + P],
                          QST[j][0:MAX_ROW + 1, h, 512 * (s // 8):512 * (s // 8) + 512],
                          start=True, stop=True).then_inc(s_sco, 1)

            def body_pe(u, j, loads, last=False):
                base = TURNS0 + TURNS * u
                jn = (j + 1) % 3
                k = 0

                def turns(entries, k):
                    for what, arg in entries:
                        if what == "tile":
                            max_tile(base + k, k, arg, jn)
                        elif what == "rows":
                            max_rows(base + k, k, arg, 2 * u + 2 if arg else 2 * u + 3)
                        else:
                            out_turn(base + k, k, arg, 2 * u + 2 + arg)
                        k += 1
                    return k

                if not last:
                    pe.wait_ge(s_stk[jn], 16 * STACK2_DMAS * loads)
                for n, s in enumerate(ORDER):
                    us, js = (u, j) if s >= SHIFT else (u + 1, jn)
                    if s < SHIFT and last:
                        break
                    if s == 8:
                        pe.wait_ge(s_row[1], 16 * (u + 1))
                    if s == 0:
                        pe.wait_ge(s_row[0], 16 * (u + 2))
                    for h in range(4):
                        scores2(us, s, h, js)
                        if h % 2 == 1:
                            k = turns((PLAN_LAST if last else PLAN)[2 * n + h // 2], k)
                    if s == 0:
                        values2(u, 15, j)
                    else:
                        if s == 1:
                            pe.wait_ge(s_vst, u + 2)
                        values2(us, s - 1, js)
                if last:
                    values2(u, 15, j)
                turns((PLAN_LAST if last else PLAN)[32], k)

            pe.sem_inc(s_pv2, 2)
            pe.wait_ge(s_stk[0], 16 * STACK2_DMAS)
            for a in range(16):
                max_tile(a, a + 1, a, 0)
            max_rows(16, 17, 0, 1)
            for a in range(16, 32):
                max_tile(a + 1, a + 2, a, 0)
                if a == 32 - 4 * SHIFT:
                    pe.wait_ge(s_row[0], 16)
                if a >= 32 - 4 * SHIFT:
                    n = a - (32 - 4 * SHIFT)
                    scores2(0, n // 4, n % 4, 0)
            pe.wait_ge(s_vst, 1)
            for s in range(SHIFT - 1):
                values2(0, s, 0)
            pe.wait_ge(s_one, 3)
            with pe.Fori(0, 5) as i:
                for j in range(3):
                    body_pe(3 * i + j, j, i + 1 if j < 2 else i + 2)
            body_pe(15, 0, 0, last=True)

            pe.wait_ge(s_avg, 1)

            def transposes2(c):
                n = NC + c
                if c >= 2:
                    pe.wait_ge(s_onc, n - 1)
                for j in range(2):
                    for i in range(4):
                        b, t = c // 2, 4 * (c % 2) + i
                        mm = pe.transpose(bank(2 * (c % 2) + j)[:, P * i:P * i + P],
                                          On2[:, t, C * b + P * j:C * b + P * j + P], identF[:, :])
                mm.then_inc(s_onT, 1)

            transposes2(0)
            for c in range(NC):
                n = NC + c
                if c + 1 < NC:
                    transposes2(c + 1)
                pe.wait_ge(s_onc, n + 1)
                if c >= 2:
                    pe.wait_ge(s_x3, n - 1)
                for i in range(4):
                    o = bank(4 + 2 * (c % 2) + i // 2)[:, C * (i % 2):C * (i % 2) + C]
                    for j in range(2):
                        mm = pe.matmul(o, OnT2[:, c % 2, j, P * i:P * i + P], wproj[:, j, :],
                                       start=(i % 2 == 0 and j == 0), stop=(j == 1), skip_group_check=True)
                mm.then_inc(s_wo, 1)

        @block.vector
        def _(dve):
            def ln_stats(k, before):
                for b in range(B):
                    before(b)
                    for i in range(TB * b, TB * b + TB):
                        dve.bn_stats(stats[:, i, :], X[:, i, :]).then_inc(s_st, 1)
                    for i in range(TB * b, TB * b + TB):
                        dve.wait_ge(s_st, NT * k + i + 1)
                        ins_ = dve.bn_aggr(mv[:, i, :], stats[:, i, :])
                    ins_.then_inc(s_ag, 1)
                    if b == 2:
                        ln_chunks(k, range(2), lambda c: None)

            def ln_chunks(k, chunks, then):
                for c in chunks:
                    dve.wait_ge(s_rs, 2 * (B * k + c // 2) + 2)
                    if NC * k + c >= 2:
                        dve.wait_ge(s_tr, NC * k + c - 1)
                    if k == 1 and c >= 2:
                        dve.wait_ge(s_xg, c - 1)
                    for i in range(4):
                        ins_ = dve.tensor_scalar(ln_chunk_buf(c)[:, i, :], X[:, 4 * c + i, :],
                                                 mv[:, 4 * c + i, 0:1], rstd[:, 4 * c + i:4 * c + i + 1],
                                                 ALU.subtract, ALU.mult)
                    ins_.then_inc(s_xn, 1)
                    then(c)

            ln_stats(0, lambda b: dve.wait_ge(s_x[b], 16))
            ln_chunks(0, range(2, NC), lambda c: None)
            dve.wait_ge(s_const, 8)
            dve.wait_ge(s_m0, 64)
            dve.wait_ge(s_gt, 1)
            def maximum0(b):
                sc = bank(4 + 2 * (b % 2), 2)[0:KX, :]
                dve.wait_ge(s_s0, b + 1)
                dve.copy_predicated(sc, M0[:, b, :], masked.to_broadcast([KX, S])).then_inc(s_mk0, 1)
                dve.wait_ge(s_mk0, b + 1)
                dve.tensor_reduce(mx0[:, b:b + 1], sc, AX, ALU.max).then_inc(s_mx0, 1)
                dve.wait_ge(s_mx0, b + 1)
                dve.tensor_scalar(nb0[:, b:b + 1], mx0[:, b:b + 1], -1.0 / 16, None, ALU.mult).then_inc(s_nb0, 1)

            def scale_values0(b):
                dve.wait_ge(s_e0, b + 1)
                dve.reciprocal(rd0[:, b:b + 1], den0[:, b:b + 1]).then_inc(s_rd0, 1)
                dve.wait_ge(s_rd0, b + 1)
                dve.tensor_scalar(V0s[:, b, :], V0[:, b, :], rd0[:, b:b + 1], gates[0:KX, 0:1],
                                  ALU.mult, ALU.mult).then_inc(s_v0, 1)

            def xattn0_batch(b):
                if b == 0:
                    maximum0(0)
                    scale_values0(0)
                if b + 1 < B:
                    maximum0(b + 1)
                for g in range(4):
                    dve.wait_ge(s_o0, 4 * b + g + 1)
                    xs = X[:, TB * b + 2 * g:TB * b + 2 * g + 2, :]
                    dve.tensor_tensor(xs, bank(g).rearrange("p (i c) -> p i c", i=2), xs, ALU.add).then_inc(s_x1, 1)
                if b + 1 < B:
                    scale_values0(b + 1)
                dve.wait_ge(s_x1, 4 * b + 4)

            def gated_ln(c):
                dve.wait_ge(s_xn, NC + c + 1)
                xs = X[:, 4 * c:4 * c + 4, :]
                dve.scalar_tensor_tensor(xs, ln_chunk_buf(c), gates[:, 2:3], xs, ALU.mult, ALU.add).then_inc(s_xg, 1)

            ln_stats(1, xattn0_batch)
            for c in range(2):
                gated_ln(c)
            ln_chunks(1, range(2, NC), gated_ln)
            G = bank(7)[:, 0:E * NT].rearrange("p (i e) -> p i e", e=E)
            dve.wait_ge(s_fc, 2 + E)
            dve.wait_ge(s_gl, NC)
            dve.tensor_reduce(gmx, G, AX, ALU.max).then_inc(s_gc, 1)
            dve.wait_ge(s_gc, 1)
            dve.tensor_tensor(eq6, G, gmx.unsqueeze(2).to_broadcast([P, NT, E]), ALU.is_equal).then_inc(s_gc, 1)
            dve.wait_ge(s_gc, 2)
            dve.tensor_tensor(eq6, eq6, wtie.unsqueeze(1).to_broadcast([P, NT, E]), ALU.mult).then_inc(s_gc, 1)
            dve.wait_ge(s_gc, 3)
            dve.tensor_reduce(gm2, eq6, AX, ALU.max).then_inc(s_gc, 1)
            dve.wait_ge(s_gc, 4)
            dve.tensor_tensor(eq6, eq6, gm2.unsqueeze(2).to_broadcast([P, NT, E]), ALU.is_equal).then_inc(s_gc, 1)
            dve.wait_ge(s_gc, 5)
            dve.tensor_copy(OH96[:, :, 0:NB16].rearrange("p i (e r) -> p i e r", e=E),
                            eq6.unsqueeze(3).to_broadcast([P, NT, E, R])).then_inc(s_gc, 1)
            dve.memset(OH96[:, :, NB16:98], 1.0).then_inc(s_gc, 1)
            for c in range(NC):
                dve.wait_ge(s_otc, c + 1)
                v = slice(512 * c, 512 * c + 512)
                dve.tensor_tensor(ysel[:, v], ysel[:, v], OHT[0:NB16, v], ALU.mult).then_inc(s_ys, 1)

            def attn_norm(c):
                v = slice(4 * c, 4 * c + 4)
                dve.wait_ge(s_ae, c + 1)
                dve.tensor_reduce(asum[:, v, :], attn[:, v, :], AX, ALU.add).then_inc(s_as, 1)
                dve.wait_ge(s_as, c + 1)
                dve.reciprocal(arec[:, v, :], asum[:, v, :]).then_inc(s_ar, 1)
                dve.wait_ge(s_ar, c + 1)
                dve.tensor_tensor(attn[:, v, :], attn[:, v, :], arec[:, v, :].to_broadcast([P, 4, L]),
                                  ALU.mult).then_inc(s_an, 1)

            for c in range(NC):
                v = slice(4 * c, 4 * c + 4)
                lg = bank(4 + c % 2)[:, 0:4 * L].rearrange("p (i l) -> p i l", i=4)
                dve.wait_ge(s_lg, c + 1)
                dve.tensor_reduce(amx[:, v, :], lg, AX, ALU.max).then_inc(s_am, 1)
                dve.wait_ge(s_am, c + 1)
                dve.tensor_tensor(attn[:, v, :], lg, amx[:, v, :].to_broadcast([P, 4, L]),
                                  ALU.subtract).then_inc(s_ad, 1)
                if c >= 1:
                    attn_norm(c - 1)
            attn_norm(NC - 1)
            for c in range(NC):
                v = slice(512 * c, 512 * c + 512)
                dve.wait_ge(s_u, c + 1)
                dve.tensor_tensor(usel[:, v], bank(4 + c % 2)[0:98, :], OHT[:, v], ALU.mult).then_inc(s_us, 1)
            dve.wait_ge(s_w1, 16 * 28)
            for i in range(3):
                dve.tensor_tensor(bd[:, i, :].rearrange("p (g d) -> p g d", g=8),
                                  w16[:, i, :].unsqueeze(1).to_broadcast([P, 8, 16]),
                                  blk[:, :].unsqueeze(2).to_broadcast([P, 8, 16]), ALU.mult).then_inc(s_bd, 1)

            def replace_zeros(c):
                v = comb[:, 4 * c:4 * c + 4, :]
                z = zfix[:, c % 2].rearrange("p (i n) -> p i n", i=4)
                dve.wait_ge(s_de, c + 1)
                if c >= 2:
                    dve.wait_ge(s_z2, c - 1)
                dve.tensor_scalar(z, v, 0.0, TINY, ALU.is_equal, ALU.mult).then_inc(s_z1, 1)
                dve.wait_ge(s_z1, c + 1)
                dve.tensor_tensor(v, v, z, ALU.add).then_inc(s_z2, 1)

            def add_log(c):
                xs = X[:, 4 * c:4 * c + 4, :]
                dve.wait_ge(s_ln, c + 1)
                dve.scalar_tensor_tensor(xs, comb[:, 4 * c:4 * c + 4, :], gates[:, 2:3], xs,
                                         ALU.mult, ALU.add).then_inc(s_x2, 1)

            def x2_batch(b):
                for c in (2 * b, 2 * b + 1):
                    if c == 0:
                        replace_zeros(0)
                    if c + 1 < NC:
                        replace_zeros(c + 1)
                    add_log(c)
                dve.wait_ge(s_x2, 2 * b + 2)

            ln_stats(2, x2_batch)
            dve.wait_ge(s_dl, NC)
            dve.memset(V1a, 0.0).then_inc(s_v1m, 1)
            dve.wait_ge(s_v1m, 1)
            dve.memset(V1a[:, :, :, D:D + 1], 1.0).then_inc(s_v1m, 1)
            dve.wait_ge(s_m1, 16)
            dve.tensor_scalar(mb1, M1u, -1.0, BIG, ALU.add, ALU.mult).then_inc(s_mk1, 1)
            dve.tensor_copy(I4.rearrange("p (j n) -> p j n", j=4),
                            identB[0:KX, 0:KX].unsqueeze(1).to_broadcast([KX, 4, KX])).then_inc(s_mk1, 1)
            dve.tensor_copy(HS, identB[0:4, 0:4].unsqueeze(2).to_broadcast([4, 4, KX])).then_inc(s_mk1, 1)
            dve.wait_ge(s_k1c, 2)
            dve.tensor_tensor(kr1, bank(6, 2).rearrange("p (j n) -> p j n", j=2)[:, :, 0:308], kpart[:, 0],
                              ALU.subtract).then_inc(s_kr, 1)
            dve.wait_ge(s_kr, 1)
            dve.tensor_copy(kpart[:, 1], kr1).then_inc(s_kr, 1)
            dve.wait_ge(s_kr, 2)
            dve.tensor_tensor(kr1, kr1, kpart[:, 1], ALU.subtract).then_inc(s_kr, 1)
            dve.wait_ge(s_kr, 3)
            dve.tensor_copy(kpart[:, 2], kr1).then_inc(s_kr, 2)

            def residue(c):
                dve.wait_ge(s_ph, c + 1)
                if c >= 2:
                    dve.wait_ge(s_pl, c - 1)
                dve.tensor_tensor(xres[:, c % 2], bank(2 * (c % 2), 2).rearrange("p (j t) -> p j t", j=2),
                                  PB[:, c % 2, 0], ALU.subtract).then_inc(s_pr, 1)

            ln_chunks(2, range(2, NC), lambda c: residue(c - 2))
            residue(NC - 2)
            residue(NC - 1)

            def reduce1(u, qs):
                for q in qs:
                    n = 8 * u + q
                    dve.wait_ge(s_mp, n + 1)
                    dve.tensor_reduce(M1[:, u % 2, q, :],
                                      bank(n % 2)[:, 0:4 * KX].rearrange("p (j n) -> p j n", j=4), AX,
                                      ALU.max).then_inc(s_mr, 1)

            def maxima1(m):
                u, v = m // 2, slice(4 * (m % 2), 4 * (m % 2) + 4)
                reduce1(u, range(v.start, v.stop))
                if m >= 4:
                    dve.wait_ge(s_mt, m - 3)
                dve.wait_ge(s_mr, 4 * m + 4)
                dve.tensor_scalar(Mn[:, u % 2, v], M1[:, u % 2, v], -1.0, None, ALU.mult).then_inc(s_mn, 1)

            def normalise1(m):
                u, q = m // 2, m % 2
                b, hg = u // 4, u % 4
                O = bank(3).rearrange("p (q j d) -> p q j d", q=4, j=4)
                dve.wait_ge(s_ot1, m + 1)
                if m >= 1:
                    dve.wait_ge(s_on, m)
                dve.reciprocal(rc1, O[:, :, :, D]).then_inc(s_rc, 1)
                dve.wait_ge(s_rc, m + 1)
                dst = On[:, TB * b + 4 * q:TB * b + 4 * q + 4, 64 * hg:64 * hg + 64]
                dve.tensor_tensor(dst.rearrange("p q (j d) -> p q j d", j=4), O[:, :, :, 0:D],
                                  rc1.unsqueeze(3).to_broadcast([P, 4, 4, D]), ALU.mult).then_inc(s_on, 1)

            maxima1(0)
            maxima1(1)
            for m in range(2 * UNITS):
                if m + 2 < 2 * UNITS:
                    maxima1(m + 2)
                if m >= 2:
                    normalise1(m - 2)
            normalise1(2 * UNITS - 2)
            normalise1(2 * UNITS - 1)

            def x3_batch(b):
                for c in (2 * b, 2 * b + 1):
                    dve.wait_ge(s_wo, c + 1)
                    dve.wait_ge(s_xb, b + 1)
                    xs = X[:, 4 * c:4 * c + 4, :]
                    dve.scalar_tensor_tensor(xs, bank(4 + 2 * (c % 2), 2).rearrange("p (i n) -> p i n", i=4),
                                             gates[:, 1:2], xs, ALU.mult, ALU.add).then_inc(s_x3, 1)
                dve.wait_ge(s_x3, 2 * b + 2)

            ln_stats(3, x3_batch)
            dve.wait_ge(s_qgl, 16)
            dve.tensor_tensor(qg2, qgc, qgc, ALU.mult).then_inc(s_qc, 1)
            dve.tensor_copy(BBm.rearrange("p (g d) -> p g d", g=8),
                            blk[:, :].unsqueeze(2).to_broadcast([P, 8, 16])).then_inc(s_qc, 1)
            dve.wait_ge(s_qk, 1)
            dve.tensor_copy(qgn, bank(6)[:, 0:2]).then_inc(s_qc, 1)
            dve.wait_ge(s_qc, 4)
            dve.tensor_tensor(qgn, qgn, qgc, ALU.mult).then_inc(s_qc, 1)
            dve.wait_ge(s_qc, 5)
            for j in range(2):
                dve.tensor_scalar(qgb[:, j, :], blk[:, :], qgn[:, j:j + 1], None, ALU.mult).then_inc(s_qc, 1)
            ln_chunks(3, range(2, NC), lambda c: None)
            for c in range(NC):
                if c == 0:
                    dve.wait_ge(s_tr, 4 * NC)
                dve.wait_ge(s_qh, c + 1)
                if c >= 1:
                    dve.wait_ge(s_ql, c)
                dve.tensor_tensor(res2[:, 0], Qf[:, c % 2], PB2[:, 0, 0], ALU.subtract).then_inc(s_qr, 1)
                dve.wait_ge(s_qp, 3 * c + 2)
                kt = KT[:, :, 512 * c:512 * c + 512]
                dve.tensor_copy(kt, bank(4, 2).rearrange("p (j t) -> p j t", j=2)).then_inc(s_kf, 1)
                dve.wait_ge(s_kh, c + 1)
                if c >= 1:
                    dve.wait_ge(s_kl, c)
                dve.tensor_tensor(res2[:, 1], kt, PB2[:, 1, 0], ALU.subtract).then_inc(s_krs, 1)
                dve.wait_ge(s_qp, 3 * c + 3)
                b, t = c // 2, 4 * (c % 2)
                for g in range(4):
                    vv = dve.tensor_copy(V2[:, 4 * b + g, t:t + 4, :],
                                         bank(6, 2).rearrange("p (i n) -> p i n", i=4)[:, :, 64 * g:64 * g + 64])
                vv.then_inc(s_vf, 1)
                if c % 2 == 0:
                    dve.wait_ge(s_qf, c + 1)
                    dve.tensor_copy(QR[:, :, b, :], Qf[:, c % 2, :, 0:REG]).then_inc(s_qrr, 1)
            ch = [0]

            def link(ins_, wait=True):
                ch[0] += 1
                ins_.then_inc(s_sc2, 1)
                if wait:
                    dve.wait_ge(s_sc2, ch[0])

            dve.wait_ge(s_sim, NC)
            dve.wait_ge(s_c2, 6 + B)
            dve.wait_ge(s_rp, 1)
            link(dve.reciprocal(rn2, rn2))
            link(dve.tensor_tensor(dt2, bank(1), rn2, ALU.mult))
            assert ch[0] == SIM_READ
            link(dve.tensor_reduce(simr, dt2.rearrange("p (i h) -> p i h", h=H), AX, ALU.add))
            link(dve.tensor_scalar(simc, simr, 1.0 / H, None, ALU.mult))
            link(dve.scalar_tensor_tensor(tmp32, regm, -BIG, simc, ALU.mult, ALU.add))
            link(dve.tensor_reduce(mm2[:, 0:1], tmp32, AX, ALU.max))
            link(dve.scalar_tensor_tensor(tmp32, regm, BIG, simc, ALU.mult, ALU.add))
            link(dve.tensor_reduce(mm2[:, 1:2], tmp32, AX, ALU.min))
            link(dve.tensor_scalar(mm2[:, 1:2], mm2[:, 1:2], -1.0, None, ALU.mult))
            dve.wait_ge(s_mmt, 1)
            link(dve.tensor_reduce(mmr, bank(2)[0:2, 0:P], AX, ALU.max))
            link(dve.tensor_scalar(mmd, identF[0:2, 0:2], mmr, None, ALU.mult))
            dve.wait_ge(s_mmb, 1)
            link(dve.tensor_copy(mmb, bank(3)[:, 0:2]))
            link(dve.tensor_tensor(rng, mmb[:, 0:1], mmb[:, 1:2], ALU.add))
            link(dve.reciprocal(rrg, rng))
            link(dve.tensor_scalar(simc, simc, mmb[:, 1:2], rrg, ALU.add, ALU.mult))
            link(dve.tensor_scalar(tmp32, simc, 0.9, None, ALU.is_gt))
            link(dve.tensor_scalar(simr, regm, -1.0, 1.0, ALU.mult, ALU.add))
            link(dve.tensor_tensor(tmp32, tmp32, simr, ALU.mult))
            link(dve.tensor_tensor(cls[:, 1, :], tmp32, regm, ALU.add))
            link(dve.tensor_scalar(cls[:, 0, :], cls[:, 1, :], -1.0, 1.0, ALU.mult, ALU.add))
            link(dve.tensor_scalar(cls[:, 2, :], tmp32, -BIG, None, ALU.mult))
            link(dve.tensor_scalar(cls[:, 3, :], cls[:, 0, :], -BIG, None, ALU.mult))
            dve.wait_ge(s_clt, 1)
            link(dve.tensor_copy(clsT, bank(2)[:, 0:P]))
            assert ch[0] == CLS_DONE
            dve.memset(W[:, 2048:2816], 0.0).then_inc(s_qrr, 1)
            dve.wait_ge(s_qrr, B + 1)
            for j in range(2):
                dve.tensor_tensor(Qbd[:, :, j, 0:8 * REG].rearrange("p b (g r) -> p b g r", g=8),
                                  QR[:, j].unsqueeze(2).to_broadcast([P, B, 8, REG]),
                                  blk[:, :].unsqueeze(1).unsqueeze(3).to_broadcast([P, B, 8, REG]),
                                  ALU.mult).then_inc(s_qrr, 1)
            dve.tensor_reduce(rmask, Rfull, AX, ALU.add).then_inc(s_c2, 1)
            dve.tensor_reduce(Rsel, Rfull.rearrange("p g r -> p r g"), AX, ALU.add).then_inc(s_c2, 1)
            dve.wait_ge(s_c2, 8 + B)

            def register_values(b):
                dve.wait_ge(s_rex, b + 1)
                dve.reciprocal(rrd[:, b:b + 1], rden[:, b:b + 1]).then_inc(s_rc2, 1)
                dve.wait_ge(s_rc2, b + 1)
                dve.wait_ge(s_rv, b + 1)
                if b >= 1:
                    dve.wait_ge(s_rsm, b)
                for j in range(2):
                    v = slice(64 * j, 64 * j + 64)
                    dve.scalar_tensor_tensor(omk[v, j].rearrange("p (g d) -> p g d", g=8),
                                             bank(0)[v, 0:P].rearrange("p (g d) -> p g d", g=8), rrd[v, b:b + 1],
                                             rmask[v].unsqueeze(2).to_broadcast([64, 8, D]), ALU.mult,
                                             ALU.mult).then_inc(s_rk, 1)
                dve.wait_ge(s_rsm, b + 1)
                dve.tensor_scalar(regn[:, b, :], bank(1)[0:REG, 0:C], 0.5, None, ALU.mult).then_inc(s_rgn, 1)

            for b in range(B):
                dve.wait_ge(s_rq, b + 1)
                dve.tensor_reduce(rmx[:, b:b + 1], bank(2 + 2 * (b % 2), 2), AX, ALU.max).then_inc(s_rm, 1)
                dve.wait_ge(s_rm, 2 * b + 1)
                dve.tensor_scalar(rnm[:, b:b + 1], rmx[:, b:b + 1], -0.25, None, ALU.mult).then_inc(s_rm, 1)
                if b >= 1:
                    register_values(b - 1)
            register_values(B - 1)

            def turn_wait(n):
                dve.wait_ge(s_turn, n + 1)

            def reduce_tile(n, k, a):
                half, q, h = a // 16, a // 4 % 4, a % 4
                turn_wait(n)
                dve.tensor_reduce(MX[:, half, h, q:q + 1], bank(2 * (k % 2), 2), AX, ALU.max).then_inc(s_tfree, 1)

            def negate(n, half):
                dve.wait_ge(s_tfree, 2 + n)
                dve.tensor_scalar(MXn[:, half], MX[:, half], -1.0, None, ALU.mult).then_inc(s_neg, 1)

            def rows_turn(n, k, half):
                turn_wait(n)
                dve.tensor_copy(mro[:, half, :], bank(2 * (k % 2))[0:16, 0:P]).then_inc(s_tfree, 1)

            def normalise2(n, k, u, half):
                O = bank(2 * (k % 2)).rearrange("p (q j d) -> p q j d", q=4, j=4)
                dve.wait_ge(s_tfree, 2 + n)
                turn_wait(n)
                dve.reciprocal(rc2, O[:, :, :, D]).then_inc(s_rc2, 1)
                dve.wait_ge(s_rc2, 2 * u + half + 1 + B)
                dst = On2[:, 4 * half:4 * half + 4, bass.ds(64 * u, 64)].rearrange("p q (j d) -> p q j d", j=4)
                dve.tensor_tensor(dst, O[:, :, :, 0:D], rc2.unsqueeze(3).to_broadcast([P, 4, 4, D]),
                                  ALU.mult).then_inc(s_tfree, 1)

            dve.sem_inc(s_tfree, 2)
            for a in range(16):
                reduce_tile(a, a + 1, a)
            negate(16, 0)
            rows_turn(16, 17, 0)
            for a in range(16, 32):
                reduce_tile(a + 1, a + 2, a)
            negate(33, 1)

            def body_dve(u, j, last=False):
                base = TURNS0 + TURNS * u
                k = 0
                for step in (PLAN_LAST if last else PLAN):
                    for what, arg in step:
                        if what == "tile":
                            reduce_tile(base + k, k, arg)
                        elif what == "rows":
                            rows_turn(base + k, k, arg)
                        else:
                            normalise2(base + k, k, u, arg)
                        k += 1
                        if (what, arg) == ("tile", 15):
                            negate(base + k, 0)
                        if (what, arg) == ("tile", 31):
                            negate(base + k, 1)

            with dve.Fori(0, 5) as i:
                for j in range(3):
                    body_dve(3 * i + j, j)
            body_dve(15, 0, last=True)
            dve.wait_ge(s_tfree, 2 + TURNS0 + TURNS * 15 + 3)
            dve.scalar_tensor_tensor(On2[0:REG, 0, :], On2[0:REG, 0, :], 0.5,
                                     regn.rearrange("p b c -> p (b c)"), ALU.mult,
                                     ALU.add).then_inc(s_avg, 1)
            for c in range(NC):
                dve.wait_ge(s_wo, NC + c + 1)
                dve.wait_ge(s_xb2, c // 2 + 1)
                xs = X[:, 4 * c:4 * c + 4, :]
                dve.scalar_tensor_tensor(xs, bank(4 + 2 * (c % 2), 2).rearrange("p (i n) -> p i n", i=4),
                                         gates[:, 3:4], xs, ALU.mult, ALU.add).then_inc(s_x3, 1)


def kernel(**inputs):
    import numpy as _np
    import concourse.bacc as _bacc
    from concourse import mybir as _mybir
    from concourse.bass_utils import run_bass_kernel_spmd as _run

    i = {k: _np.asarray(v) for k, v in inputs.items()}
    lay = {
        "x": i["x"],
        "ctxT": i["ctx_1024"].transpose(2, 0, 1).reshape(C, B * KX),
        "wk0T": i["L0_xattn_Wk"].T,
        "wq0": i["L0_xattn_Wq"],
        "wv0T": i["L0_xattn_Wv"].T,
        "mask0T": i["mask_BxSxS2_bk0"].transpose(0, 2, 1),
        "mask1T": i["mask_1x1xSxS2_bk0"][0, 0].T,
        "g_xattn": i["g_xattn"],
        "g_ffn": i["g_ffn"],
        "w_gate": i["L0_ffn_w_gate"],
        "ballT": i["L0_ffn_B"].transpose(2, 0, 1).reshape(C, E * R),
        "AT": i["L0_ffn_A"].transpose(0, 2, 1).reshape(E * R, L),
        "A1": i["L0_ffn_A"].transpose(1, 0, 2).reshape(L, E * R),
        "wtT": i["L0_ffn_wt_w"].T,
        "wt_b": i["L0_ffn_wt_b"],
        "wdT": i["L0_ffn_wd_w"].T,
        "wd_b": i["L0_ffn_wd_b"],
        "scale": i["L0_ffn_scale"],
        "wv1T": i["L1_xattn_Wv"].T,
        "wk1T": i["L1_xattn_Wk"].T,
        "wq1": i["L1_xattn_Wq"],
        "wo1T": i["L1_xattn_Wo"].T,
        "bo1": i["L1_xattn_bo"],
        "g_info": i["L1_ffn_g_info"],
        "wqkv": i["L1_ffn_W_qkv"],
        "wproj": i["L1_ffn_W_proj"],
        "bproj": i["L1_ffn_b_proj"],
    }
    nc = _bacc.Bacc("TRN2", target_bir_lowering=False, num_devices=1)
    arrays, args = {}, {}
    for name, a in lay.items():
        a = _np.ascontiguousarray(a)
        arrays[f"in_{name}"] = a
        args[name] = nc.dram_tensor(f"in_{name}", a.shape, _mybir.dt.from_np(a.dtype), kind="ExternalInput").ap()
    out = nc.dram_tensor("out_0", (B, S, C), F32, kind="ExternalOutput").ap()
    build_program(nc, args, out)
    r = _run(nc, [arrays], core_ids=[0])
    return r.results[0]["out_0"]
```

```python
from contextlib import ExitStack

import numpy as np
import concourse.bass as bass
from concourse import mybir

F32 = mybir.dt.float32
BF16 = mybir.dt.bfloat16
U8 = mybir.dt.uint8
ALU = mybir.AluOpType
ACT = mybir.ActivationFunctionType
AX = mybir.AxisListType.X

B, S, C = 4, 1024, 256
KX = 77
H, D = 16, 16
E, L, R = 6, 100, 16
REG = 5
P = 128
T = B * S
NT = T // P
NC = T // 512
TB = S // P
UNITS = B * 4
BIG = 2.0 ** 66
LN_EPS = 1e-5
TINY = float(np.finfo(np.float32).eps)
Q_ORDER, K_ORDER = (0, 0, 0, 1, 1, 2), (0, 1, 2, 0, 1, 0)
SR = 96
NEG_ROW, POS_ROW, MAX_ROW = 96, 97, 98


def build_program(nc, ins, out):
    ctx = ExitStack()
    with ctx:
        def sb(name, shape, dt=F32):
            return ctx.enter_context(nc.sbuf_tensor(name, shape, dt))

        def sem(name):
            return ctx.enter_context(nc.semaphore(name))

        X = sb("X", [P, NT, C])
        R1 = sb("R1", [P, 8192])
        R2 = sb("R2", [P, 8192])
        R3 = sb("R3", [P, 8192])
        R4 = sb("R4", [P, 4096])
        XNT = R1[:, :].rearrange("p (j t) -> p j t", j=2)

        XN = sb("XN", [P, 2, 4, C])
        stats = sb("stats", [P, NT, 6])
        mv = sb("mv", [P, NT, 2])
        rstd = sb("rstd", [P, NT])
        mhalf = sb("mhalf", [P, NT])
        identF = sb("identF", [P, P])
        identB = sb("identB", [P, P], BF16)
        gates = sb("gates", [P, 4])
        small = sb("small", [P, 640])

        ps = ctx.enter_context(nc.psum_tensor("ps", [P, 4096], F32))

        def bank(i, n=1):
            return ps[:, 512 * i:512 * (i + n)]

        W = sb("W", [P, 4608])
        at = [0]

        def w(n):
            at[0] += n
            assert at[0] <= 4608
            return W[:, at[0] - n:at[0]]

        def w2(n):
            return w(2 * n).rearrange("p (j n) -> p j n", j=2)

        ctxT = w2(B * KX)
        wbig = w(1536)
        wk0 = wbig[:, 0:512].rearrange("p (j n) -> p j n", j=2)
        wq0 = wbig[:, 512:1024].rearrange("p (j n) -> p j n", j=2)
        wv0 = wbig[:, 1024:1536].rearrange("p (j n) -> p j n", j=2)
        wqkv = wbig.rearrange("p (j n) -> p j n", j=2)
        wA = w(1616)

        def wa(a, n, j=None):
            v = wA[:, a:a + n]
            return v if j is None else v.rearrange("p (j n) -> p j n", j=j)

        ballg, wtT, wdT = wa(0, 204, 2), wa(204, 512, 2), wa(716, 512, 2)
        ballT, wg = ballg[:, :, 0:96], ballg[:, :, 96:102]
        AT, A1x = wa(1228, 100), wa(1328, 98)
        BW = sb("BW", [P, C])
        BWt = sb("BWt", [P, 2, 97])
        wo1 = sb("wo1", [P, 2, C])
        wproj = sb("wproj", [P, 2, C])
        bo1 = sb("bo1", [P, C])
        bp2 = sb("bp2", [P, C])
        w16 = sb("w16", [P, 3, 16])
        bd = sb("bd", [P, 3, P])
        blk = sb("blk", [P, 8])

        R2f = R2[:, :]
        R3f = R3[:, :]

        s_x = [sem(f"x_loaded{b}") for b in range(B)]
        s_w0 = sem("xattn0_weights_loaded")
        s_m0 = sem("mask0_loaded")
        s_g = sem("gates_loaded")
        s_const = sem("constants_made")
        s_gt = sem("gates_tanh")
        s_ks = sem("setup_product")
        s_ksc = sem("setup_copied")
        s_st = sem("stats_done")
        s_ag = sem("aggregated")
        s_rs = sem("rstd_done")
        s_xn = sem("chunk_normalised")
        s_tr = sem("chunk_transposed")
        s_xt = sem("chunk_transpose_copied")

        R5 = sb("R5", [P, 4096])
        block = ctx.enter_context(nc.Block())
        kT0 = R2f[:, 0:616].rearrange("p (j n) -> p j n", j=2)
        KW0 = R2f[:, 616:1232].rearrange("p (j n) -> p j n", j=2)
        V0 = R2f[0:KX, 1232:2256].rearrange("p (b n) -> p b n", b=B)
        P0 = R2f[0:KX, 2256:6352].rearrange("p (b n) -> p b n", b=B)
        V0s = R2f[0:KX, 6352:7376].rearrange("p (b n) -> p b n", b=B)
        M0 = R3f[0:KX, 0:1024].bitcast(U8).rearrange("p (b n) -> p b n", b=B)
        masked = R3f[0:KX, 1024:1025]
        mx0 = small[0:KX, 0:4]
        nb0 = small[0:KX, 4:8]
        den0 = small[0:KX, 8:12]
        rd0 = small[0:KX, 12:16]
        graw = small[:, 16:20]
        s_s0 = sem("scores0")
        s_nb0 = sem("scores0_masked_max_negmax")
        s_e0 = sem("probs0")
        s_rd0 = sem("recip0")
        s_v0 = sem("values0_scaled")
        s_o0 = sem("out0")
        s_x1 = sem("x1_added")

        NB16 = E * R
        OH96 = R3f[:, 0:1568].bitcast(BF16).rearrange("p (i n) -> p i n", i=NT)
        attn = R3f[:, 1568:4768].rearrange("p (i l) -> p i l", i=NT)
        OHT = R4[0:98, 0:2048].bitcast(BF16)
        ysel = R2f[0:NB16, 0:4096]
        yg = R2f[0:NB16 + E, 0:4096]
        usel = R2f[0:98, 0:4096]
        aT = R2f[0:L, 4096:8192]
        comb = R3f.rearrange("p (i c) -> p i c", i=NT)
        zfix = R4[:, 2048:4096].rearrange("p (u n) -> p u n", u=2)
        gmx = small[:, 32:64]
        eq6 = small[:, 64:256].rearrange("p (i e) -> p i e", e=E)
        gm2 = small[:, 256:288]
        wtie = small[:, 288:294]
        amx = small[:, 296:328].rearrange("p (i o) -> p i o", o=1)
        asum = small[:, 328:360].rearrange("p (i o) -> p i o", o=1)
        arec = small[:, 360:392].rearrange("p (i o) -> p i o", o=1)
        fscale = small[:, 392:393]
        s_wf = sem("ffn0_weights_loaded")
        s_fc = sem("ffn0_constants")
        s_fs = sem("ffn0_setup_product")
        s_fsc = sem("ffn0_setup_copied")
        s_xg = sem("gated_ln_added")
        s_gl = sem("gate_logits")
        s_gc = sem("gate_chain")
        s_ot = sem("onehot_transposed")
        s_otc = sem("onehot_copied")
        s_y = sem("y_product")
        s_yc = sem("y_copied")
        s_ys = sem("y_selected")
        s_lg = sem("landmark_logits")
        s_am = sem("landmark_max")
        s_ad = sem("landmark_minus_max")
        s_ae = sem("landmark_exp")
        s_as = sem("landmark_sum")
        s_ar = sem("landmark_recip")
        s_an = sem("landmark_attn")
        s_at = sem("attn_transposed")
        s_atc = sem("attn_copied")
        s_u = sem("u_product")
        s_us = sem("u_selected")
        s_dl = sem("delta_product")
        s_de = sem("delta_exp")
        s_z1 = sem("zero_found")
        s_z2 = sem("zero_replaced")
        s_ln = sem("combined_log")
        s_x2 = sem("x2_added")

        XP = nc.dram_tensor("x_parts", (3, C, T), BF16).ap()
        KXP = nc.dram_tensor("ctx_key_parts", (3, C, B * KX), BF16).ap()
        SR1 = SR + 4
        K1s = R2f[0:SR1, 0:2464].bitcast(BF16).rearrange("p (h n) -> p h n", h=H)
        V1a = R2f[0:KX, 2464:4512].rearrange("p (b h d) -> p b h d", b=B, h=H)
        mb1 = R2f[0:KX, 4512:5024].bitcast(BF16)
        M1u = R2f[0:KX, 5024:5280].bitcast(U8)
        I4 = R2f[0:KX, 5280:5434].bitcast(BF16)
        Oe = R2f[:, 6100:7124].rearrange("p (u n) -> p u n", u=2)
        k1T = R5[:, 0:616].rearrange("p (j n) -> p j n", j=2)
        kr1 = R5[:, 616:1232].rearrange("p (j n) -> p j n", j=2)
        kpart = R5[:, 1232:2156].bitcast(BF16).rearrange("p (a j n) -> p a j n", a=3, j=2)
        P1 = R3f[0:KX, 0:4096].rearrange("p (u j n) -> p u j n", u=2, j=4)
        PB = R3f[:, 4096:7168].bitcast(BF16).rearrange("p (u a j n) -> p u a j n", u=2, a=3, j=2)
        xres = R4[:, 2048:4096].rearrange("p (u j n) -> p u j n", u=2, j=2)
        Xs = [v.bitcast(BF16).rearrange("p (j n) -> p j n", j=4)
              for v in (R4[0:SR1, 0:2048], R5[0:SR1, 0:2048], R5[0:SR1, 2048:4096])]
        On = R1[:, :].rearrange("p (i c) -> p i c", i=NT)
        OnT = R3f[:, 0:2048].rearrange("p (u j n) -> p u j n", u=2, j=2)
        M1 = small[:, 400:464].rearrange("p (u q j) -> p u q j", u=2, q=8)
        Mn = small[:, 464:528].rearrange("p (u q j) -> p u q j", u=2, q=8)
        rc1 = small[:, 528:544].rearrange("p (q j) -> p q j", q=4)
        s_w1 = sem("layer1_weights_loaded")
        s_bd = sem("block_diagonals_made")
        s_k1 = sem("ctx_keys_product")
        s_k1c = sem("ctx_keys_copied")
        s_kr = sem("ctx_keys_residue")
        s_kw = sem("ctx_key_parts_written")
        s_k1s = sem("ctx_key_stack_loaded")
        s_v1 = sem("ctx_values_product")
        s_v1c = sem("ctx_values_copied")
        s_v1m = sem("ctx_values_preset")
        s_mk1 = sem("mask1_made")
        s_m1 = sem("mask1_loaded")
        s_ph = sem("part_h")
        s_pr = sem("part_residue")
        s_pm = sem("part_m")
        s_pl = sem("part_l")
        s_pw = [sem(f"parts_written{n}") for n in range(2)]
        s_xs = [sem(f"x_stack_loaded{n}") for n in range(3)]
        s_mp = sem("max1_product")
        s_mr = sem("max1_reduced")
        s_mn = sem("max1_negated")
        s_mt = sem("max1_transposed")
        s_mrc = sem("max1_rows")
        s_sc = sem("scores1")
        s_e1 = sem("probs1")
        s_pv = sem("values1_product")
        s_oc = sem("out1_copied")
        s_ot1 = sem("out1_transposed")
        s_rc = sem("out1_recip")
        s_on = sem("out1_normalised")
        s_gb = sem("gated_bias")
        s_xb = sem("bias_added")
        s_onT = sem("heads_transposed")
        s_onc = sem("heads_copied")
        s_wo = sem("projected")
        s_x3 = sem("x3_added")

        STACK_DMAS = 6
        FIRST = 4

        def half_in(m):
            return FIRST + 4 * (m // 8) + m % 8 if m % 8 < 4 and m // 8 + 1 < B else None

        TURNS1 = []
        for m in range(2 * UNITS):
            if half_in(m) is not None:
                TURNS1.append(("half", half_in(m)))
            TURNS1 += [("score", 4 * m + j) for j in range(4)]

        def bank_of(what, n):
            return bank(4 + TURNS1.index((what, n)) % 3)


        QP = nc.dram_tensor("q_parts", (3, B * C, S), BF16).ap()
        KP = nc.dram_tensor("k_parts", (3, B * C, S), BF16).ap()
        MR = nc.dram_tensor("max_rows", (2, 16, P), BF16).ap()
        CR = nc.dram_tensor("class_rows", (4, B, 4, S), BF16).ap()
        KT = R2[:, :].rearrange("p (j t) -> p j t", j=2)
        V2 = R3[:, :].rearrange("p (u k n) -> p u k n", u=UNITS, k=TB)
        On2 = R1[:, :].rearrange("p (k u n) -> p k (u n)", u=UNITS, k=TB)
        PB2 = R5[:, 0:3072].bitcast(BF16).rearrange("p (u a j n) -> p u a j n", u=2, a=3, j=2)
        res2 = XN[:, :, :, :].rearrange("p u i c -> p u (i c)").rearrange("p u (j n) -> p u j n", j=2)
        Qf = R4[:, 0:2048].rearrange("p (u j n) -> p u j n", u=2, j=2)
        Qsq = R4[:, 2048:4096].rearrange("p (u j n) -> p u j n", u=2, j=2)
        QST = [v.bitcast(BF16).rearrange("p (j n) -> p j n", j=4)
               for v in (R4[:, 0:2048], R2[:, 0:2048], R2[:, 4096:6144])]
        KST = [v.bitcast(BF16).rearrange("p (j n) -> p j n", j=4)
               for v in (R4[:, 2048:4096], R2[:, 2048:4096], R2[:, 6144:8192])]
        VST = [R5[:, 1024 * n:1024 * n + 1024].rearrange("p (k j d) -> p k j d", k=TB, j=4) for n in range(3)]
        regn = R5[0:REG, 3072:4096].rearrange("p (b c) -> p b c", b=B)
        PR = W[:, 0:4096].rearrange("p (u j n) -> p u j n", u=2, j=4)
        XNf = XN[:, :, :, :].rearrange("p u i c -> p (u i c)")
        Oe2 = XNf[:, 0:1024].rearrange("p (u n) -> p u n", u=2)
        mro = XNf[0:16, 1024:1152].bitcast(BF16).rearrange("p (u n) -> p u n", u=2)
        crow = XNf[0:1, 0:2048].bitcast(BF16)
        Pn = W[:, 0:1024]
        PnT = W[:, 1024:2048].rearrange("p (k n) -> p k n", k=TB)
        Qbd = W[:, 2048:2560].rearrange("p (b j n) -> p b j n", b=B, j=2)
        omk = W[:, 2560:2816].rearrange("p (j n) -> p j n", j=2)
        rn2 = W[:, 2816:3328]
        dt2 = W[:, 3328:3840]
        sm2 = sb("sm2", [P, 1024])
        qgc = sm2[:, 0:2]
        qg2 = sm2[:, 2:4]
        qgn = sm2[:, 4:6]
        blk32 = sm2[:, 840:872]
        qgb = sm2[:, 872:936].rearrange("p (j g) -> p j g", j=2)
        sums = W[:, 3840:4352]
        BBm = sm2[:, 24:152]
        Rfull = sm2[:, 152:192].rearrange("p (g r) -> p g r", g=8)
        Rsel = sm2[:, 192:197]
        rmask = sm2[:, 200:208]
        regm = sm2[:, 208:240]
        QR = sm2[:, 240:280].rearrange("p (j b r) -> p j b r", j=2, b=B)
        simc = sm2[:, 280:312]
        cls = sm2[:, 312:440].rearrange("p (k i) -> p k i", k=4)
        tmp32 = sm2[:, 440:472]
        mm2 = sm2[:, 472:474]
        mmr = sm2[0:2, 474:475]
        mmd = sm2[0:2, 476:478]
        ones2 = sm2[0:2, 480:608]
        mmb = sm2[:, 608:610]
        rng = sm2[:, 610:611]
        rrg = sm2[:, 611:612]
        clsT = sm2[:, 612:676].bitcast(BF16)
        onesb = sm2[0:1, 676:708].bitcast(BF16)
        rmx = sm2[:, 708:712]
        rnm = sm2[:, 712:716]
        rden = sm2[:, 716:720]
        rrd = sm2[:, 720:724]
        MX = sm2[:, 728:760].rearrange("p (u q j) -> p u q j", u=2, q=4)
        rc2 = sm2[:, 792:808].rearrange("p (q j) -> p q j", q=4)
        simr = sm2[:, 808:840]
        s_wq3 = sem("wqkv_loaded")
        s_qgl = sem("q_g_loaded")
        s_qc = sem("q_g_chain")
        s_qk = sem("q_g_product")
        s_c2 = sem("class_constants")
        s_gb2 = sem("gated_bias2")
        s_xb2 = sem("bias2_added")
        s_qp = sem("qkv_product")
        s_qh = sem("q_part_h")
        s_qf = sem("q_copied")
        s_qs = sem("q_squared")
        s_qm = sem("q_part_m")
        s_kh = sem("k_part_h")
        s_km = sem("k_part_m")
        s_qr = sem("q_residue")
        s_krs = sem("k_residue")
        s_kf = sem("k_copied")
        s_vf = sem("v_copied")
        s_ql = sem("q_part_l")
        s_kl = sem("k_part_l")
        s_qw = sem("q_parts_written")
        s_kw2 = sem("k_parts_written")
        s_qrr = sem("register_queries_kept")
        s_sim = sem("sim_products")
        s_smc = sem("sim_products_copied")
        s_smt = sem("sim_products_transposed")
        s_smk = sem("sim_products_kept")
        s_sc2 = sem("sim_chain")
        s_rp = sem("norms_made")
        s_mmt = sem("extremes_transposed")
        s_mmb = sem("extremes_broadcast")
        s_clt = sem("classes_transposed")
        s_clw = sem("class_rows_written")
        s_clw2 = sem("register_key_row_written")
        s_crl = sem("register_key_row_loaded")
        s_rq = sem("register_scores")
        s_rm = sem("register_chain")
        s_rex = sem("register_probs")
        s_rpt = sem("register_probs_transposed")
        s_rpc = sem("register_probs_copied")
        s_rv = sem("register_values")
        s_rk = sem("register_masked")
        s_rsm = sem("register_summed")
        s_rgn = sem("register_kept")
        s_stk = [sem(f"stacks_loaded{n}") for n in range(3)]
        s_one = sem("max_row_factor_set")
        s_mrw = [sem(f"max_rows_in_dram{n}") for n in range(2)]
        s_row = [sem(f"max_rows_loaded{n}") for n in range(2)]
        s_turn = sem("turn_filled")
        s_tfree = sem("turn_free")
        s_sco = sem("scores2")
        s_sfree = sem("score_bank_free")
        s_pv2 = sem("values2_product")
        s_oe2 = sem("out2_copied")
        s_vst = sem("values_staged")
        s_vpre = sem("value_stage_preset")
        s_rc2 = sem("out2_recip")
        s_avg = sem("registers_averaged")
        s_out = sem("output_written")

        OnT2 = W[:, 0:2048].rearrange("p (u j n) -> p u j n", u=2, j=2)
        SIM_READ, CLS_DONE = 2, 23
        STACK2_DMAS = 14
        LEAD = 6
        PROLOGUE, left = [("register scores", 0)], list(range(32 - LEAD))

        def add_tiles(n):
            for a in left[:n]:
                PROLOGUE.append(("tile", a))
                if a == 15:
                    PROLOGUE.append(("rows", 0))
            del left[:n]

        add_tiles(2)
        for b in range(B):
            if b + 1 < B:
                PROLOGUE.append(("register scores", b + 1))
            add_tiles(2)
            PROLOGUE.append(("register transposes", b))
            add_tiles(2)
            PROLOGUE.append(("register values", b))
            add_tiles(1)
            PROLOGUE.append(("register sum", b))
            add_tiles(1)
        assert not left

        SHIFT = 2
        ORDER = [(n + SHIFT) % 16 for n in range(16)]
        PLAN = [[("tile", n)] for n in range(32)] + [[("out", 1)]]
        PLAN[1].append(("rows", 1))
        PLAN[19].append(("rows", 0))
        PLAN[18].append(("out", 0))
        PLAN_LAST = [[] for _ in range(32)] + [[("out", 1)]]
        PLAN_LAST[1].append(("rows", 1))
        PLAN_LAST[18].append(("out", 0))
        TURNS0 = 33
        TURNS = sum(len(x) for x in PLAN)
        flat, flat_last = sum(PLAN, []), sum(PLAN_LAST, [])
        ROWS1, ROWS0, ROWS1_LAST = flat.index(("rows", 1)), flat.index(("rows", 0)), flat_last.index(("rows", 1))

        def ln_chunk_buf(c):
            return XN[:, c % 2]

        @block.sync
        def _(sp):
            def load_x(b):
                sp.dma_start(X[:, TB * b:TB * b + TB, :],
                             ins["x"][b].rearrange("(i p) c -> p i c", p=P)).then_inc(s_x[b], 16)

            load_x(0)
            for dst, src in ((ctxT, ins["ctxT"]), (wk0, ins["wk0T"]), (wq0, ins["wq0"]), (wv0, ins["wv0T"])):
                sp.dma_start(dst, src.rearrange("(j p) n -> p j n", p=P)).then_inc(s_w0, 16)
            for b in range(1, B):
                load_x(b)
            for b in range(B):
                sp.dma_start(M0[:, b, :], ins["mask0T"][b]).then_inc(s_m0, 16)
            for i, n in enumerate(("g_xattn", "g_ffn")):
                sp.dma_start(graw[:, 2 * i:2 * i + 2],
                             ins[n].rearrange("(a n) -> a n", a=1).to_broadcast([P, 2])).then_inc(s_g, 16)
            sp.dma_start(wg, ins["w_gate"].rearrange("(j p) n -> p j n", p=P)).then_inc(s_wf, 16)
            sp.dma_start(ballT, ins["ballT"].rearrange("(j p) n -> p j n", p=P)).then_inc(s_wf, 16)
            sp.dma_start(wtT, ins["wtT"].rearrange("(j p) n -> p j n", p=P)).then_inc(s_wf, 16)
            sp.dma_start(wdT, ins["wdT"].rearrange("(j p) n -> p j n", p=P)).then_inc(s_wf, 16)
            sp.dma_start(AT[0:NB16, :], ins["AT"]).then_inc(s_wf, 16)
            sp.wait_ge(s_fc, 2)
            sp.dma_start(A1x[1:L, 0:NB16], ins["A1"][1:L, :]).then_inc(s_wf, 16)
            sp.dma_start(BWt[:, :, 96], ins["wt_b"].rearrange("(j p) -> p j", p=P),
                         allow_slow_non_contiguous=True).then_inc(s_wf, 16)
            sp.dma_start(BW[97:98, :], ins["wd_b"].rearrange("(a n) -> a n", a=1)).then_inc(s_wf, 16)
            sp.dma_start(fscale, ins["scale"].rearrange("(a n) -> a n", a=1).to_broadcast([P, 1])).then_inc(s_wf, 16)
            sp.dma_start(wo1[:, :, :], ins["wo1T"].rearrange("(j p) n -> p j n", p=P)).then_inc(s_w1, 16)
            sp.dma_start(wproj[:, :, :], ins["wproj"].rearrange("(j p) n -> p j n", p=P)).then_inc(s_w1, 16)
            sp.dma_start(bo1[:, :], ins["bo1"].rearrange("(a n) -> a n", a=1).to_broadcast([P, C])).then_inc(s_w1, 16)
            sp.dma_start(bp2[:, :], ins["bproj"].rearrange("(a n) -> a n", a=1).to_broadcast([P, C])).then_inc(s_w1, 16)
            for i, n in enumerate(("wv1T", "wk1T", "wq1")):
                for g in range(8):
                    sp.dma_start(w16[16 * g:16 * g + 16, i, :], ins[n]).then_inc(s_w1, 16)
            sp.wait_ge(s_kr, 5)
            sp.dma_start(KXP.rearrange("a (j p) n -> p a j n", p=P), kpart).then_inc(s_kw, 16)
            sp.wait_ge(s_kw, 16)
            sp.wait_ge(s_u, NC)
            sp.wait_ge(s_dl, NC)
            sp.dma_start(M1u, ins["mask1T"]).then_inc(s_m1, 16)
            for n, p in enumerate(K_ORDER):
                sp.dma_start(K1s[16 * n:16 * n + 16],
                             KXP[p].rearrange("(h d) n -> d h n", d=D)).then_inc(s_k1s, 16)

            def write_parts(c):
                sp.wait_ge(s_pl, 2 * c + 2)
                sp.dma_start(XP[:, :, 512 * c:512 * c + 512].rearrange("a (j p) n -> p a j n", p=P),
                             PB[:, c % 2]).then_inc(s_pw[c % 2], 16)

            def load_x_stack(u):
                b, hg = u // 4, u % 4
                if u >= 3:
                    sp.wait_ge(s_sc, 8 * (u - 2))
                for n, p in enumerate(Q_ORDER):
                    sp.dma_start(Xs[u % 3][16 * n:16 * n + 16],
                                 XP[p, 64 * hg:64 * hg + 64, S * b:S * b + S]
                                 .rearrange("(j d) t -> d j t", d=D)).then_inc(s_xs[u % 3], 16)

            write_parts(0)
            write_parts(1)
            for u in range(UNITS):
                b = u // 4
                if u % 4 == 0:
                    sp.wait_ge(s_pw[0], 16 * (b + 1))
                    sp.wait_ge(s_pw[1], 16 * (b + 1))
                load_x_stack(u)
                if u % 4 == 3 and b + 1 < B:
                    write_parts(2 * b + 2)
                    write_parts(2 * b + 3)
            sp.wait_ge(s_ksc, 6)
            sp.wait_ge(s_ks, 6)
            sp.dma_start(wqkv, ins["wqkv"].rearrange("(j p) n -> p j n", p=P)).then_inc(s_wq3, 16)
            sp.dma_start(qgc, ins["g_info"][0, 0].rearrange("(j p) -> p j", p=P),
                         allow_slow_non_contiguous=True).then_inc(s_qgl, 16)
            for c in range(NC):
                rows = slice(C * (c // 2), C * (c // 2) + C)
                t = slice(512 * (c % 2), 512 * (c % 2) + 512)
                sp.wait_ge(s_ql, c + 1)
                for a in range(3):
                    sp.dma_start(QP[a, rows, t].rearrange("(j p) n -> p j n", p=P), PB2[:, 0, a]).then_inc(s_qw, 16)
                sp.wait_ge(s_kl, c + 1)
                for a in range(3):
                    sp.dma_start(KP[a, rows, t].rearrange("(j p) n -> p j n", p=P), PB2[:, 1, a]).then_inc(s_kw2, 16)
            CRu = CR.rearrange("k b g t -> k (b g) t")

            def load_parts(u, j):
                for dst, parts, order in ((QST[j], QP, Q_ORDER), (KST[j], KP, K_ORDER)):
                    for n, a in enumerate(order):
                        src = parts[a].rearrange("(u j d) t -> u d j t", u=UNITS, d=D)
                        sp.dma_start(dst[16 * n:16 * n + 16], src[u]).then_inc(s_stk[j], 16)

            def load_class_rows(u, j):
                for dst, k in ((QST[j], 0), (KST[j], 2)):
                    sp.dma_start(dst[NEG_ROW:POS_ROW + 1],
                                 CRu[k:k + 2].rearrange("k u t -> u k t")[u].unsqueeze(1)
                                 .to_broadcast([2, 4, S])).then_inc(s_stk[j], 16)

            def load_stacks(u, j):
                load_parts(u, j)
                load_class_rows(u, j)

            sp.wait_ge(s_qw, 48 * NC)
            sp.wait_ge(s_kw2, 48 * NC)
            sp.wait_ge(s_sim, NC)
            load_parts(0, 0)
            sp.wait_ge(s_sc2, CLS_DONE)
            for k in (2, 0, 1, 3):
                for b in range(B):
                    row = TB * (B * k + b)
                    sp.dma_start(CR[k, b].rearrange("g (i n) -> i g n", n=P),
                                 clsT[row:row + TB].unsqueeze(1).to_broadcast([TB, 4, P])
                                 ).then_inc(s_clw if k != 2 else s_clw2, 16)
                if k == 2:
                    sp.wait_ge(s_clw2, 16 * B)
                    sp.dma_start(crow.rearrange("p (b t) -> p b t", b=B),
                                 CR[2, :, 0, :].unsqueeze(0)).then_inc(s_crl, 16)
            sp.wait_ge(s_clw, 16 * 3 * B)
            sp.wait_ge(s_one, 1)
            load_class_rows(0, 0)

            def store_row(j, half, filled, stored):
                sp.wait_ge(s_tfree, filled)
                sp.dma_start(MR[half], mro[:, half, :]).then_inc(s_mrw[half], 16)
                sp.wait_ge(s_mrw[half], 16 * stored + 16)
                sp.dma_start(QST[j][MAX_ROW:MAX_ROW + 1, :, 512 * half:512 * half + 512],
                             MR[half].rearrange("(h q) n -> h (q n)", h=4).unsqueeze(0)).then_inc(s_row[half], 16)

            store_row(0, 0, 2 + 17, 0)
            sp.wait_ge(s_rq, B)
            sp.wait_ge(s_one, 3)
            load_stacks(1, 1)
            load_stacks(2, 2)

            def body_sp(u, j, last=False, load=True):
                base = 2 + TURNS0 + TURNS * u + 1
                store_row(j, 1, base + (ROWS1_LAST if last else ROWS1), u)
                if not last:
                    store_row((j + 1) % 3, 0, base + ROWS0, u + 1)
                if load:
                    sp.wait_ge(s_pv2, 2 + 16 * (u + 1))
                    load_stacks(u + 3, j)

            with sp.Fori(0, 4) as i:
                for j in range(3):
                    body_sp(3 * i + j, j)
            body_sp(12, 0)
            body_sp(13, 1, load=False)
            body_sp(14, 2, load=False)
            body_sp(15, 0, last=True, load=False)
            for c in range(NC):
                sp.wait_ge(s_x3, NC + c + 1)
                sp.dma_start(out[c // 2].rearrange("(i p) c -> p i c", p=P)[:, 4 * (c % 2):4 * (c % 2) + 4, :],
                             X[:, 4 * c:4 * c + 4, :]).then_inc(s_out, 16)
            sp.wait_ge(s_out, 16 * NC)

        @block.gpsimd
        def _(pool):
            pool.memset(identF[:, :], 0.0).then_inc(s_const, 1)
            pool.memset(blk[:, :], 1.0).then_inc(s_const, 1)
            pool.memset(mhalf[:, :], -0.5).then_inc(s_const, 1)
            pool.memset(masked, 1e-9 * 16.0).then_inc(s_const, 1)
            pool.wait_ge(s_const, 4)
            pool.affine_select(out=identF[:, :], in_=identF[:, :], compare_op=ALU.not_equal, fill=1.0,
                               base=0, pattern=[[-1, P]], channel_multiplier=1).then_inc(s_const, 1)
            pool.wait_ge(s_const, 5)
            pool.tensor_copy(identB[:, :], identF[:, :]).then_inc(s_const, 1)
            pool.affine_select(out=blk[:, :], in_=blk[:, :], compare_op=ALU.is_ge, fill=0.0,
                               base=0, pattern=[[-16, 8]], channel_multiplier=1).then_inc(s_const, 1)
            pool.wait_ge(s_const, 7)
            pool.affine_select(out=blk[:, :], in_=blk[:, :], compare_op=ALU.is_ge, fill=0.0,
                               base=15, pattern=[[16, 8]], channel_multiplier=-1).then_inc(s_const, 1)

            def ln_rstd(k):
                for b in range(B):
                    v = slice(TB * b, TB * b + TB)
                    pool.wait_ge(s_ag, B * k + b + 1)
                    pool.tensor_scalar(rstd[:, v], mv[:, v, 1], LN_EPS, None, ALU.add).then_inc(s_rs, 1)
                    pool.wait_ge(s_rs, 2 * (B * k + b) + 1)
                    pool.tensor_tensor(rstd[:, v], rstd[:, v], mhalf[:, v], ALU.pow).then_inc(s_rs, 1)

            ln_rstd(0)
            pool.memset(A1x[0:L, :], 1.0).then_inc(s_fc, 1)
            pool.wait_ge(s_fc, 1)
            pool.memset(A1x[0:1, 0:97], 0.0).then_inc(s_fc, 1)
            for e in range(E):
                pool.memset(wtie[:, e:e + 1], float(E - e)).then_inc(s_fc, 1)

            ln_rstd(1)
            ln_rstd(2)
            pool.wait_ge(s_w1, 16 * 28)
            pool.wait_ge(s_gt, 1)
            pool.tensor_scalar(bo1[:, :], bo1[:, :], gates[:, 1:2], None, ALU.mult).then_inc(s_gb, 1)
            pool.wait_ge(s_gb, 1)

            for n in range(2 * NC):
                if n >= FIRST:
                    pool.wait_ge(s_pr, n + 1)
                    if n // 2 >= 2:
                        pool.wait_ge(s_pw[n // 2 % 2], 16 * (n // 4))
                    pool.wait_ge(s_pl, n)
                    pool.tensor_copy(PB[:, n // 2 % 2, 1, n % 2], xres[:, n // 2 % 2, n % 2]).then_inc(s_pm, 1)
                pool.wait_ge(s_pm, n + 1)
                pool.tensor_tensor(PB[:, n // 2 % 2, 2, n % 2], xres[:, n // 2 % 2, n % 2],
                                   PB[:, n // 2 % 2, 1, n % 2], ALU.subtract).then_inc(s_pl, 1)
            for b in range(B):
                pool.wait_ge(s_xn, NC * 2 + 2 * b + 2)
                xs = X[:, TB * b:TB * b + TB, :]
                pool.tensor_tensor(xs, xs, bo1[:, :].unsqueeze(1).to_broadcast([P, TB, C]), ALU.add).then_inc(s_xb, 1)

            pool.memset(Rfull, 0.0).then_inc(s_c2, 1)
            pool.memset(regm, 0.0).then_inc(s_c2, 1)
            pool.memset(ones2, 1.0).then_inc(s_c2, 1)
            pool.memset(onesb, 1.0).then_inc(s_c2, 1)
            pool.wait_ge(s_c2, 4)
            for q in range(2):
                v = Rfull[64 * q:64 * q + 64]
                pool.affine_select(out=v, in_=v, compare_op=ALU.not_equal, fill=1.0, base=0,
                                   pattern=[[-REG, 8], [-1, REG]], channel_multiplier=1).then_inc(s_c2, 1)
                pool.wait_ge(s_c2, 5 + q)
            for b in range(B):
                pool.memset(regm[0:REG, TB * b:TB * b + 1], 1.0).then_inc(s_c2, 1)
            ln_rstd(3)
            pool.wait_ge(s_qk, 1)
            pool.wait_ge(s_qc, 3)
            pool.tensor_tensor(qgn, qgn, mhalf[:, 0:2], ALU.pow).then_inc(s_qc, 1)
            pool.tensor_scalar(bp2[:, :], bp2[:, :], gates[:, 3:4], None, ALU.mult).then_inc(s_gb2, 1)
            for c in range(NC):
                pool.wait_ge(s_qm, c + 1)
                pool.tensor_tensor(PB2[:, 0, 2], res2[:, 0], PB2[:, 0, 1], ALU.subtract).then_inc(s_ql, 1)
                pool.wait_ge(s_km, c + 1)
                pool.tensor_tensor(PB2[:, 1, 2], res2[:, 1], PB2[:, 1, 1], ALU.subtract).then_inc(s_kl, 1)
            pool.wait_ge(s_kl, NC)
            pool.wait_ge(s_sim, NC)
            pool.memset(KST[0][NEG_ROW:MAX_ROW + 1], 1.0).then_inc(s_one, 1)
            pool.wait_ge(s_one, 1)
            pool.wait_ge(s_kw2, 48 * NC)
            pool.wait_ge(s_qw, 48 * NC)
            for j in range(3):
                pool.memset(VST[j], 0.0).then_inc(s_vpre, 1)
            pool.wait_ge(s_vpre, 3)
            for j in range(3):
                pool.memset(VST[j][:, :, :, D:D + 1], 1.0).then_inc(s_vpre, 1)
            pool.wait_ge(s_vf, NC)

            def stage_values(u, j):
                pool.tensor_copy(VST[j][:, :, :, 0:D].unsqueeze(1),
                                 V2[:, bass.ds(u, 1)].rearrange("p u k (j d) -> p u k j d", j=4)).then_inc(s_vst, 1)

            for j in range(3):
                stage_values(j, j)
            pool.wait_ge(s_vst, 3)
            pool.wait_ge(s_rq, B)
            for j in (1, 2):
                pool.wait_ge(s_one, j)
                pool.memset(KST[j][NEG_ROW:MAX_ROW + 1], 1.0).then_inc(s_one, 1)
            pool.wait_ge(s_one, 3)
            pool.wait_ge(s_gb2, 1)
            pool.wait_ge(s_xn, 4 * NC)
            for b in range(B):
                xs = X[:, TB * b:TB * b + TB, :]
                pool.tensor_tensor(xs, xs, bp2[:, :].unsqueeze(1).to_broadcast([P, TB, C]), ALU.add).then_inc(s_xb2, 1)
            with pool.Fori(0, 4) as i:
                for j in range(3):
                    pool.wait_ge(s_pv2, 2 + 16 * (3 * i + j + 1))
                    stage_values(3 * i + j + 3, j)
            pool.wait_ge(s_pv2, 2 + 16 * 13)
            stage_values(15, 0)

        @block.scalar
        def _(act):
            act.wait_ge(s_g, 32)
            act.activation(gates[:, :], graw, ACT.Tanh).then_inc(s_gt, 1)
            for n, (dst, i, rows, cols) in enumerate(
                    [(kT0[:, j, :], 4 + j, P, 308) for j in range(2)]
                    + [(KW0[:, j, :], 6 + j, P, 308) for j in range(2)]):
                act.wait_ge(s_ks, n + 1)
                act.copy(dst, bank(i)[0:rows, 0:cols]).then_inc(s_ksc, 1)
            for n in range(2):
                act.wait_ge(s_ks, 5 + n)
                act.copy(V0[:, 2 * n:2 * n + 2, :], bank(4 + n)[0:KX, :].rearrange("p (b n) -> p b n", b=2)).then_inc(s_ksc, 1)

            def ln_copy(k, then=lambda c: None):
                for c in range(NC):
                    act.wait_ge(s_tr, NC * k + c + 1)
                    act.copy(XNT[:, :, 512 * c:512 * c + 512],
                             bank(2 * (c % 2), 2).rearrange("p (j t) -> p j t", j=2)).then_inc(s_xt, 1)
                    then(c)

            ln_copy(0)
            for b in range(B):
                act.wait_ge(s_nb0, 3 * b + 3)
                act.activation(P0[:, b, :], bank(4 + 2 * (b % 2), 2)[0:KX, :], ACT.Exp, bias=nb0[:, b:b + 1],
                               scale=1.0 / 16, accum_out=den0[:, b:b + 1]).then_inc(s_e0, 1)

            for j in range(2):
                act.wait_ge(s_fs, j + 1)
                act.copy(BWt[:, j, 0:NB16], bank(4 + j)[:, 0:NB16]).then_inc(s_fsc, 1)
            act.wait_ge(s_fs, 3)
            act.copy(BW[0:97, :], bank(6)[0:97, 0:C]).then_inc(s_fsc, 1)
            def y_copy(c):
                act.wait_ge(s_y, c + 1)
                act.copy(yg[:, 512 * c:512 * c + 512], bank(5 + c % 2)[0:NB16 + E, :]).then_inc(s_yc, 1)

            ln_copy(1, lambda c: y_copy(c - 1) if c >= 1 else None)
            y_copy(NC - 1)
            act.wait_ge(s_k1, 1)
            act.copy(k1T, bank(0, 2).rearrange("p (j n) -> p j n", j=2)[:, :, 0:308]).then_inc(s_k1c, 1)
            act.wait_ge(s_k1, 2)
            act.copy(kpart[:, 0], bank(2, 2).rearrange("p (j n) -> p j n", j=2)[:, :, 0:308]).then_inc(s_k1c, 1)
            for c in range(NC):
                act.wait_ge(s_ot, c + 1)
                act.copy(OHT[:, 512 * c:512 * c + 512], bank(4 + c % 2)[0:98, :]).then_inc(s_otc, 1)
            for c in range(NC):
                v = attn[:, 4 * c:4 * c + 4, :]
                act.wait_ge(s_ad, c + 1)
                act.activation(v, v, ACT.Exp, scale=C ** -0.5).then_inc(s_ae, 1)
            for c in range(NC):
                act.wait_ge(s_at, c + 1)
                act.copy(aT[:, 512 * c:512 * c + 512], bank(6 + c % 2)[0:L, :]).then_inc(s_atc, 1)
            act.wait_ge(s_atc, NC)

            def log(c):
                v = comb[:, 4 * c:4 * c + 4, :]
                act.wait_ge(s_z2, c + 1)
                act.activation(v, v, ACT.Ln).then_inc(s_ln, 1)

            for c in range(NC):
                act.wait_ge(s_dl, c + 1)
                act.activation(comb[:, 4 * c:4 * c + 4, :],
                               bank(2 * (c % 2), 2).rearrange("p (i n) -> p i n", i=4), ACT.Exp,
                               scale=fscale).then_inc(s_de, 1)
                if c >= 1:
                    log(c - 1)
            log(NC - 1)

            def part_h(n, src):
                c = n // 2
                act.wait_ge(s_tr, NC * 2 + n + 1)
                if c >= 2:
                    act.wait_ge(s_pw[c % 2], 16 * (c // 2))
                act.copy(PB[:, c % 2, 0, n % 2], src).then_inc(s_ph, 1)

            def part_m(n):
                act.wait_ge(s_pr, n + 1)
                act.copy(PB[:, n // 2 % 2, 1, n % 2], xres[:, n // 2 % 2, n % 2]).then_inc(s_pm, 1)

            for n in range(FIRST):
                part_h(n, bank(n))
                if n >= 1:
                    part_m(n - 1)
            part_m(FIRST - 1)
            act.wait_ge(s_v1, 1)
            act.wait_ge(s_v1m, 2)
            for j in range(2):
                act.copy(V1a[:, :, 8 * j:8 * j + 8, 0:D],
                         bank(4 + j)[0:KX, :].rearrange("p (b h d) -> p b h d", b=B, h=8)).then_inc(s_v1c, 1)

            def max_rows1(m):
                act.wait_ge(s_mt, m + 1)
                if m >= 6:
                    act.wait_ge(s_sc, 4 * (m - 5))
                act.copy(Xs[m // 2 % 3][SR:SR1, :, 512 * (m % 2):512 * (m % 2) + 512],
                         bank(2)[SR:SR1, :].unsqueeze(1).to_broadcast([4, 4, 512])).then_inc(s_mrc, 1)

            max_rows1(0)
            max_rows1(1)
            for m in range(2 * UNITS):
                if half_in(m) is not None:
                    part_h(half_in(m), bank_of("half", half_in(m)))
                if m >= 2:
                    act.wait_ge(s_pv, m - 1)
                for j in range(4):
                    n = 4 * m + j
                    act.wait_ge(s_sc, n + 1)
                    act.activation(P1[:, m % 2, j, :], bank_of("score", n)[0:KX, :], ACT.Exp,
                                   scale=0.25).then_inc(s_e1, 1)
                if m + 2 < 2 * UNITS:
                    max_rows1(m + 2)

            for c in range(NC):
                act.wait_ge(s_onT, c + 1)
                if c >= 2:
                    act.wait_ge(s_wo, c - 1)
                act.copy(OnT[:, c % 2], bank(2 * (c % 2), 2).rearrange("p (j t) -> p j t", j=2)).then_inc(s_onc, 1)

            act.wait_ge(s_onT, NC)
            for c in range(NC):
                act.wait_ge(s_tr, NC * 4 + c + 1)
                act.copy(XNT[:, :, 512 * c:512 * c + 512],
                         bank(2 * (c % 2), 2).rearrange("p (j t) -> p j t", j=2)).then_inc(s_xt, 1)

            def copy_sums(c):
                act.wait_ge(s_sim, c + 1)
                if c >= 1:
                    act.wait_ge(s_smt, c)
                act.copy(sums, bank(0)).then_inc(s_smc, 1)

            for c in range(NC):
                q = bank(2, 2).rearrange("p (j t) -> p j t", j=2)
                act.wait_ge(s_qp, 3 * c + 1)
                if c >= 2:
                    act.wait_ge(s_sim, c - 1)
                    act.wait_ge(s_qrr, c // 2)
                act.copy(Qf[:, c % 2], q).then_inc(s_qf, 1)
                act.wait_ge(s_qf, c + 1)
                if c >= 1:
                    act.wait_ge(s_qw, 48 * c)
                act.copy(PB2[:, 0, 0], Qf[:, c % 2]).then_inc(s_qh, 1)
                act.activation(Qsq[:, c % 2], Qf[:, c % 2], ACT.Square).then_inc(s_qs, 1)
                act.wait_ge(s_qr, c + 1)
                act.copy(PB2[:, 0, 1], res2[:, 0]).then_inc(s_qm, 1)
                act.wait_ge(s_kf, c + 1)
                if c >= 1:
                    act.wait_ge(s_kw2, 48 * c)
                act.copy(PB2[:, 1, 0], KT[:, :, 512 * c:512 * c + 512]).then_inc(s_kh, 1)
                act.wait_ge(s_krs, c + 1)
                act.copy(PB2[:, 1, 1], res2[:, 1]).then_inc(s_km, 1)
                if c >= 1:
                    copy_sums(c - 1)
            copy_sums(NC - 1)
            act.wait_ge(s_smk, 2 * NC)
            act.activation(rn2, rn2, ACT.Sqrt).then_inc(s_rp, 1)
            for b in range(B):
                act.wait_ge(s_rm, 2 * b + 2)
                if b >= 1:
                    act.wait_ge(s_rpt, b)
                act.activation(Pn, bank(4, 2), ACT.Exp, bias=rnm[:, b:b + 1], scale=0.25,
                               accum_out=rden[:, b:b + 1]).then_inc(s_rex, 1)
                act.wait_ge(s_rpt, b + 1)
                if b >= 1:
                    act.wait_ge(s_rv, b)
                act.copy(PnT, bank(6, 2).rearrange("p (k n) -> p k n", k=TB)).then_inc(s_rpc, 1)
            act.wait_ge(s_rv, B)

            def exps(u, s, j):
                act.wait_ge(s_pv2, 16 * u + s + 1)
                for h in range(4):
                    n = 4 * s + h
                    act.wait_ge(s_sco, 64 * u + n + 1)
                    act.activation(PR[:, s % 2, h, :], bank(4 + (64 * j + n) % 3), ACT.Exp,
                                   scale=0.25).then_inc(s_sfree, 1)

            def copy_out2(u, half):
                act.wait_ge(s_pv2, 16 * u + 8 * half + 10)
                act.copy(Oe2[:, half, :], bank(7)).then_inc(s_oe2, 1)

            def body_act(u, j, last=False):
                for s in ORDER:
                    if s >= SHIFT:
                        exps(u, s, j)
                    elif not last:
                        exps(u + 1, s, (j + 1) % 3)
                    if s == 8:
                        copy_out2(u, 0)
                    if s == 0:
                        copy_out2(u, 1)

            act.sem_inc(s_sfree, 3)
            act.sem_inc(s_oe2, 1)
            for s in range(SHIFT):
                exps(0, s, 0)
            with act.Fori(0, 5) as i:
                for j in range(3):
                    body_act(3 * i + j, j)
            body_act(15, 0, last=True)
            for c in range(NC):
                n = NC + c
                act.wait_ge(s_onT, n + 1)
                if c >= 2:
                    act.wait_ge(s_wo, n - 1)
                act.copy(OnT2[:, c % 2], bank(2 * (c % 2), 2).rearrange("p (j t) -> p j t", j=2)).then_inc(s_onc, 1)

        @block.tensor
        def _(pe):
            def keep_warm(i, n):
                for _ in range(n):
                    pe.matmul(bank(i), identB[:, :], identB[:, :].unsqueeze(1).to_broadcast([P, 4, P]),
                              start=True, stop=True)

            pe.wait_ge(s_w0, 64)
            for j in range(2):
                for i in range(2):
                    mm = pe.matmul(bank(4 + j)[:, 0:308], wk0[:, i, P * j:P * j + P], ctxT[:, i, :],
                                   start=(i == 0), stop=(i == 1))
                mm.then_inc(s_ks, 1)
            pe.wait_ge(s_ksc, 2)
            for j in range(2):
                for i in range(2):
                    mm = pe.matmul(bank(6 + j)[:, 0:308], wq0[:, i, P * j:P * j + P], kT0[:, i, :],
                                   start=(i == 0), stop=(i == 1))
                mm.then_inc(s_ks, 1)
            for n in range(2):
                for b in (2 * n, 2 * n + 1):
                    for i in range(2):
                        mm = pe.matmul(bank(4 + n)[0:KX, C * (b % 2):C * (b % 2) + C],
                                       ctxT[:, i, KX * b:KX * b + KX], wv0[:, i, :],
                                       start=(i == 0 and b % 2 == 0), stop=(i == 1), skip_group_check=True)
                mm.then_inc(s_ks, 1)

            def ln_transposes(k, then=lambda c: None):
                pe.wait_ge(s_const, 8)
                for c in range(NC):
                    pe.wait_ge(s_xn, NC * k + c + 1)
                    if NC * k + c >= 2:
                        pe.wait_ge(s_xt, NC * k + c - 1)
                    for j in range(2):
                        for i in range(4):
                            mm = pe.transpose(bank(2 * (c % 2) + j)[:, P * i:P * i + P],
                                              ln_chunk_buf(c)[:, i, P * j:P * j + P], identF[:, :])
                    mm.then_inc(s_tr, 1)
                    then(c)

            def scores0(b):
                pe.wait_ge(s_xt, 2 * b + 2)
                if b < 2:
                    pe.wait_ge(s_ksc, 6)
                else:
                    pe.wait_ge(s_e0, b - 1)
                for q in range(2):
                    for i in range(2):
                        mm = pe.matmul(bank(4 + 2 * (b % 2) + q)[0:KX, :], KW0[:, i, KX * b:KX * b + KX],
                                       XNT[:, i, S * b + 512 * q:S * b + 512 * q + 512],
                                       start=(i == 0), stop=(i == 1))
                mm.then_inc(s_s0, 1)

            ln_transposes(0, lambda c: scores0(c // 2 - 1) if c in (3, 5) else None)
            for b in range(B):
                if 2 <= b + 1 < B:
                    scores0(b + 1)
                if b == 0:
                    pe.wait_ge(s_xt, NC)
                pe.wait_ge(s_v0, b + 1)
                for g in range(4):
                    n = 4 * b + g
                    if n >= 4:
                        pe.wait_ge(s_x1, n - 3)
                    for i in range(2):
                        q = P * (2 * g + i)
                        mm = pe.matmul(bank(g)[:, C * i:C * i + C], P0[:, b, q:q + P], V0s[:, b, :],
                                       start=(i == 0), stop=True, skip_group_check=True)
                    mm.then_inc(s_o0, 1)

            pe.wait_ge(s_wf, 16 * 9)
            pe.wait_ge(s_e0, B)
            for j in range(2):
                for i in range(2):
                    mm = pe.matmul(bank(4 + j)[:, 0:NB16], wtT[:, i, P * j:P * j + P], ballT[:, i, :],
                                   start=(i == 0), stop=(i == 1))
                mm.then_inc(s_fs, 1)
            pe.wait_ge(s_fsc, 2)
            for j in range(2):
                mm = pe.matmul(bank(6)[0:97, 0:C], BWt[:, j, :], wdT[:, j, :], start=(j == 0), stop=(j == 1))
            mm.then_inc(s_fs, 1)
            pe.wait_ge(s_x1, 4 * B)
            pe.wait_ge(s_fsc, 3)

            def y_and_gates(c):
                pe.wait_ge(s_xt, NC + c + 1)
                if c >= 2:
                    pe.wait_ge(s_yc, c - 1)
                for j in range(2):
                    mm = pe.matmul(bank(5 + c % 2)[0:NB16 + E, :], ballg[:, j, :], XNT[:, j, 512 * c:512 * c + 512],
                                   start=(j == 0), stop=(j == 1))
                mm.then_inc(s_y, 1)

            def gates_back(c):
                pe.wait_ge(s_yc, c + 1)
                for i in range(4 * c, 4 * c + 4):
                    mm = pe.matmul(bank(7)[:, E * i:E * i + E], yg[:, P * i:P * i + P],
                                   identF[0:NB16 + E, NB16:NB16 + E], start=(i == 0), stop=True,
                                   skip_group_check=True)
                mm.then_inc(s_gl, 1)

            def with_y(c):
                if c >= 1:
                    y_and_gates(c - 1)
                if c >= 2:
                    gates_back(c - 2)

            ln_transposes(1, with_y)
            y_and_gates(NC - 1)
            gates_back(NC - 2)
            gates_back(NC - 1)
            pe.wait_ge(s_bd, 3)
            pe.wait_ge(s_xt, 2 * NC)
            for j in range(2):
                mm = pe.matmul(bank(j)[:, 0:308], bd[:, 1, :], ctxT[:, j, :], start=True, stop=True)
            mm.then_inc(s_k1, 1)
            pe.wait_ge(s_k1c, 1)
            for j in range(2):
                mm = pe.matmul(bank(2 + j)[:, 0:308], bd[:, 2, :], k1T[:, j, :], start=True, stop=True)
            mm.then_inc(s_k1, 1)
            pe.wait_ge(s_gc, 7)
            for c in range(NC):
                if c >= 2:
                    pe.wait_ge(s_otc, c - 1)
                for i in range(4):
                    mm = pe.matmul(bank(4 + c % 2)[0:98, P * i:P * i + P], OH96[:, 4 * c + i, :], identB[:, :],
                                   start=True, stop=True)
                mm.then_inc(s_ot, 1)
            pe.wait_ge(s_otc, NC)
            for c in range(NC):
                pe.wait_ge(s_ys, c + 1)
                if c >= 2:
                    pe.wait_ge(s_ad, c - 1)
                for i in range(4):
                    t = 512 * c + P * i
                    mm = pe.matmul(bank(4 + c % 2)[:, L * i:L * i + L], ysel[:, t:t + P], AT[0:NB16, :],
                                   start=(i == 0), stop=True, skip_group_check=True)
                mm.then_inc(s_lg, 1)
            for c in range(NC):
                pe.wait_ge(s_an, c + 1)
                if c >= 2:
                    pe.wait_ge(s_atc, c - 1)
                for i in range(4):
                    mm = pe.transpose(bank(6 + c % 2)[0:L, P * i:P * i + P], attn[:, 4 * c + i, :], identF[:, :])
                mm.then_inc(s_at, 1)
            for c in range(NC):
                pe.wait_ge(s_atc, c + 1)
                if c >= 2:
                    pe.wait_ge(s_us, c - 1)
                else:
                    pe.wait_ge(s_ad, NC)
                pe.matmul(bank(4 + c % 2)[0:98, :], A1x[0:L, :], aT[:, 512 * c:512 * c + 512],
                          start=True, stop=True).then_inc(s_u, 1)
            pe.wait_ge(s_kr, 1)
            for c in range(NC):
                pe.wait_ge(s_us, c + 1)
                if c >= 2:
                    pe.wait_ge(s_de, c - 1)
                for i in range(4):
                    t = 512 * c + P * i
                    o = bank(2 * (c % 2) + i // 2)[:, C * (i % 2):C * (i % 2) + C]
                    pe.matmul(o, usel[:, t:t + P], BW[0:98, :], start=(i % 2 == 0), stop=False,
                              skip_group_check=True)
                    for j in range(2):
                        mm = pe.matmul(o, XNT[:, j, t:t + P], wdT[:, j, :], start=False, stop=(j == 1),
                                       skip_group_check=True)
                mm.then_inc(s_dl, 1)

            pe.wait_ge(s_us, NC)
            for j in range(2):
                for b in range(B):
                    mm = pe.matmul(bank(4 + j)[0:KX, P * b:P * b + P], ctxT[:, j, KX * b:KX * b + KX], bd[:, 0, :],
                                   start=(b == 0), stop=True, skip_group_check=True)
            mm.then_inc(s_v1, 1)
            pe.wait_ge(s_de, NC)

            def transpose_half(n, dst):
                pe.wait_ge(s_xn, NC * 2 + n // 2 + 1)
                for i in range(4):
                    mm = pe.transpose(dst[:, P * i:P * i + P],
                                      ln_chunk_buf(n // 2)[:, i, P * (n % 2):P * (n % 2) + P], identF[:, :])
                mm.then_inc(s_tr, 1)

            for n in range(FIRST):
                transpose_half(n, bank(n))
            pe.wait_ge(s_pr, FIRST)
            pe.wait_ge(s_k1s, 16 * STACK_DMAS)
            pe.wait_ge(s_mk1, 3)
            pe.wait_ge(s_v1c, 2)

            def max_product1(u, qs):
                b, hg = u // 4, u % 4
                pe.wait_ge(s_xs[u % 3], 16 * STACK_DMAS * (u // 3 + 1))
                for q in qs:
                    n = 8 * u + q
                    if n >= 2:
                        pe.wait_ge(s_mr, n - 1)
                    o = bank(n % 2)[:, 0:4 * KX]
                    pe.matmul(o, mb1[:, P * q:P * q + P], I4, start=True, stop=False, skip_group_check=True)
                    for j in range(4):
                        mm = pe.matmul(o[:, KX * j:KX * j + KX], Xs[u % 3][0:SR, j, P * q:P * q + P],
                                       K1s[0:SR, 4 * hg + j, KX * b:KX * b + KX], start=False, stop=True,
                                       skip_group_check=True)
                    mm.then_inc(s_mp, 1)

            def max_transposes1(m):
                pe.wait_ge(s_mn, m + 1)
                if m >= 1:
                    pe.wait_ge(s_mrc, m)
                for i in range(4):
                    mm = pe.matmul(bank(2)[SR:SR1, P * i:P * i + P], Mn[:, m // 2 % 2, 4 * (m % 2) + i, :],
                                   identF[:, :], start=True, stop=True)
                mm.then_inc(s_mt, 1)

            def take_bank(what, n):
                turn = TURNS1.index((what, n))
                if turn >= 3:
                    before, i = TURNS1[turn - 3]
                    pe.wait_ge(s_e1 if before == "score" else s_pr, i + 1)
                return bank_of(what, n)

            def scores1(m):
                u, q = m // 2, m % 2
                if half_in(m) is not None:
                    transpose_half(half_in(m), take_bank("half", half_in(m)))
                b, hg = u // 4, u % 4
                pe.wait_ge(s_mrc, m + 1)
                for j in range(4):
                    n = 4 * m + j
                    if u + 1 < UNITS:
                        max_product1(u + 1, (4 * q + j,))
                    o = take_bank("score", n)[0:KX, :]
                    t = slice(512 * q, 512 * q + 512)
                    pe.matmul(o, K1s[:, 4 * hg + j, KX * b:KX * b + KX], Xs[u % 3][:, j, t], start=True, stop=False)
                    pe.matmul(o, I4[:, 0:KX], mb1[:, t], start=False, stop=True).then_inc(s_sc, 1)

            def values1(m):
                u = m // 2
                pe.wait_ge(s_e1, 4 * m + 4)
                if m >= 1:
                    pe.wait_ge(s_oc, m)
                for j in range(4):
                    mm = pe.matmul(bank(7)[32 * j:32 * j + 32, :], V1a[:, u // 4, 4 * (u % 4) + j, :],
                                   P1[:, m % 2, j, :], start=True, stop=True)
                mm.then_inc(s_pv, 1)

            def out_transposes1(m):
                pe.wait_ge(s_oc, m + 1)
                if m >= 1:
                    pe.wait_ge(s_on, m)
                for i in range(4):
                    mm = pe.transpose(bank(3)[:, P * i:P * i + P], Oe[:, m % 2, P * i:P * i + P], identF[:, :])
                mm.then_inc(s_ot1, 1)

            for q in range(2):
                max_product1(0, range(4 * q, 4 * q + 4))
                max_transposes1(q)
            keep_warm(4, 16)
            for m in range(2 * UNITS):
                scores1(m)
                if m >= 1:
                    values1(m - 1)
                if m >= 2:
                    out_transposes1(m - 2)
                if m + 2 < 2 * UNITS:
                    max_transposes1(m + 2)
            values1(2 * UNITS - 1)
            out_transposes1(2 * UNITS - 2)
            out_transposes1(2 * UNITS - 1)

            def transposes1(c):
                if c >= 2:
                    pe.wait_ge(s_onc, c - 1)
                for j in range(2):
                    for i in range(4):
                        mm = pe.transpose(bank(2 * (c % 2) + j)[:, P * i:P * i + P],
                                          On[:, 4 * c + i, P * j:P * j + P], identF[:, :])
                mm.then_inc(s_onT, 1)

            pe.wait_ge(s_on, 2 * UNITS)
            transposes1(0)
            for c in range(NC):
                if c + 1 < NC:
                    transposes1(c + 1)
                pe.wait_ge(s_onc, c + 1)
                if c >= 2:
                    pe.wait_ge(s_x3, c - 1)
                for i in range(4):
                    o = bank(4 + 2 * (c % 2) + i // 2)[:, C * (i % 2):C * (i % 2) + C]
                    for j in range(2):
                        mm = pe.matmul(o, OnT[:, c % 2, j, P * i:P * i + P], wo1[:, j, :],
                                       start=(i % 2 == 0 and j == 0), stop=(j == 1), skip_group_check=True)
                mm.then_inc(s_wo, 1)

            pe.wait_ge(s_qc, 2)
            pe.wait_ge(s_x3, NC)
            pe.matmul(bank(6)[:, 0:2], BBm, qg2, start=True, stop=True).then_inc(s_qk, 1)
            pe.wait_ge(s_onc, NC)
            for c in range(NC):
                pe.wait_ge(s_xn, NC * 3 + c + 1)
                if c >= 2:
                    pe.wait_ge(s_xt, NC * 2 + c - 1)
                for j in range(2):
                    for i in range(4):
                        mm = pe.transpose(bank(2 * (c % 2) + j)[:, P * i:P * i + P],
                                          ln_chunk_buf(c)[:, i, P * j:P * j + P], identF[:, :])
                mm.then_inc(s_tr, 1)
            pe.wait_ge(s_xt, 3 * NC)
            pe.wait_ge(s_wq3, 16)
            pe.wait_ge(s_qc, 7)

            def sim_products(c):
                pe.wait_ge(s_qs, c + 1)
                if c >= 1:
                    pe.wait_ge(s_smc, c)
                for j in range(2):
                    pe.matmul(bank(0)[32 * j:32 * j + 32, :], blk32, Qsq[:, c % 2, j, :], start=True, stop=True)
                for j in range(2):
                    mm = pe.matmul(bank(0)[64 + 32 * j:96 + 32 * j, :], qgb[:, j, :], Qf[:, c % 2, j, :],
                                   start=True, stop=True)
                mm.then_inc(s_sim, 1)

            def sim_transposes(c):
                pe.wait_ge(s_smc, c + 1)
                if c >= 1:
                    pe.wait_ge(s_smk, 2 * c)
                for i in range(4):
                    mm = pe.transpose(bank(1)[:, P * i:P * i + P], sums[:, P * i:P * i + P], identF[:, :])
                mm.then_inc(s_smt, 1)

            for c in range(NC):
                t = slice(512 * c, 512 * c + 512)
                for kind in range(2):
                    if c >= 1:
                        if kind == 0:
                            pe.wait_ge(s_qf, c)
                        else:
                            pe.wait_ge(s_kf, c)
                    for j in range(2):
                        for i in range(2):
                            mm = pe.matmul(bank(2 + 2 * kind + j), wqkv[:, i, C * kind + P * j:C * kind + P * j + P],
                                           XNT[:, i, t], start=(i == 0), stop=(i == 1))
                    mm.then_inc(s_qp, 1)
                if c >= 1:
                    pe.wait_ge(s_vf, c)
                for i in range(4):
                    for j in range(2):
                        mm = pe.matmul(bank(6 + i // 2)[:, C * (i % 2):C * (i % 2) + C],
                                       XNT[:, j, 512 * c + P * i:512 * c + P * i + P], wqkv[:, j, 2 * C:3 * C],
                                       start=(i % 2 == 0 and j == 0), stop=(j == 1), skip_group_check=True)
                mm.then_inc(s_qp, 1)
                if c >= 2:
                    sim_transposes(c - 2)
                if c >= 1:
                    sim_products(c - 1)
            sim_transposes(NC - 2)
            sim_products(NC - 1)
            sim_transposes(NC - 1)
            pe.wait_ge(s_sc2, 9)
            pe.transpose(bank(2)[0:2, 0:P], mm2, identF[:, :]).then_inc(s_mmt, 1)
            pe.wait_ge(s_sc2, 11)
            pe.matmul(bank(3)[:, 0:2], ones2, mmd, start=True, stop=True).then_inc(s_mmb, 1)
            pe.wait_ge(s_sc2, CLS_DONE - 1)
            pe.transpose(bank(2)[:, 0:P], cls.rearrange("p k i -> p (k i)"), identF[:, :]).then_inc(s_clt, 1)
            pe.wait_ge(s_sc2, CLS_DONE)
            pe.wait_ge(s_crl, 16)

            def register_scores(b):
                if b >= 1:
                    pe.wait_ge(s_rex, b)
                for q in range(2):
                    t = slice(S * b + 512 * q, S * b + 512 * q + 512)
                    for j in range(2):
                        o = bank(4 + q)[64 * j:64 * j + 64, :]
                        pe.matmul(o, Qbd[:, b, j, :], KT[:, j, t], start=True, stop=False)
                        mm = pe.matmul(o, onesb, crow[:, t], start=False, stop=True)
                mm.then_inc(s_rq, 1)

            def register_transposes(b):
                pe.wait_ge(s_rex, b + 1)
                if b >= 1:
                    pe.wait_ge(s_rgn, b)
                for k in range(TB):
                    mm = pe.transpose(bank(6 + k // 4)[:, P * (k % 4):P * (k % 4) + P], Pn[:, P * k:P * k + P],
                                      identF[:, :])
                mm.then_inc(s_rpt, 1)

            def register_values(b):
                pe.wait_ge(s_rpc, b + 1)
                for j in range(2):
                    for k in range(TB):
                        mm = pe.matmul(bank(6)[64 * j:64 * j + 64, 0:P], PnT[:, k, 64 * j:64 * j + 64],
                                       V2[:, 4 * b + 2 * j:4 * b + 2 * j + 2, k, :],
                                       start=(k == 0), stop=(k == TB - 1))
                mm.then_inc(s_rv, 1)

            def register_sum(b):
                pe.wait_ge(s_rk, 2 * b + 2)
                pe.matmul(bank(7)[0:REG, 0:C], Rsel, omk.rearrange("p j n -> p (j n)"),
                          start=True, stop=True).then_inc(s_rsm, 1)

            def take_turn(n, k):
                pe.wait_ge(s_tfree, n + 1)
                return bank(2 * (k % 2), 2)

            def max_tile(n, k, a, j):
                pl = take_turn(n, k)
                q, h = a // 4, a % 4
                for i in range(2):
                    mm = pe.matmul(pl[:, 512 * i:512 * i + 512], QST[j][0:MAX_ROW, h, P * q:P * q + P],
                                   KST[j][0:MAX_ROW, h, 512 * i:512 * i + 512], start=True, stop=True)
                mm.then_inc(s_turn, 1)

            def max_rows(n, k, half):
                pl = take_turn(n, k)
                pe.transpose(pl[0:16, 0:P], MX[:, half].rearrange("p j q -> p (j q)"), identF[:, :]).then_inc(s_turn, 1)

            def out_turn(n, k, half, seen):
                pl = take_turn(n, k)
                pe.wait_ge(s_oe2, seen)
                for i in range(4):
                    mm = pe.transpose(pl[:, P * i:P * i + P], Oe2[:, half, P * i:P * i + P], identF[:, :])
                mm.then_inc(s_turn, 1)

            def values2(u, s, j):
                half, k = s // 8, s % 8
                pe.wait_ge(s_sfree, 3 + 64 * u + 4 * s + 4)
                if k == 0:
                    pe.wait_ge(s_oe2, 2 * u + half + 1)
                for h in range(4):
                    mm = pe.matmul(bank(7)[32 * h:32 * h + 32, :], VST[j][:, k, h, :], PR[:, s % 2, h, :],
                                   start=(k == 0), stop=(k == TB - 1))
                mm.then_inc(s_pv2, 1)

            def scores2(u, s, h, j):
                n = 4 * s + h
                pe.wait_ge(s_sfree, 64 * u + n + 1)
                pe.matmul(bank(4 + (64 * j + n) % 3), KST[j][0:MAX_ROW + 1, h, P * (s % 8):P * (s % 8) + P],
                          QST[j][0:MAX_ROW + 1, h, 512 * (s // 8):512 * (s // 8) + 512],
                          start=True, stop=True).then_inc(s_sco, 1)

            def body_pe(u, j, loads, last=False):
                base = TURNS0 + TURNS * u
                jn = (j + 1) % 3
                k = 0

                def turns(entries, k):
                    for what, arg in entries:
                        if what == "tile":
                            max_tile(base + k, k, arg, jn)
                        elif what == "rows":
                            max_rows(base + k, k, arg)
                        else:
                            out_turn(base + k, k, arg, 2 * u + 2 + arg)
                        k += 1
                    return k

                if not last:
                    pe.wait_ge(s_stk[jn], 16 * STACK2_DMAS * loads)
                for n, s in enumerate(ORDER):
                    us, js = (u, j) if s >= SHIFT else (u + 1, jn)
                    if s < SHIFT and last:
                        break
                    if s == 8:
                        pe.wait_ge(s_row[1], 16 * (u + 1))
                    if s == 0:
                        pe.wait_ge(s_row[0], 16 * (u + 2))
                    for h in range(4):
                        scores2(us, s, h, js)
                        if h % 2 == 1:
                            k = turns((PLAN_LAST if last else PLAN)[2 * n + h // 2], k)
                    if s == 0:
                        values2(u, 15, j)
                    else:
                        if s == 1:
                            pe.wait_ge(s_vst, u + 2)
                        values2(us, s - 1, js)
                if last:
                    values2(u, 15, j)
                turns((PLAN_LAST if last else PLAN)[32], k)

            pe.sem_inc(s_pv2, 2)
            pe.wait_ge(s_qrr, B + 3)
            n = 0
            for what, arg in PROLOGUE:
                if what == "register scores":
                    register_scores(arg)
                elif what == "register transposes":
                    register_transposes(arg)
                elif what == "register values":
                    register_values(arg)
                elif what == "register sum":
                    register_sum(arg)
                else:
                    if n == 0:
                        pe.wait_ge(s_stk[0], 16 * STACK2_DMAS)
                    if what == "tile":
                        max_tile(n, n + 1, arg, 0)
                    else:
                        pe.wait_ge(s_tfree, n + 2)
                        max_rows(n, n + 1, arg)
                    n += 1
            pe.wait_ge(s_row[0], 16)
            pe.wait_ge(s_rgn, B)
            for i in range(4 * SHIFT):
                scores2(0, i // 4, i % 4, 0)
                if i < LEAD:
                    max_tile(n + i, n + i + 1, 32 - LEAD + i, 0)
            pe.wait_ge(s_vst, 1)
            for s in range(SHIFT - 1):
                values2(0, s, 0)
            pe.wait_ge(s_one, 3)
            with pe.Fori(0, 5) as i:
                for j in range(3):
                    body_pe(3 * i + j, j, i + 1 if j < 2 else i + 2)
            body_pe(15, 0, 0, last=True)

            pe.wait_ge(s_avg, 1)

            def transposes2(c):
                n = NC + c
                if c >= 2:
                    pe.wait_ge(s_onc, n - 1)
                for j in range(2):
                    for i in range(4):
                        b, t = c // 2, 4 * (c % 2) + i
                        mm = pe.transpose(bank(2 * (c % 2) + j)[:, P * i:P * i + P],
                                          On2[:, t, C * b + P * j:C * b + P * j + P], identF[:, :])
                mm.then_inc(s_onT, 1)

            transposes2(0)
            for c in range(NC):
                n = NC + c
                if c + 1 < NC:
                    transposes2(c + 1)
                pe.wait_ge(s_onc, n + 1)
                if c >= 2:
                    pe.wait_ge(s_x3, n - 1)
                for i in range(4):
                    o = bank(4 + 2 * (c % 2) + i // 2)[:, C * (i % 2):C * (i % 2) + C]
                    for j in range(2):
                        mm = pe.matmul(o, OnT2[:, c % 2, j, P * i:P * i + P], wproj[:, j, :],
                                       start=(i % 2 == 0 and j == 0), stop=(j == 1), skip_group_check=True)
                mm.then_inc(s_wo, 1)

        @block.vector
        def _(dve):
            def ln_stats(k, before):
                for b in range(B):
                    before(b)
                    for i in range(TB * b, TB * b + TB):
                        dve.bn_stats(stats[:, i, :], X[:, i, :]).then_inc(s_st, 1)
                    for i in range(TB * b, TB * b + TB):
                        dve.wait_ge(s_st, NT * k + i + 1)
                        ins_ = dve.bn_aggr(mv[:, i, :], stats[:, i, :])
                    ins_.then_inc(s_ag, 1)
                    if k == 0 and b >= 1:
                        ln_chunks(k, range(2 * b - 2, 2 * b), lambda c: None)
                    if k >= 1 and b == 2:
                        ln_chunks(k, range(2), lambda c: None)

            def ln_chunks(k, chunks, then):
                for c in chunks:
                    dve.wait_ge(s_rs, 2 * (B * k + c // 2) + 2)
                    if NC * k + c >= 2:
                        before = (0, NC, 2 * NC, 4 * NC)[k]
                        dve.wait_ge(s_tr, before + (2 * (c - 1) if k == 2 and c >= 2 else c - 1))
                    if k == 1 and c >= 2:
                        dve.wait_ge(s_xg, c - 1)
                    for i in range(4):
                        ins_ = dve.tensor_scalar(ln_chunk_buf(c)[:, i, :], X[:, 4 * c + i, :],
                                                 mv[:, 4 * c + i, 0:1], rstd[:, 4 * c + i:4 * c + i + 1],
                                                 ALU.subtract, ALU.mult)
                    ins_.then_inc(s_xn, 1)
                    then(c)

            ln_stats(0, lambda b: dve.wait_ge(s_x[b], 16))
            ln_chunks(0, range(NC - 2, NC), lambda c: None)
            dve.wait_ge(s_const, 8)
            dve.wait_ge(s_m0, 64)
            dve.wait_ge(s_gt, 1)
            def maximum0(b):
                sc = bank(4 + 2 * (b % 2), 2)[0:KX, :]
                dve.wait_ge(s_s0, b + 1)
                dve.copy_predicated(sc, M0[:, b, :], masked.to_broadcast([KX, S])).then_inc(s_nb0, 1)
                dve.wait_ge(s_nb0, 3 * b + 1)
                dve.tensor_reduce(mx0[:, b:b + 1], sc, AX, ALU.max).then_inc(s_nb0, 1)
                dve.wait_ge(s_nb0, 3 * b + 2)
                dve.tensor_scalar(nb0[:, b:b + 1], mx0[:, b:b + 1], -1.0 / 16, None, ALU.mult).then_inc(s_nb0, 1)

            def scale_values0(b):
                dve.wait_ge(s_e0, b + 1)
                dve.reciprocal(rd0[:, b:b + 1], den0[:, b:b + 1]).then_inc(s_rd0, 1)
                dve.wait_ge(s_rd0, b + 1)
                dve.tensor_scalar(V0s[:, b, :], V0[:, b, :], rd0[:, b:b + 1], gates[0:KX, 0:1],
                                  ALU.mult, ALU.mult).then_inc(s_v0, 1)

            def xattn0_batch(b):
                if b == 0:
                    maximum0(0)
                    scale_values0(0)
                if b + 1 < B:
                    maximum0(b + 1)
                for g in range(4):
                    dve.wait_ge(s_o0, 4 * b + g + 1)
                    xs = X[:, TB * b + 2 * g:TB * b + 2 * g + 2, :]
                    dve.tensor_tensor(xs, bank(g).rearrange("p (i c) -> p i c", i=2), xs, ALU.add).then_inc(s_x1, 1)
                if b + 1 < B:
                    scale_values0(b + 1)
                dve.wait_ge(s_x1, 4 * b + 4)

            def gated_ln(c):
                dve.wait_ge(s_xn, NC + c + 1)
                xs = X[:, 4 * c:4 * c + 4, :]
                dve.scalar_tensor_tensor(xs, ln_chunk_buf(c), gates[:, 2:3], xs, ALU.mult, ALU.add).then_inc(s_xg, 1)

            ln_stats(1, xattn0_batch)
            for c in range(2):
                gated_ln(c)
            ln_chunks(1, range(2, NC), gated_ln)
            dve.wait_ge(s_w1, 16 * 28)
            for i in range(3):
                dve.tensor_tensor(bd[:, i, :].rearrange("p (g d) -> p g d", g=8),
                                  w16[:, i, :].unsqueeze(1).to_broadcast([P, 8, 16]),
                                  blk[:, :].unsqueeze(2).to_broadcast([P, 8, 16]), ALU.mult).then_inc(s_bd, 1)

            G = bank(7)[:, 0:E * NT].rearrange("p (i e) -> p i e", e=E)
            dve.wait_ge(s_fc, 2 + E)
            dve.wait_ge(s_gl, NC)
            dve.tensor_reduce(gmx, G, AX, ALU.max).then_inc(s_gc, 1)
            dve.wait_ge(s_gc, 1)
            dve.tensor_tensor(eq6, G, gmx.unsqueeze(2).to_broadcast([P, NT, E]), ALU.is_equal).then_inc(s_gc, 1)
            dve.wait_ge(s_gc, 2)
            dve.tensor_tensor(eq6, eq6, wtie.unsqueeze(1).to_broadcast([P, NT, E]), ALU.mult).then_inc(s_gc, 1)
            dve.wait_ge(s_gc, 3)
            dve.tensor_reduce(gm2, eq6, AX, ALU.max).then_inc(s_gc, 1)
            dve.wait_ge(s_gc, 4)
            dve.tensor_tensor(eq6, eq6, gm2.unsqueeze(2).to_broadcast([P, NT, E]), ALU.is_equal).then_inc(s_gc, 1)
            dve.wait_ge(s_gc, 5)
            dve.tensor_copy(OH96[:, :, 0:NB16].rearrange("p i (e r) -> p i e r", e=E),
                            eq6.unsqueeze(3).to_broadcast([P, NT, E, R])).then_inc(s_gc, 1)
            dve.memset(OH96[:, :, NB16:98], 1.0).then_inc(s_gc, 1)
            for c in range(NC):
                dve.wait_ge(s_otc, c + 1)
                v = slice(512 * c, 512 * c + 512)
                dve.tensor_tensor(ysel[:, v], ysel[:, v], OHT[0:NB16, v], ALU.mult).then_inc(s_ys, 1)

            dve.wait_ge(s_k1c, 2)
            dve.tensor_tensor(kr1, bank(2, 2).rearrange("p (j n) -> p j n", j=2)[:, :, 0:308], kpart[:, 0],
                              ALU.subtract).then_inc(s_kr, 1)
            dve.wait_ge(s_kr, 1)
            dve.tensor_copy(kpart[:, 1], kr1).then_inc(s_kr, 1)
            dve.wait_ge(s_kr, 2)
            dve.tensor_tensor(kr1, kr1, kpart[:, 1], ALU.subtract).then_inc(s_kr, 1)
            dve.wait_ge(s_kr, 3)
            dve.tensor_copy(kpart[:, 2], kr1).then_inc(s_kr, 2)

            def attn_norm(c):
                v = slice(4 * c, 4 * c + 4)
                dve.wait_ge(s_ae, c + 1)
                dve.tensor_reduce(asum[:, v, :], attn[:, v, :], AX, ALU.add).then_inc(s_as, 1)
                dve.wait_ge(s_as, c + 1)
                dve.reciprocal(arec[:, v, :], asum[:, v, :]).then_inc(s_ar, 1)
                dve.wait_ge(s_ar, c + 1)
                dve.tensor_tensor(attn[:, v, :], attn[:, v, :], arec[:, v, :].to_broadcast([P, 4, L]),
                                  ALU.mult).then_inc(s_an, 1)

            for c in range(NC):
                v = slice(4 * c, 4 * c + 4)
                lg = bank(4 + c % 2)[:, 0:4 * L].rearrange("p (i l) -> p i l", i=4)
                dve.wait_ge(s_lg, c + 1)
                dve.tensor_reduce(amx[:, v, :], lg, AX, ALU.max).then_inc(s_am, 1)
                dve.wait_ge(s_am, c + 1)
                dve.tensor_tensor(attn[:, v, :], lg, amx[:, v, :].to_broadcast([P, 4, L]),
                                  ALU.subtract).then_inc(s_ad, 1)
                if c >= 1:
                    attn_norm(c - 1)
            attn_norm(NC - 1)
            for c in range(NC):
                v = slice(512 * c, 512 * c + 512)
                dve.wait_ge(s_u, c + 1)
                dve.tensor_tensor(usel[:, v], bank(4 + c % 2)[0:98, :], OHT[:, v], ALU.mult).then_inc(s_us, 1)
            def replace_zeros(c):
                v = comb[:, 4 * c:4 * c + 4, :]
                z = zfix[:, c % 2].rearrange("p (i n) -> p i n", i=4)
                dve.wait_ge(s_de, c + 1)
                if c >= 2:
                    dve.wait_ge(s_z2, c - 1)
                dve.tensor_scalar(z, v, 0.0, TINY, ALU.is_equal, ALU.mult).then_inc(s_z1, 1)
                dve.wait_ge(s_z1, c + 1)
                dve.tensor_tensor(v, v, z, ALU.add).then_inc(s_z2, 1)

            def add_log(c):
                xs = X[:, 4 * c:4 * c + 4, :]
                dve.wait_ge(s_ln, c + 1)
                dve.scalar_tensor_tensor(xs, comb[:, 4 * c:4 * c + 4, :], gates[:, 2:3], xs,
                                         ALU.mult, ALU.add).then_inc(s_x2, 1)

            def x2_batch(b):
                for c in (2 * b, 2 * b + 1):
                    if c == 0:
                        replace_zeros(0)
                    if c + 1 < NC:
                        replace_zeros(c + 1)
                    add_log(c)
                dve.wait_ge(s_x2, 2 * b + 2)

            ln_stats(2, x2_batch)
            def residue(n, src):
                c = n // 2
                dve.wait_ge(s_ph, n + 1)
                if c >= 2:
                    dve.wait_ge(s_pl, n - 3)
                dve.tensor_tensor(xres[:, c % 2, n % 2], src, PB[:, c % 2, 0, n % 2],
                                  ALU.subtract).then_inc(s_pr, 1)

            for n in range(FIRST):
                residue(n, bank(n))
            dve.wait_ge(s_dl, NC)
            dve.memset(V1a, 0.0).then_inc(s_v1m, 1)
            dve.wait_ge(s_v1m, 1)
            dve.memset(V1a[:, :, :, D:D + 1], 1.0).then_inc(s_v1m, 1)
            dve.wait_ge(s_m1, 16)
            dve.tensor_scalar(mb1, M1u, -1.0, BIG, ALU.add, ALU.mult).then_inc(s_mk1, 1)
            dve.tensor_copy(I4.rearrange("p (j n) -> p j n", j=4),
                            identB[0:KX, 0:KX].unsqueeze(1).to_broadcast([KX, 4, KX])).then_inc(s_mk1, 1)
            for g in range(4):
                sel = dve.tensor_copy(K1s[SR:SR1, 4 * g:4 * g + 4, :],
                                      identB[SR:SR1, SR:SR1].unsqueeze(2).to_broadcast([4, 4, B * KX]))
            sel.then_inc(s_mk1, 1)
            ln_chunks(2, [2], lambda c: None)

            def reduce1(u, qs):
                for q in qs:
                    n = 8 * u + q
                    dve.wait_ge(s_mp, n + 1)
                    dve.tensor_reduce(M1[:, u % 2, q, :],
                                      bank(n % 2)[:, 0:4 * KX].rearrange("p (j n) -> p j n", j=4), AX,
                                      ALU.max).then_inc(s_mr, 1)

            def maxima1(m, between=lambda: None):
                u, v = m // 2, slice(4 * (m % 2), 4 * (m % 2) + 4)
                reduce1(u, range(v.start, v.start + 2))
                between()
                reduce1(u, range(v.start + 2, v.stop))
                if m >= 4:
                    dve.wait_ge(s_mt, m - 3)
                dve.wait_ge(s_mr, 4 * m + 4)
                dve.tensor_scalar(Mn[:, u % 2, v], M1[:, u % 2, v], -1.0, None, ALU.mult).then_inc(s_mn, 1)

            def normalise1(m):
                u, q = m // 2, m % 2
                b, hg = u // 4, u % 4
                O = bank(3).rearrange("p (q j d) -> p q j d", q=4, j=4)
                dve.wait_ge(s_ot1, m + 1)
                if m >= 1:
                    dve.wait_ge(s_on, m)
                dve.reciprocal(rc1, O[:, :, :, D]).then_inc(s_rc, 1)
                dve.wait_ge(s_rc, m + 1)
                dst = On[:, TB * b + 4 * q:TB * b + 4 * q + 4, 64 * hg:64 * hg + 64]
                dve.tensor_tensor(dst.rearrange("p q (j d) -> p q j d", j=4), O[:, :, :, 0:D],
                                  rc1.unsqueeze(3).to_broadcast([P, 4, 4, D]), ALU.mult).then_inc(s_on, 1)

            def copy_out1(m):
                dve.wait_ge(s_pv, m + 1)
                if m >= 2:
                    dve.wait_ge(s_ot1, m - 1)
                dve.tensor_copy(Oe[:, m % 2], bank(7)).then_inc(s_oc, 1)

            maxima1(0)
            maxima1(1)
            for m in range(2 * UNITS):
                n = half_in(m)
                if m + 2 < 2 * UNITS:
                    maxima1(m + 2, lambda: residue(n, bank_of("half", n)) if n is not None else None)
                if m >= 1:
                    copy_out1(m - 1)
                c = 2 * (m // 8) + {0: 3, 6: 4}.get(m % 8, NC)
                if c < NC:
                    ln_chunks(2, [c], lambda c: None)
                if m >= 2:
                    normalise1(m - 2)
            copy_out1(2 * UNITS - 1)
            normalise1(2 * UNITS - 2)
            normalise1(2 * UNITS - 1)

            def x3_batch(b):
                for c in (2 * b, 2 * b + 1):
                    dve.wait_ge(s_wo, c + 1)
                    dve.wait_ge(s_xb, b + 1)
                    xs = X[:, 4 * c:4 * c + 4, :]
                    dve.scalar_tensor_tensor(xs, bank(4 + 2 * (c % 2), 2).rearrange("p (i n) -> p i n", i=4),
                                             gates[:, 1:2], xs, ALU.mult, ALU.add).then_inc(s_x3, 1)
                dve.wait_ge(s_x3, 2 * b + 2)

            ln_stats(3, x3_batch)
            dve.memset(blk32, 0.0).then_inc(s_bd, 1)
            dve.wait_ge(s_bd, 4)
            dve.tensor_copy(blk32[:, 0:8], blk[:, :]).then_inc(s_bd, 1)
            dve.wait_ge(s_bd, 5)
            dve.wait_ge(s_qgl, 16)
            dve.tensor_tensor(qg2, qgc, qgc, ALU.mult).then_inc(s_qc, 1)
            dve.tensor_copy(BBm.rearrange("p (g d) -> p g d", g=8),
                            blk[:, :].unsqueeze(2).to_broadcast([P, 8, 16])).then_inc(s_qc, 1)
            dve.wait_ge(s_qk, 1)
            dve.tensor_copy(qgn, bank(6)[:, 0:2]).then_inc(s_qc, 1)
            dve.wait_ge(s_qc, 4)
            dve.tensor_tensor(qgn, qgn, qgc, ALU.mult).then_inc(s_qc, 1)
            dve.wait_ge(s_qc, 5)
            for j in range(2):
                dve.tensor_scalar(qgb[:, j, :], blk32, qgn[:, j:j + 1], None, ALU.mult).then_inc(s_qc, 1)
            ln_chunks(3, range(2, NC), lambda c: None)
            def keep_sums(c):
                dve.wait_ge(s_smt, c + 1)
                for kind, dst in enumerate((rn2, dt2)):
                    v = bank(1).rearrange("p (i g m) -> p i g m", i=4, g=4)[:, :, 2 * kind:2 * kind + 2, 0:8]
                    dve.tensor_copy(dst[:, 64 * c:64 * c + 64].rearrange("p (i g m) -> p i g m", i=4, g=2),
                                    v).then_inc(s_smk, 1)

            for c in range(NC):
                if c == 0:
                    dve.wait_ge(s_tr, 5 * NC)
                dve.wait_ge(s_qh, c + 1)
                if c >= 1:
                    dve.wait_ge(s_ql, c)
                dve.tensor_tensor(res2[:, 0], Qf[:, c % 2], PB2[:, 0, 0], ALU.subtract).then_inc(s_qr, 1)
                dve.wait_ge(s_qp, 3 * c + 2)
                kt = KT[:, :, 512 * c:512 * c + 512]
                dve.tensor_copy(kt, bank(4, 2).rearrange("p (j t) -> p j t", j=2)).then_inc(s_kf, 1)
                dve.wait_ge(s_kh, c + 1)
                if c >= 1:
                    dve.wait_ge(s_kl, c)
                dve.tensor_tensor(res2[:, 1], kt, PB2[:, 1, 0], ALU.subtract).then_inc(s_krs, 1)
                dve.wait_ge(s_qp, 3 * c + 3)
                b, t = c // 2, 4 * (c % 2)
                for g in range(4):
                    vv = dve.tensor_copy(V2[:, 4 * b + g, t:t + 4, :],
                                         bank(6, 2).rearrange("p (i n) -> p i n", i=4)[:, :, 64 * g:64 * g + 64])
                vv.then_inc(s_vf, 1)
                if c % 2 == 0:
                    dve.wait_ge(s_qf, c + 1)
                    dve.tensor_copy(QR[:, :, b, :], Qf[:, c % 2, :, 0:REG]).then_inc(s_qrr, 1)
                if c >= 2:
                    keep_sums(c - 2)
            keep_sums(NC - 2)
            keep_sums(NC - 1)
            ch = [0]

            def link(ins_, wait=True):
                ch[0] += 1
                ins_.then_inc(s_sc2, 1)
                if wait:
                    dve.wait_ge(s_sc2, ch[0])

            dve.wait_ge(s_sim, NC)
            dve.wait_ge(s_c2, 6 + B)
            dve.wait_ge(s_rp, 1)
            link(dve.reciprocal(rn2, rn2))
            link(dve.tensor_tensor(dt2, dt2, rn2, ALU.mult))
            assert ch[0] == SIM_READ
            link(dve.tensor_reduce(simr, dt2.rearrange("p (i h) -> p i h", h=H), AX, ALU.add))
            link(dve.tensor_scalar(simc, simr, 1.0 / H, None, ALU.mult))
            link(dve.scalar_tensor_tensor(tmp32, regm, -BIG, simc, ALU.mult, ALU.add))
            link(dve.tensor_reduce(mm2[:, 0:1], tmp32, AX, ALU.max))
            link(dve.scalar_tensor_tensor(tmp32, regm, BIG, simc, ALU.mult, ALU.add))
            link(dve.tensor_reduce(mm2[:, 1:2], tmp32, AX, ALU.min))
            link(dve.tensor_scalar(mm2[:, 1:2], mm2[:, 1:2], -1.0, None, ALU.mult))
            dve.wait_ge(s_mmt, 1)
            link(dve.tensor_reduce(mmr, bank(2)[0:2, 0:P], AX, ALU.max))
            link(dve.tensor_scalar(mmd, identF[0:2, 0:2], mmr, None, ALU.mult))
            dve.wait_ge(s_mmb, 1)
            link(dve.tensor_copy(mmb, bank(3)[:, 0:2]))
            link(dve.tensor_tensor(rng, mmb[:, 0:1], mmb[:, 1:2], ALU.add))
            link(dve.reciprocal(rrg, rng))
            link(dve.tensor_scalar(simc, simc, mmb[:, 1:2], rrg, ALU.add, ALU.mult))
            link(dve.tensor_scalar(tmp32, simc, 0.9, None, ALU.is_gt))
            link(dve.tensor_scalar(simr, regm, -1.0, 1.0, ALU.mult, ALU.add))
            link(dve.tensor_tensor(tmp32, tmp32, simr, ALU.mult))
            link(dve.tensor_tensor(cls[:, 1, :], tmp32, regm, ALU.add))
            link(dve.tensor_scalar(cls[:, 0, :], cls[:, 1, :], -1.0, 1.0, ALU.mult, ALU.add))
            link(dve.tensor_scalar(cls[:, 2, :], tmp32, -BIG, None, ALU.mult))
            link(dve.tensor_scalar(cls[:, 3, :], cls[:, 0, :], -BIG, None, ALU.mult))
            dve.wait_ge(s_clt, 1)
            link(dve.tensor_copy(clsT, bank(2)[:, 0:P]))
            assert ch[0] == CLS_DONE
            dve.memset(W[:, 2048:2816], 0.0).then_inc(s_qrr, 1)
            dve.wait_ge(s_qrr, B + 1)
            for j in range(2):
                dve.tensor_tensor(Qbd[:, :, j, 0:8 * REG].rearrange("p b (g r) -> p b g r", g=8),
                                  QR[:, j].unsqueeze(2).to_broadcast([P, B, 8, REG]),
                                  blk[:, :].unsqueeze(1).unsqueeze(3).to_broadcast([P, B, 8, REG]),
                                  ALU.mult).then_inc(s_qrr, 1)
            dve.tensor_reduce(rmask, Rfull, AX, ALU.add).then_inc(s_c2, 1)
            dve.tensor_reduce(Rsel, Rfull.rearrange("p g r -> p r g"), AX, ALU.add).then_inc(s_c2, 1)
            dve.wait_ge(s_c2, 8 + B)

            def register_maximum(b):
                dve.wait_ge(s_rq, b + 1)
                dve.tensor_reduce(rmx[:, b:b + 1], bank(4, 2), AX, ALU.max).then_inc(s_rm, 1)
                dve.wait_ge(s_rm, 2 * b + 1)
                dve.tensor_scalar(rnm[:, b:b + 1], rmx[:, b:b + 1], -0.25, None, ALU.mult).then_inc(s_rm, 1)

            def register_masked(b):
                dve.wait_ge(s_rex, b + 1)
                dve.reciprocal(rrd[:, b:b + 1], rden[:, b:b + 1]).then_inc(s_rc2, 1)
                dve.wait_ge(s_rc2, b + 1)
                dve.wait_ge(s_rv, b + 1)
                if b >= 1:
                    dve.wait_ge(s_rsm, b)
                for j in range(2):
                    v = slice(64 * j, 64 * j + 64)
                    dve.scalar_tensor_tensor(omk[v, j].rearrange("p (g d) -> p g d", g=8),
                                             bank(6)[v, 0:P].rearrange("p (g d) -> p g d", g=8), rrd[v, b:b + 1],
                                             rmask[v].unsqueeze(2).to_broadcast([64, 8, D]), ALU.mult,
                                             ALU.mult).then_inc(s_rk, 1)

            def register_kept(b):
                dve.wait_ge(s_rsm, b + 1)
                dve.tensor_scalar(regn[:, b, :], bank(7)[0:REG, 0:C], 0.5, None, ALU.mult).then_inc(s_rgn, 1)

            def turn_wait(n):
                dve.wait_ge(s_turn, n + 1)

            def reduce_tile(n, k, a):
                half, q, h = a // 16, a // 4 % 4, a % 4
                turn_wait(n)
                dve.tensor_reduce(MX[:, half, h, q:q + 1], bank(2 * (k % 2), 2), AX, ALU.max).then_inc(s_tfree, 1)

            def rows_turn(n, k, half):
                turn_wait(n)
                dve.tensor_scalar(mro[:, half, :], bank(2 * (k % 2))[0:16, 0:P], -1.0, None,
                                  ALU.mult).then_inc(s_tfree, 1)

            def normalise2(n, k, u, half):
                O = bank(2 * (k % 2)).rearrange("p (q j d) -> p q j d", q=4, j=4)
                dve.wait_ge(s_tfree, 2 + n)
                turn_wait(n)
                dve.reciprocal(rc2, O[:, :, :, D]).then_inc(s_rc2, 1)
                dve.wait_ge(s_rc2, 2 * u + half + 1 + B)
                dst = On2[:, 4 * half:4 * half + 4, bass.ds(64 * u, 64)].rearrange("p q (j d) -> p q j d", j=4)
                dve.tensor_tensor(dst, O[:, :, :, 0:D], rc2.unsqueeze(3).to_broadcast([P, 4, 4, D]),
                                  ALU.mult).then_inc(s_tfree, 1)

            dve.sem_inc(s_tfree, 2)
            n = 0
            for what, arg in PROLOGUE:
                if what == "register scores":
                    register_maximum(arg)
                elif what == "register values":
                    register_masked(arg)
                elif what == "register sum":
                    register_kept(arg)
                elif what == "tile":
                    reduce_tile(n, n + 1, arg)
                    n += 1
                elif what == "rows":
                    dve.wait_ge(s_rq, B)
                    rows_turn(n, n + 1, arg)
                    n += 1
            for i in range(LEAD):
                reduce_tile(n + i, n + i + 1, 32 - LEAD + i)

            def body_dve(u, j, last=False):
                base = TURNS0 + TURNS * u
                k = 0
                for step in (PLAN_LAST if last else PLAN):
                    for what, arg in step:
                        if what == "tile":
                            reduce_tile(base + k, k, arg)
                        elif what == "rows":
                            rows_turn(base + k, k, arg)
                        else:
                            normalise2(base + k, k, u, arg)
                        k += 1

            with dve.Fori(0, 5) as i:
                for j in range(3):
                    body_dve(3 * i + j, j)
            body_dve(15, 0, last=True)
            dve.wait_ge(s_tfree, 2 + TURNS0 + TURNS * 15 + 3)
            dve.scalar_tensor_tensor(On2[0:REG, 0, :], On2[0:REG, 0, :], 0.5,
                                     regn.rearrange("p b c -> p (b c)"), ALU.mult,
                                     ALU.add).then_inc(s_avg, 1)
            for c in range(NC):
                dve.wait_ge(s_wo, NC + c + 1)
                dve.wait_ge(s_xb2, c // 2 + 1)
                xs = X[:, 4 * c:4 * c + 4, :]
                dve.scalar_tensor_tensor(xs, bank(4 + 2 * (c % 2), 2).rearrange("p (i n) -> p i n", i=4),
                                         gates[:, 3:4], xs, ALU.mult, ALU.add).then_inc(s_x3, 1)


def kernel(**inputs):
    import numpy as _np
    import concourse.bacc as _bacc
    from concourse import mybir as _mybir
    from concourse.bass_utils import run_bass_kernel_spmd as _run

    i = {k: _np.asarray(v) for k, v in inputs.items()}
    lay = {
        "x": i["x"],
        "ctxT": i["ctx_1024"].transpose(2, 0, 1).reshape(C, B * KX),
        "wk0T": i["L0_xattn_Wk"].T,
        "wq0": i["L0_xattn_Wq"],
        "wv0T": i["L0_xattn_Wv"].T,
        "mask0T": i["mask_BxSxS2_bk0"].transpose(0, 2, 1),
        "mask1T": i["mask_1x1xSxS2_bk0"][0, 0].T,
        "g_xattn": i["g_xattn"],
        "g_ffn": i["g_ffn"],
        "w_gate": i["L0_ffn_w_gate"],
        "ballT": i["L0_ffn_B"].transpose(2, 0, 1).reshape(C, E * R),
        "AT": i["L0_ffn_A"].transpose(0, 2, 1).reshape(E * R, L),
        "A1": i["L0_ffn_A"].transpose(1, 0, 2).reshape(L, E * R),
        "wtT": i["L0_ffn_wt_w"].T,
        "wt_b": i["L0_ffn_wt_b"],
        "wdT": i["L0_ffn_wd_w"].T,
        "wd_b": i["L0_ffn_wd_b"],
        "scale": i["L0_ffn_scale"],
        "wv1T": i["L1_xattn_Wv"].T,
        "wk1T": i["L1_xattn_Wk"].T,
        "wq1": i["L1_xattn_Wq"],
        "wo1T": i["L1_xattn_Wo"].T,
        "bo1": i["L1_xattn_bo"],
        "g_info": i["L1_ffn_g_info"],
        "wqkv": i["L1_ffn_W_qkv"],
        "wproj": i["L1_ffn_W_proj"],
        "bproj": i["L1_ffn_b_proj"],
    }
    nc = _bacc.Bacc("TRN2", target_bir_lowering=False, num_devices=1)
    arrays, args = {}, {}
    for name, a in lay.items():
        a = _np.ascontiguousarray(a)
        arrays[f"in_{name}"] = a
        args[name] = nc.dram_tensor(f"in_{name}", a.shape, _mybir.dt.from_np(a.dtype), kind="ExternalInput").ap()
    out = nc.dram_tensor("out_0", (B, S, C), F32, kind="ExternalOutput").ap()
    build_program(nc, args, out)
    r = _run(nc, [arrays], core_ids=[0])
    return r.results[0]["out_0"]
```
